# Optimizing a Trainium2 kernel written in Bass

```python
import numpy as np
import jax
import jax.numpy as jnp

def _softmax(x, axis=-1):
    return jax.nn.softmax(x, axis=axis)

def _gelu(x):
    return jax.nn.gelu(x, approximate=True)

def _silu(x):
    return jax.nn.silu(x)

def _sigmoid(x):
    return jax.nn.sigmoid(x)

def _layernorm(x, axis=-1, eps=1e-05):
    m = jnp.mean(x, axis=axis, keepdims=True)
    v = jnp.var(x, axis=axis, keepdims=True)
    return (x - m) / jnp.sqrt(v + eps)

def _scatter_add(tgt, idx, src, axis=0):
    return tgt.at[idx].add(src)

def _segment_sum(src, seg, n):
    return jax.ops.segment_sum(src, seg, n)
kernel_name = 'mk_vit_tower_d1_tok_img256_r4_616a53'

def setup_inputs(seed: int=0):
    np.random.seed(seed)
    _w = jnp.asarray

    def _rec_inputs():
        import jax
        import jax.numpy as jnp
        _rk = jax.random.key(seed)
        x = -0.000928989 + 1.00043 * jax.random.normal(jax.random.fold_in(_rk, 1), (32, 64, 64, 1), jnp.float32)
        return x
    x = _rec_inputs()

    def _L0_tok_setup():
        import jax, jax.numpy as jnp
        import numpy as np
        B, S, D_A, D_V, D_U, L, M1, M2 = (16, 64, 3, 32, 1, 4, 12, 12)
        MID = 4 * D_U

        def conv1x1(x, w, b):
            return jnp.einsum('bixy,oi->boxy', x, w) + b[None, :, None, None]

        def fourier_layer(x, fw_i):
            Bm, C, M, N = x.shape
            x_ft = jnp.fft.rfft2(x, s=(M, N), norm='ortho')
            w_lo = fw_i[0, ..., 0] + 1j * fw_i[0, ..., 1]
            w_hi = fw_i[1, ..., 0] + 1j * fw_i[1, ..., 1]
            lo = jnp.einsum('bixy,ioxy->boxy', x_ft[:, :, :M1, :M2], w_lo)
            hi = jnp.einsum('bixy,ioxy->boxy', x_ft[:, :, -M1:, :M2], w_hi)
            out_ft = jnp.zeros(x_ft.shape, dtype=x_ft.dtype)
            out_ft = out_ft.at[:, :, :M1, :M2].set(lo)
            out_ft = out_ft.at[:, :, -M1:, :M2].set(hi)
            return jnp.fft.irfft2(out_ft, s=(M, N), norm='ortho')

        def make_grid(b, sx, sy):
            gx = jnp.broadcast_to(jnp.linspace(0.0, 1.0, sx)[None, :, None], (b, sx, sy))
            gy = jnp.broadcast_to(jnp.linspace(0.0, 1.0, sy)[None, None, :], (b, sx, sy))
            return jnp.stack([gx, gy], axis=-1)
        key = jax.random.key(seed)
        ks = jax.random.split(key, 12)
        sc_v = 1.0 / np.sqrt(D_V)
        inp = {'x': jax.random.normal(ks[0], (B, S, S, D_A - 2), dtype=jnp.float32), 'p_w': jax.random.normal(ks[1], (D_V, D_A), dtype=jnp.float32) / np.sqrt(D_A), 'p_b': jnp.zeros((D_V,), dtype=jnp.float32), 'fw': jax.random.normal(ks[2], (L, 2, D_V, D_V, M1, M2, 2), dtype=jnp.float32) * sc_v, 'w1_w': jax.random.normal(ks[3], (L, D_V, D_V), dtype=jnp.float32) * sc_v, 'w1_b': jnp.zeros((L, D_V), dtype=jnp.float32), 'w2_w': jax.random.normal(ks[4], (L, D_V, D_V), dtype=jnp.float32) * sc_v, 'w2_b': jnp.zeros((L, D_V), dtype=jnp.float32), 'q1_w': jax.random.normal(ks[5], (MID, D_V), dtype=jnp.float32) * sc_v, 'q1_b': jnp.zeros((MID,), dtype=jnp.float32), 'q2_w': jax.random.normal(ks[6], (D_U, MID), dtype=jnp.float32) / np.sqrt(MID), 'q2_b': jnp.zeros((D_U,), dtype=jnp.float32)}
        return inp
    _L0_tok_all = _L0_tok_setup()
    _L0_tok_in = {k: v for k, v in _L0_tok_all.items() if k in ('p_w', 'p_b', 'fw', 'w1_w', 'w1_b', 'w2_w', 'w2_b', 'q1_w', 'q1_b', 'q2_w', 'q2_b')}
    del _L0_tok_all

    def _L0_attn_setup():
        import jax, jax.numpy as jnp
        import numpy as np
        key = jax.random.key(seed)
        ks = jax.random.split(key, 5)
        b, t, e, h = (8, 256, 64, 8)
        w = lambda k, shape: jax.random.normal(k, shape, dtype=jnp.float32) * 0.02
        return {'x': jax.random.normal(ks[0], (b, t, e), dtype=jnp.float32), 'Wq': w(ks[1], (e, e * h)), 'bq': jnp.zeros((e * h,), jnp.float32), 'Wk': w(ks[2], (e, e * h)), 'bk': jnp.zeros((e * h,), jnp.float32), 'Wv': w(ks[3], (e, e * h)), 'bv': jnp.zeros((e * h,), jnp.float32), 'Wu': w(ks[4], (e * h, e)), 'bu': jnp.zeros((e,), jnp.float32)}
    _L0_attn_all = _L0_attn_setup()
    _L0_attn_in = {k: v for k, v in _L0_attn_all.items() if k in ('Wq', 'bq', 'Wk', 'bk', 'Wv', 'bv', 'Wu', 'bu')}
    del _L0_attn_all

    def _L0_ffn_setup():
        import jax, jax.numpy as jnp
        import numpy as np
        DIM = 64
        HEADS = 8
        NUM_KEYS = 64
        NUM_KV = NUM_KEYS ** 2
        PK_TOPK = 16
        FINAL_TOPK = 16
        DIM_KEY = DIM // 2
        P = 2

        def _pk(x, Wq_pk, pk_keys):
            b, n, _ = x.shape
            q = (x @ Wq_pk).reshape(b, n, P, HEADS, DIM_KEY).transpose(2, 0, 1, 3, 4)
            sim = jnp.einsum('pbnhd,pkhd->pbnhk', q, pk_keys)
            scores, idx = jax.lax.top_k(sim, PK_TOPK)
            idx0 = idx[0]
            idx1 = idx[1] * NUM_KEYS
            index = (idx0[..., :, None] + idx1[..., None, :]).reshape(b, n, HEADS, PK_TOPK * PK_TOPK)
            score = (scores[0][..., :, None] + scores[1][..., None, :]).reshape(b, n, HEADS, PK_TOPK * PK_TOPK)
            final_scores, pk_idx = jax.lax.top_k(score, FINAL_TOPK)
            final_indices = jnp.take_along_axis(index, pk_idx, axis=-1)
            final_scores = jax.nn.softmax(final_scores, axis=-1)
            return (final_scores, final_indices)
        key = jax.random.key(seed)
        ks = jax.random.split(key, 7)
        b, n = (2, 256)
        std = 0.02
        x = jax.random.normal(ks[0], (b, n, DIM), dtype=jnp.float32)
        Wq_pk = jax.random.normal(ks[1], (DIM, P * HEADS * DIM_KEY), dtype=jnp.float32) * std
        pk_keys = jax.random.normal(ks[2], (P, NUM_KEYS, HEADS, DIM_KEY), dtype=jnp.float32) * std
        Wq = jax.random.normal(ks[3], (DIM, HEADS * DIM), dtype=jnp.float32) * std
        keys_table = jax.random.normal(ks[4], (NUM_KV * HEADS, DIM), dtype=jnp.float32) * std
        values_table = jax.random.normal(ks[5], (NUM_KV * HEADS, DIM), dtype=jnp.float32) * std
        Wo = jax.random.normal(ks[6], (DIM * HEADS, DIM), dtype=jnp.float32) * std
        return {'x': x, 'Wq_pk': Wq_pk, 'pk_keys': pk_keys, 'Wq': Wq, 'keys_table': keys_table, 'values_table': values_table, 'Wo': Wo}
    _L0_ffn_all = _L0_ffn_setup()
    _L0_ffn_in = {k: v for k, v in _L0_ffn_all.items() if k in ('Wq_pk', 'pk_keys', 'Wq', 'keys_table', 'values_table', 'Wo')}
    del _L0_ffn_all
    return {'x': x, 'L0_tok_p_w': _L0_tok_in['p_w'], 'L0_tok_p_b': _L0_tok_in['p_b'], 'L0_tok_fw': _L0_tok_in['fw'], 'L0_tok_w1_w': _L0_tok_in['w1_w'], 'L0_tok_w1_b': _L0_tok_in['w1_b'], 'L0_tok_w2_w': _L0_tok_in['w2_w'], 'L0_tok_w2_b': _L0_tok_in['w2_b'], 'L0_tok_q1_w': _L0_tok_in['q1_w'], 'L0_tok_q1_b': _L0_tok_in['q1_b'], 'L0_tok_q2_w': _L0_tok_in['q2_w'], 'L0_tok_q2_b': _L0_tok_in['q2_b'], 'L0_attn_Wq': _L0_attn_in['Wq'], 'L0_attn_bq': _L0_attn_in['bq'], 'L0_attn_Wk': _L0_attn_in['Wk'], 'L0_attn_bk': _L0_attn_in['bk'], 'L0_attn_Wv': _L0_attn_in['Wv'], 'L0_attn_bv': _L0_attn_in['bv'], 'L0_attn_Wu': _L0_attn_in['Wu'], 'L0_attn_bu': _L0_attn_in['bu'], 'L0_ffn_Wq_pk': _L0_ffn_in['Wq_pk'], 'L0_ffn_pk_keys': _L0_ffn_in['pk_keys'], 'L0_ffn_Wq': _L0_ffn_in['Wq'], 'L0_ffn_keys_table': _L0_ffn_in['keys_table'], 'L0_ffn_values_table': _L0_ffn_in['values_table'], 'L0_ffn_Wo': _L0_ffn_in['Wo']}

def reference(x, L0_tok_p_w, L0_tok_p_b, L0_tok_fw, L0_tok_w1_w, L0_tok_w1_b, L0_tok_w2_w, L0_tok_w2_b, L0_tok_q1_w, L0_tok_q1_b, L0_tok_q2_w, L0_tok_q2_b, L0_attn_Wq, L0_attn_bq, L0_attn_Wk, L0_attn_bk, L0_attn_Wv, L0_attn_bv, L0_attn_Wu, L0_attn_bu, L0_ffn_Wq_pk, L0_ffn_pk_keys, L0_ffn_Wq, L0_ffn_keys_table, L0_ffn_values_table, L0_ffn_Wo):
    import jax
    import jax.numpy as jnp

    def _L0_tok_ref(x, p_w, p_b, fw, w1_w, w1_b, w2_w, w2_b, q1_w, q1_b, q2_w, q2_b):
        import jax, jax.numpy as jnp
        import numpy as np
        B, S, D_A, D_V, D_U, L, M1, M2 = (16, 64, 3, 32, 1, 4, 12, 12)
        MID = 4 * D_U

        def conv1x1(x, w, b):
            return jnp.einsum('bixy,oi->boxy', x, w) + b[None, :, None, None]

        def fourier_layer(x, fw_i):
            Bm, C, M, N = x.shape
            x_ft = jnp.fft.rfft2(x, s=(M, N), norm='ortho')
            w_lo = fw_i[0, ..., 0] + 1j * fw_i[0, ..., 1]
            w_hi = fw_i[1, ..., 0] + 1j * fw_i[1, ..., 1]
            lo = jnp.einsum('bixy,ioxy->boxy', x_ft[:, :, :M1, :M2], w_lo)
            hi = jnp.einsum('bixy,ioxy->boxy', x_ft[:, :, -M1:, :M2], w_hi)
            out_ft = jnp.zeros(x_ft.shape, dtype=x_ft.dtype)
            out_ft = out_ft.at[:, :, :M1, :M2].set(lo)
            out_ft = out_ft.at[:, :, -M1:, :M2].set(hi)
            return jnp.fft.irfft2(out_ft, s=(M, N), norm='ortho')

        def make_grid(b, sx, sy):
            gx = jnp.broadcast_to(jnp.linspace(0.0, 1.0, sx)[None, :, None], (b, sx, sy))
            gy = jnp.broadcast_to(jnp.linspace(0.0, 1.0, sy)[None, None, :], (b, sx, sy))
            return jnp.stack([gx, gy], axis=-1)
        b, sx, sy = (x.shape[0], x.shape[1], x.shape[2])
        grid = make_grid(b, sx, sy)
        h = jnp.concatenate([x, grid], axis=-1)
        h = jnp.transpose(h, (0, 3, 1, 2))
        h = conv1x1(h, p_w, p_b)
        for i in range(L):
            x1 = fourier_layer(h, fw[i])
            x1 = jax.nn.relu(conv1x1(x1, w1_w[i], w1_b[i]))
            x1 = conv1x1(x1, w2_w[i], w2_b[i])
            h = h + x1
        h = conv1x1(h, q1_w, q1_b)
        h = jax.nn.relu(h)
        h = conv1x1(h, q2_w, q2_b)
        return jnp.squeeze(h)

    def _L0_attn_ref(x, Wq, bq, Wk, bk, Wv, bv, Wu, bu):
        import jax, jax.numpy as jnp
        import numpy as np
        b, t, e = x.shape
        h = Wq.shape[1] // e
        q = (x @ Wq + bq).reshape(b, t, h, e)
        k = (x @ Wk + bk).reshape(b, t, h, e)
        v = (x @ Wv + bv).reshape(b, t, h, e)
        scores = jnp.einsum('bihe,bjhe->bhij', q, k) / jnp.sqrt(jnp.asarray(e, jnp.float32))
        i = jnp.arange(t)[:, None]
        j = jnp.arange(t)[None, :]
        scores = jnp.where(j >= i, -jnp.inf, scores)
        scores = jnp.where(i == 0, 0.0, scores)
        att = jax.nn.softmax(scores, axis=-1)
        att = jnp.where(i == 0, 0.0, att)
        out = jnp.einsum('bhij,bjhe->bihe', att, v).reshape(b, t, h * e)
        return out @ Wu + bu

    def _L0_ffn_ref(x, Wq_pk, pk_keys, Wq, keys_table, values_table, Wo):
        import jax, jax.numpy as jnp
        import numpy as np
        DIM = 64
        HEADS = 8
        NUM_KEYS = 64
        NUM_KV = NUM_KEYS ** 2
        PK_TOPK = 16
        FINAL_TOPK = 16
        DIM_KEY = DIM // 2
        P = 2

        def _pk(x, Wq_pk, pk_keys):
            b, n, _ = x.shape
            q = (x @ Wq_pk).reshape(b, n, P, HEADS, DIM_KEY).transpose(2, 0, 1, 3, 4)
            sim = jnp.einsum('pbnhd,pkhd->pbnhk', q, pk_keys)
            scores, idx = jax.lax.top_k(sim, PK_TOPK)
            idx0 = idx[0]
            idx1 = idx[1] * NUM_KEYS
            index = (idx0[..., :, None] + idx1[..., None, :]).reshape(b, n, HEADS, PK_TOPK * PK_TOPK)
            score = (scores[0][..., :, None] + scores[1][..., None, :]).reshape(b, n, HEADS, PK_TOPK * PK_TOPK)
            final_scores, pk_idx = jax.lax.top_k(score, FINAL_TOPK)
            final_indices = jnp.take_along_axis(index, pk_idx, axis=-1)
            final_scores = jax.nn.softmax(final_scores, axis=-1)
            return (final_scores, final_indices)
        b, n, d = x.shape
        q = (x @ Wq).reshape(b, n, HEADS, DIM) * DIM ** (-0.5)
        kv_scores, indices = _pk(x, Wq_pk, pk_keys)
        offsets = jnp.arange(HEADS, dtype=indices.dtype) * NUM_KV
        ind = indices + offsets[None, None, :, None]
        k = jnp.einsum('bnhk,bnhkd->bnhd', kv_scores, keys_table[ind])
        v = jnp.einsum('bnhk,bnhkd->bnhd', kv_scores, values_table[ind])
        sim = jnp.einsum('bihd,bjhd->bhij', q, k)
        neg = -jnp.finfo(sim.dtype).max
        causal = jnp.tril(jnp.ones((n, n), dtype=bool))
        sim = jnp.where(causal, sim, neg)
        attn = jax.nn.softmax(sim, axis=-1)
        out = jnp.einsum('bhij,bjhd->bhid', attn, v)
        out = out.transpose(0, 2, 1, 3).reshape(b, n, HEADS * DIM)
        return out @ Wo
    h = _L0_tok_ref(x, L0_tok_p_w, L0_tok_p_b, L0_tok_fw, L0_tok_w1_w, L0_tok_w1_b, L0_tok_w2_w, L0_tok_w2_b, L0_tok_q1_w, L0_tok_q1_b, L0_tok_q2_w, L0_tok_q2_b)
    h = h + _L0_attn_ref(_layernorm(h, axis=-1), L0_attn_Wq, L0_attn_bq, L0_attn_Wk, L0_attn_bk, L0_attn_Wv, L0_attn_bv, L0_attn_Wu, L0_attn_bu)
    h = h + _L0_ffn_ref(_layernorm(h, axis=-1), L0_ffn_Wq_pk, L0_ffn_pk_keys, L0_ffn_Wq, L0_ffn_keys_table, L0_ffn_values_table, L0_ffn_Wo)
    return h

_drawn_inputs = setup_inputs


def setup_inputs(seed=0):
    import zlib

    import numpy as np

    out = dict(_drawn_inputs(seed))
    spreads = {'L0_tok_p_b': (0.0, 0.1),
     'L0_tok_w1_b': (0.0, 0.1),
     'L0_tok_w2_b': (0.0, 0.1),
     'L0_tok_q1_b': (0.0, 0.1),
     'L0_attn_bq': (0.0, 0.8),
     'L0_attn_bk': (0.0, 2.0),
     'L0_attn_bv': (0.0, 0.1),
     'L0_attn_bu': (0.0, 0.1)}
    factors = {'L0_attn_Wq': 8.0,
     'L0_attn_Wk': 8.0,
     'L0_ffn_Wq_pk': 8.0,
     'L0_ffn_pk_keys': 8.0,
     'L0_ffn_Wq': 64.0,
     'L0_ffn_keys_table': 64.0,
     'L0_ffn_values_table': 8.0,
     'L0_ffn_Wo': 8.0}
    for name, (base, spread) in spreads.items():
        noise = np.random.default_rng([zlib.crc32(name.encode()), seed]).standard_normal(out[name].shape)
        drawn = base * np.exp(spread * noise) if base else spread * noise
        out[name] = jnp.asarray(drawn.astype(out[name].dtype))
    for name, factor in factors.items():
        out[name] = (out[name] * factor).astype(out[name].dtype)
    return out
```

```python
from contextlib import ExitStack

import numpy as np

import concourse.bass as bass
from concourse import mybir

ALU = mybir.AluOpType
ACT = mybir.ActivationFunctionType
AX = mybir.AxisListType
F32 = mybir.dt.float32
U32 = mybir.dt.uint32

P = 128
B, S = 32, 64
C = 32
L = 4
M1 = 12
GB = 4
G = B // GB
HE = 8
K = 16
NK = 64
NKV = NK * NK
MID = 4
J = M1 * M1
XP = S // 2
BANK = 512
PAIRS = [(a, K // (a + 1)) for a in range(K)]
NC = sum(n for _, n in PAIRS)
RING = 4
PIECES = 2 * HE
FY, FX = 2 * 2 * M1, 3 * 2 * M1
PAD = 96
BIG = 1e30
LOWEST = -3e38
EPS = 1e-5


def shape_constants():
    one = np.zeros
    w = 2 * np.pi / S
    kx = np.concatenate([np.arange(M1), np.arange(S - M1, S)])
    y, ky = np.arange(S), np.arange(M1)
    fy = one((2, S, 2, M1, 2))
    for i in range(2):
        fy[i, :, i, :, 0] = np.cos(w * np.outer(y, ky)) / 8
        fy[i, :, i, :, 1] = -np.sin(w * np.outer(y, ky)) / 8
    fyp = one((P, PAD))
    fyp[:, :FY] = fy.reshape(P, FY)
    co, si = np.cos(w * np.outer(y, kx)) / 8, np.sin(w * np.outer(y, kx)) / 8
    fx = one((S, 2, 3, 2 * M1))
    fx[:, 0, 0], fx[:, 1, 0] = co, si
    fx[:, 0, 1], fx[:, 1, 1] = -si, co
    fx[:, 0, 2], fx[:, 1, 2] = si, -co
    fxp = one((P, PAD))
    fxp[:, :FX] = fx.reshape(P, FX)
    iv = one((M1, 2, 2, S, 2))
    for h in range(2):
        c, s = co[:, h * M1:(h + 1) * M1].T, si[:, h * M1:(h + 1) * M1].T
        iv[:, h, 0, :, 0], iv[:, h, 0, :, 1] = c, s
        iv[:, h, 1, :, 0], iv[:, h, 1, :, 1] = -s, c
    ivp = one((P, P))
    ivp[:4 * M1] = iv.reshape(4 * M1, P)
    g = one((4, 32, 2, 2, S))
    amp = np.where(ky == 0, 1.0, 2.0)[:, None] / 8
    for p in range(2):
        for i in range(2):
            g[2 * p + i, 0:2 * M1:2, p, i] = amp * np.cos(w * np.outer(ky, y))
            g[2 * p + i, 1:2 * M1:2, p, i] = -amp * np.sin(w * np.outer(ky, y))
    lin = np.linspace(0.0, 1.0, S, dtype=np.float32)
    grid = one((2, S, XP, 3))
    grid[..., 0] = lin.reshape(XP, 2).T[:, None, :]
    grid[..., 1] = lin[None, :, None]
    grid[..., 2] = 1.0
    i, j = np.arange(S)[:, None], np.arange(S)[None, :]
    strict = np.tile(np.where(j >= i, -BIG, 0.0), (2, 1))
    causal = np.tile(np.where(j > i, -BIG, 0.0), (2, 1))
    rows = np.tile((np.arange(S) > 0) * 1.0, 2)[:, None]
    img = np.kron(np.eye(GB), np.ones((C, MID)))
    q2m = np.kron(np.eye(4), np.vstack([np.kron(np.eye(GB), np.ones((MID, 1))), one((16, GB))]))
    hoff = np.tile(np.arange(HE) * float(NKV), (P, 1))
    iota = np.tile(np.arange(NC) * 1.0, (P, 1))
    parts = dict(fy=fyp, fx=fxp, iv=ivp, g=g.reshape(P, 2 * P), ident=np.eye(P), grid=grid.reshape(P, 3 * XP),
                 strict=strict, causal=causal, rows=rows, img=img, q2m=q2m, hoff=hoff, iota=iota)
    at, o = {}, 0
    for n, a in parts.items():
        at[n] = (o, a.shape[1])
        o += a.shape[1]
    return at, np.ascontiguousarray(np.concatenate(list(parts.values()), 1), dtype=np.float32)


CONST_AT, CONST = shape_constants()

PE_STEPS = ["mid", "image", "h1", "x1", "x2", "qpk", "sims0", "sims1"]
ACT_STEPS = ["mid", "sd1", "x1", "sd2", "x2", "qpk", "sims0", "exp0", "sims1", "exp1"]
DVE_STEPS = ["image", "h1", "var1", "xn1", "h2", "var2", "xn2", "top0", "top1"]
ATT_PE = [["q0", "q1", "q2", "q3", "k0", "k1", "k2", "k3", "v0", "v1", "scores", "pT0", "pT1", "o", "y"],
          ["q0", "q1", "q2", "q3", "k0", "k1", "k2", "k3", "scores", "pT0", "pT1", "o", "y"]]
ATT_ACT = [["q0", "q1", "q2", "q3", "v0", "v1", "exp", "pT", "oT"], ["q0", "q1", "q2", "q3", "exp", "pT", "oT"]]
ATT_DVE = ["k0", "k1", "k2", "k3", "shifted", "prob", "pT", "oT"]


def wait_apart(eng, sem, value, turns):
    eng.wait_ge(sem, value)
    if not isinstance(value, int):
        eng.sem_inc(turns, 1)


def reached(eng, sem, steps, name, turn, apart_from=None):
    value = turn * len(steps) + steps.index(name) + 1
    if apart_from is None:
        eng.wait_ge(sem, value)
    else:
        wait_apart(eng, sem, value, apart_from)


def strided(t, start, dims, rows=(0, P)):
    pitch = 1
    for n in t.shape[1:]:
        pitch *= n
    return bass.AP(tensor=t, offset=start + rows[0] * pitch,
                   ap=[[pitch, rows[1] - rows[0]]] + [[a, b] for a, b in dims])


DVE_SEQ = 64


class Steps:

    def __init__(self, sem, per, turn):
        self.sem, self.per, self.turn, self.n = sem, per, turn, 0

    def add(self, ins):
        ins.then_inc(self.sem, 1)
        self.n += 1

    def so_far(self, eng):
        eng.wait_ge(self.sem, self.turn * self.per + self.n)

    def so_far_apart(self, eng, turns):
        wait_apart(eng, self.sem, self.turn * self.per + self.n, turns)

    def close(self):
        assert self.n == self.per, (self.sem, self.n)


def build(nc, x, const, w2s, w1s, fw, b1, b2, w2q, q1t, q2c, q2b, wq, wk, wv, wu, bu, wpk, pk, wq2, wo, table, out):
    ctx = ExitStack()
    with ctx:
        def sb(name, n, dt=F32):
            return ctx.enter_context(nc.sbuf_tensor(name, [P, n], dt))

        def sem(name):
            return ctx.enter_context(nc.semaphore(name))

        cst = sb("cst", CONST.shape[1])

        def const_of(name, rows=(0, P)):
            o, n = CONST_AT[name]
            return cst[rows[0]:rows[1], o:o + n]

        ident = const_of("ident")
        w2_all, w1_all = sb("w2_all", L * C), sb("w1_all", L * P)
        w2_now, w1_now, q_now = sb("w2_now", C), sb("w1_now", P), sb("q_now", C)
        q_all = sb("q_all", (L + 1) * C)
        fw_now = sb("fw_now", J * C)
        b1_all, b2_all = sb("b1_all", L * C), sb("b2_all", L * 16)
        w2q_s, q1_s, q2_s, q2b_s, q2blk = sb("w2q_s", (2 * L + 1) * P), sb("q1_s", MID), sb("q2_s", 1), sb("q2b_s", 1), sb("q2blk", 16)
        wq_s, wk_s, wv_s, wpk_s, wq2_s = (sb(n, HE * S) for n in ("wq_s", "wk_s", "wv_s", "wpk_s", "wq2_s"))
        wu_s, wo_s, bu_s = sb("wu_s", 4 * S), sb("wo_s", 4 * S), sb("bu_s", S)
        pk_s = sb("pk_s", 4 * 4 * NK)

        img_in = sb("img_in", XP * GB)
        pixT = sb("pixT", XP * P)
        pix = sb("pix", XP * P)
        ux = sb("ux", M1 * P)
        uxT = sb("uxT", M1 * P)
        vk = sb("vk", 3 * 2 * J)
        modes = sb("modes", J * 16)
        mixed = sb("mixed", 576)
        mixT = sb("mixT", M1 * P)
        zx = sb("zx", 16 * P)
        zxT = sb("zxT", 16 * P)
        mid = sb("mid", 2 * BANK)

        hT = sb("hT", GB * S)
        h1, h2, h2p = sb("h1", 2 * S), sb("h2", 2 * S), sb("h2p", 2 * S)
        zero = sb("zero", C)
        stat, mv, rs, xn = sb("stat", 12), sb("mv", 4), sb("rs", 10), sb("xn", 2 * S)
        xT, xT2, xT2p = sb("xT", GB * S), sb("xT2", GB * S), sb("xT2p", GB * S)
        qT, kT = pixT[0:S, 0:HE * GB * S], pixT[0:S, HE * GB * S:2 * HE * GB * S]
        vv = sb("vv", 2 * HE * S)
        sc, pT, oT = zxT, ux, uxT
        red = sb("red", 48)
        qpk = sb("qpk", 4 * GB * S)
        sims, sims2, oneh = ux, uxT, pix
        vi = sb("vi", 2 * 2 * HE * K)
        iu = sb("iu", 2 * HE * K, U32)
        cand = sb("cand", 2 * HE * NC)
        cand2 = sb("cand2", HE * NC)
        top, pos, posf = sb("top", HE * K), sb("pos", HE * K, U32), sb("posf", HE * K)
        found, den = sb("found", HE * K), sb("den", 2 * HE)
        idx = sb("idx", 2 * HE * K, U32)
        idx1n = sb("idx1n", HE * K, U32)
        wts, wts1n = sb("wts", 2 * HE * K), sb("wts1n", HE * K)
        ring = sb("ring", RING * K * P)
        kv = sb("kv", 2 * HE * P)
        res = sb("res", 2 * S)

        ps = ctx.enter_context(nc.psum_tensor("ps", [P, 8, BANK], F32))

        loaded, built, slots, gath = sem("loaded"), sem("built"), sem("slots_free"), [sem(f"gathered{i}") for i in range(RING)]
        memz = sem("zeroed")
        pe_turns, dve_turns, pool_turns = sem("pe_turns"), sem("dve_turns"), sem("pool_turns")
        qall_pe = sem("qall_pe")
        img_sem, img_done = sem("image_in"), sem("image_ready")
        fw_sem, staged = sem("fw_in"), sem("layer_weights")
        a_full, a_act, a_dve = sem("ux_full"), sem("ux_act"), sem("ux_dve")
        t1_full, t1_act, t1_dve = sem("pix_full"), sem("pix_act"), sem("pix_dve")
        t2_full, t2_act, t2_dve = sem("uxT_full"), sem("uxT_act"), sem("uxT_dve")
        v_full, v_act, v_dve = sem("vk_full"), sem("vk_act"), sem("vk_dve")
        q_full = sem("mid_layer")
        c_full, c_done, c_seq = sem("modes_full"), sem("modes_done"), sem("modes_seq")
        m_full, m_act, m_dve = sem("mixed_full"), sem("mixed_act"), sem("mixed_dve")
        e_full, e_act, e_dve, e_seq = sem("mixT_full"), sem("mixT_act"), sem("mixT_dve"), sem("mixT_seq")
        f_full, f_act, f_dve = sem("zx_full"), sem("zx_act"), sem("zx_dve")
        t3_full, t3_act, t3_dve = sem("zxT_full"), sem("zxT_act"), sem("zxT_dve")
        r_full, r_act, r_dve = sem("relu_full"), sem("relu_act"), sem("relu_dve")
        l1_full, l1_act, l1_dve = sem("last_full"), sem("last_act"), sem("last_dve")
        pe_step, act_step, dve_step = sem("pe_step"), sem("act_step"), sem("dve_step")
        att = [dict(pe=sem(f"att{i}_pe"), act=sem(f"att{i}_act"), dve=sem(f"att{i}_dve")) for i in range(2)]
        piece_seq, idx_ready = sem("piece_seq"), sem("idx_ready")
        att_seq = [sem("att0_seq"), sem("att1_seq")]
        dve_seq, end_seq = sem("dve_seq"), sem("end_seq")
        saved, out_ready, stored = sem("saved"), sem("out_ready"), sem("stored")

        N_LOADS = 18

        def ux_tile(t):
            return (strided(ux, t * 32, [(2, 16), (P, M1), (1, 2)]),
                    strided(ps, (2 + t) * BANK, [(2 * M1, 16), (2, M1), (1, 2)]))

        def vk_tile(t):
            return (strided(vk, t * 6, [(1, 6), (J, 6), (M1, M1)]),
                    strided(ps, (5 + t) * BANK, [(FX, 6), (M1, 6), (1, M1)]))

        def mixed_tile(t):
            return (strided(mixed, t * 24, [(4, 6), (48, 12), (1, 4)]),
                    strided(ps, (6 + t) * BANK, [(48, 6), (4, 12), (1, 4)]))

        def mixT_tile(k):
            r = (0, 4 * M1)
            return (strided(mixT, k * BANK, [(P, 4), (C, GB), (1, C)], r),
                    strided(ps, (2 + k) * BANK, [(C, 4), (P, GB), (1, C)], r))

        def zx_tile(k):
            return (strided(zx, k * 8, [(2, 4), (32, S), (1, 2)]),
                    strided(ps, (5 + k) * BANK, [(P, 4), (2, S), (1, 2)]))

        def pixT_tile(t):
            return (strided(pixT, (t // 2 * 8 + t % 2) * P, [(2 * P, 4), (1, P)]),
                    strided(ps, (6, 7, 2, 3, 4, 5, 6, 7)[t] * BANK, [(P, 4), (1, P)]))

        def oT_tile(b2):
            return (strided(oT, b2 * S, [(P, 2), (2 * P, 4), (1, S)]),
                    strided(ps, b2 * BANK, [(4 * S, 2), (S, 4), (1, S)]))

        block = ctx.enter_context(nc.Block())

        @block.sync
        def _(sp):
            loads = [(cst[:, :], const), (w2_all[:, :], w2s), (b2_all[0:2 * C, :], b2), (w2q_s[0:C + 1, :], w2q),
                     (q1_s[0:C + 1, :], q1t), (q2_s[:, :], q2c), (q2b_s[:, :], q2b), (b1_all[0:1, :], b1),
                     (wq_s[0:S + 1, :], wq), (wk_s[0:S + 1, :], wk), (wv_s[0:S + 1, :], wv), (wpk_s[0:S + 1, :], wpk),
                     (wq2_s[0:S + 1, :], wq2), (wu_s[:, :], wu), (wo_s[:, :], wo), (bu_s[:, :], bu), (pk_s[:, :], pk),
                     (w1_all[:, :], w1s)]
            assert len(loads) == N_LOADS
            sp.dma_start(img_in[:, :], x[0]).then_inc(img_sem, 16)
            for dst, src in loads:
                sp.dma_start(dst, src).then_inc(loaded, 16)
            def layer_weights(g):
                with sp.Fori(1, L) as l:
                    sp.wait_ge(m_full, (g * L + l) * 2)
                    sp.dma_start(fw_now[:, :], fw[bass.ds(l, 1)].rearrange("a p n -> (a p) n")).then_inc(fw_sem, 16)

            sp.dma_start(fw_now[:, :], fw[0]).then_inc(fw_sem, 16)
            with sp.Fori(1, G) as g:
                layer_weights(g - 1)
                sp.wait_ge(m_full, g * L * 2)
                sp.dma_start(fw_now[:, :], fw[0]).then_inc(fw_sem, 16)
                sp.wait_ge(img_done, g)
                sp.dma_start(img_in[:, :], x[bass.ds(g, 1)].rearrange("a p n -> (a p) n")).then_inc(img_sem, 16)
            layer_weights(G - 1)

        @block.tensor
        def _(pe):
            def mm(out_, lhsT, rhs, start=True, stop=True, **kw):
                return nc.tensor.matmul(out_, lhsT, rhs, start=start, stop=stop, **kw)

            def turned(out_, in_, rows=P):
                return nc.tensor.transpose(out_, in_, ident[0:rows, 0:rows])

            def pix_tile(c, bank, sem_):
                for i in range(4):
                    xp = 4 * c + i
                    last = turned(ps[:, bank, i * P:(i + 1) * P], pixT[:, xp * P:(xp + 1) * P])
                last.then_inc(sem_, 1)

            def mid_layer(weights, last):
                for c in range(8):
                    q = c % 4
                    ins = mm(ps[32 * q:32 * q + 32, c // 4, :], weights, pix[:, c * BANK:(c + 1) * BANK],
                             start=False, stop=last, skip_group_check=True)
                return ins

            def layer(n):
                for xp in range(XP):
                    t, i = divmod(xp, 8)
                    ins = mm(ps[:, 2 + t, i * FY:i * FY + PAD], pixT[:, xp * P:(xp + 1) * P], const_of("fy"))
                    if i == 7:
                        ins.then_inc(a_full, 1)
                pix_tile(0, 6, t1_full)
                pix_tile(1, 7, t1_full)
                pe.wait_ge(a_act, n * 2 + 2)
                pe.wait_ge(a_dve, n * 2 + 2)
                pix_tile(2, 2, t1_full)
                pix_tile(3, 3, t1_full)
                pe.wait_ge(t1_act, n * 4 + 1)
                for ky in range(M1):
                    t, i = divmod(ky, 4)
                    ins = turned(ps[:, 4 + t, i * P:(i + 1) * P], ux[:, ky * P:(ky + 1) * P])
                    if i == 3:
                        ins.then_inc(t2_full, 1)
                pe.wait_ge(t1_dve, n * 4 + 2)
                pe.wait_ge(t1_act, n * 4 + 2)
                pix_tile(4, 7, t1_full)
                pix_tile(5, 2, t1_full)
                pix_tile(6, 3, t1_full)
                pe.wait_ge(t2_act, n * 2 + 2)
                pe.wait_ge(t2_dve, n + 1)
                pix_tile(7, 4, t1_full)
                for ky in range(M1):
                    t, i = divmod(ky, 6)
                    ins = mm(ps[:, 5 + t, i * FX:i * FX + PAD], uxT[:, ky * P:(ky + 1) * P], const_of("fx"))
                    if i == 5:
                        ins.then_inc(v_full, 1)
                pe.wait_ge(staged, n * 3 + 3)
                pe.wait_ge(t1_act, n * 4 + 4)
                pe.wait_ge(t1_dve, n * 4 + 4)
                mid_layer(q_now[:, :], False).then_inc(q_full, 1)
                pe.wait_ge(v_act, n + 1)
                wait_apart(pe, v_dve, n + 1, pe_turns)
                for ro in range(2):
                    for half in range(2):
                        for ri in range(2):
                            comp = (0, 2, 1, 0)[2 * ro + ri]
                            slot = 2 * half + ri
                            for b in range(GB):
                                r = slice(32 * b, 32 * b + 32)
                                ins = mm(ps[32 * slot:32 * slot + 32, 2 + b, ro * J:(ro + 1) * J], w2_now[r, :],
                                         vk[r, (2 * comp + half) * J:(2 * comp + half + 1) * J], skip_group_check=True)
                ins.then_inc(c_full, 1)
                pe.wait_ge(fw_sem, n * 16 + 16)
                pe.wait_ge(c_done, n + 1)
                for kx in range(M1):
                    for ky in range(M1):
                        j, q = kx * M1 + ky, ky % 4
                        at = ((kx % 6) * 3 + ky // 4) * 16
                        ins = mm(ps[32 * q:32 * q + 32, 6 + kx // 6, at:at + 16], fw_now[:, j * C:(j + 1) * C],
                                 modes[:, j * 16:(j + 1) * 16], skip_group_check=True)
                    if kx % 6 == 5:
                        ins.then_inc(m_full, 1)
                pe.wait_ge(m_act, n + 1)
                pe.wait_ge(m_dve, n + 1)
                for kyi in range(3):
                    for b in range(GB):
                        ins = mm(ps[0:4 * M1, 2 + kyi, b * P:(b + 1) * P],
                                 mixed[:, (kyi * GB + b) * 48:(kyi * GB + b + 1) * 48], w1_now[:, :])
                    ins.then_inc(e_full, 1)
                pe.wait_ge(e_act, n + 1)
                pe.wait_ge(e_dve, n * 2 + 2)
                for ky in range(M1):
                    kyi, q = divmod(ky, 4)
                    ins = mm(ps[:, 5 + kyi, q * P:(q + 1) * P],
                             mixT[:, ky * P:(ky + 1) * P], const_of("iv"))
                    if q == 3:
                        ins.then_inc(f_full, 1)
                pe.wait_ge(f_act, n * 2 + 2)
                pe.wait_ge(f_dve, n + 1)
                for xq in range(16):
                    t, i = divmod(xq, 4)
                    ins = turned(ps[:, 2 + t, i * P:(i + 1) * P], zx[:, xq * P:(xq + 1) * P])
                    if i == 3:
                        ins.then_inc(t3_full, 1)
                pe.wait_ge(t3_act, n * 2 + 2)
                pe.wait_ge(t3_dve, n * 2 + 2)
                o = CONST_AT["g"][0]
                for t in range(8):
                    xqq, p = divmod(t, 2)
                    if t == 6:
                        pe.wait_ge(r_act, n * 4 + 1)
                    if t == 7:
                        pe.wait_ge(r_dve, n * 4 + 1)
                    mm(ps[:, (6, 7, 2, 3, 4, 5, 6, 7)[t], :], cst[:, o + p * P:o + (p + 1) * P],
                       zxT[:, xqq * BANK:(xqq + 1) * BANK]).then_inc(r_full, 1)
                pe.wait_ge(r_act, n * 4 + 4)
                pe.wait_ge(r_dve, n * 4 + 4)

            def tokenizer(g):
                pe.wait_ge(img_done, g + 1)
                for c in range(8):
                    q = c % 4
                    mm(ps[32 * q:32 * q + 32, c // 4, 0:16], zero[:, 0:C], zero[:, 0:16], start=True, stop=False,
                       skip_group_check=True)
                with pe.Fori(0, L) as l:
                    layer(g * L + l)
                for c in range(8):
                    if c == 6:
                        pe.wait_ge(l1_act, g * 4 + 1)
                        pe.wait_ge(l1_dve, g * 4 + 1)
                    pix_tile(c, (2, 3, 4, 5, 6, 7, 2, 3)[c], l1_full)
                pe.wait_ge(l1_act, g * 4 + 4)
                pe.wait_ge(l1_dve, g * 4 + 4)
                mid_layer(q_all[:, L * C:(L + 1) * C], True).then_inc(pe_step, 1)
                reached(pe, act_step, ACT_STEPS, "mid", g)
                for i in range(8):
                    ins = mm(ps[:, 4, i * 16:(i + 1) * 16], mid[:, i * P:(i + 1) * P], q2blk[:, :])
                ins.then_inc(pe_step, 1)
                reached(pe, dve_step, DVE_STEPS, "image", g, pe_turns)
                for t in range(2):
                    ins = turned(ps[:, 5, t * S:(t + 1) * S], hT[0:S, t * P:(t + 1) * P], S)
                ins.then_inc(pe_step, 1)

            def features_down(g, name):
                reached(pe, dve_step, DVE_STEPS, name, g, pe_turns)
                for t in range(2):
                    ins = turned(ps[0:S, 6, t * P:(t + 1) * P], xn[:, t * S:(t + 1) * S])
                ins.then_inc(pe_step, 1)

            def attention(i, turn):
                at, steps = att[i], ATT_PE[i]
                X, W = ((xT, wq_s), (xT2p, wq2_s))[i]
                for t in range(4):
                    for h in (2 * t, 2 * t + 1):
                        ins = mm(ps[0:S, 2 + t, (h % 2) * 256:(h % 2 + 1) * 256], W[0:S + 1, h * S:(h + 1) * S], X[0:S + 1, :])
                    ins.then_inc(at["pe"], 1)
                for t in range(4):
                    for h in (2 * t, 2 * t + 1):
                        if i == 0:
                            ins = mm(ps[0:S, (6, 7, 0, 1)[t], (h % 2) * 256:(h % 2 + 1) * 256],
                                     wk_s[0:S + 1, h * S:(h + 1) * S], X[0:S + 1, :])
                        else:
                            for tt in range(2):
                                ins = turned(ps[0:S, (6, 7, 0, 1)[t], (h % 2) * 256 + tt * P:(h % 2) * 256 + (tt + 1) * P],
                                             kv[:, (tt * HE + h) * P:(tt * HE + h) * P + S])
                    ins.then_inc(at["pe"], 1)
                if i == 0:
                    for t in range(2):
                        reached(pe, at["act"], ATT_ACT[i], f"q{t}", turn)
                        mm(ps[:, 2 + t, :], X[0:S + 1, t * P:(t + 1) * P], wv_s[0:S + 1, :]).then_inc(at["pe"], 1)
                reached(pe, at["act"], ATT_ACT[i], "q3", turn)
                reached(pe, at["dve"], ATT_DVE, "k3", turn, pe_turns)
                for hp in range(4):
                    for b in range(GB):
                        for h2 in range(2):
                            h = 2 * hp + h2
                            c = h * GB * S + b * S
                            ins = mm(ps[S * h2:S * h2 + S, 4 + hp // 2, (hp % 2) * 256 + b * S:(hp % 2) * 256 + (b + 1) * S],
                                     qT[:, c:c + S], kT[:, c:c + S], skip_group_check=True)
                ins.then_inc(at["pe"], 1)
                reached(pe, at["dve"], ATT_DVE, "prob", turn)
                for k in range(8):
                    ins = turned(ps[:, 6 + k // 4, (k % 4) * P:(k % 4 + 1) * P], sc[:, k * P:(k + 1) * P])
                    if k % 4 == 3:
                        ins.then_inc(at["pe"], 1)
                reached(pe, at["act"], ATT_ACT[i], "pT", turn)
                reached(pe, at["dve"], ATT_DVE, "pT", turn, pe_turns)
                for hp in range(4):
                    for bp in range(2):
                        for h2 in range(2):
                            for b2 in range(2):
                                r = slice(S * b2, S * b2 + S)
                                h = 2 * hp + h2
                                v = vv[r, bp * 512 + h * S:bp * 512 + (h + 1) * S] if i == 0 else \
                                    kv[r, (bp * HE + h) * P + S:(bp * HE + h + 1) * P]
                                ins = mm(ps[S * h2:S * h2 + S, b2, (bp * 4 + hp) * S:(bp * 4 + hp + 1) * S], v,
                                         pT[r, (hp * 2 + bp) * P + h2 * S:(hp * 2 + bp) * P + (h2 + 1) * S],
                                         skip_group_check=True)
                ins.then_inc(at["pe"], 1)
                reached(pe, at["act"], ATT_ACT[i], "oT", turn)
                reached(pe, at["dve"], ATT_DVE, "oT", turn)
                W = (wu_s, wo_s)[i]
                for bp in range(2):
                    for hp in range(4):
                        ins = mm(ps[:, 2, bp * S:(bp + 1) * S], oT[:, (hp * 2 + bp) * P:(hp * 2 + bp + 1) * P],
                                 W[:, hp * S:(hp + 1) * S], start=(hp == 0), stop=(hp == 3), skip_group_check=True)
                ins.then_inc(at["pe"], 1)

            def key_scores(g):
                reached(pe, act_step, ACT_STEPS, "x2", g)
                for c in range(4):
                    ins = mm(ps[:, 3 + c // 2, (c % 2) * 256:(c % 2 + 1) * 256], wpk_s[0:S + 1, c * P:(c + 1) * P], xT2[0:S + 1, :])
                ins.then_inc(pe_step, 1)
                reached(pe, act_step, ACT_STEPS, "qpk", g)
                for t in range(2):
                    for c in range(4):
                        ins = mm(ps[:, (5, 6, 7, 0)[2 * t + c // 2], (c % 2) * 256:(c % 2 + 1) * 256],
                                 qpk[:, c * 256 + t * P:c * 256 + (t + 1) * P], pk_s[:, c * 256:(c + 1) * 256])
                    ins.then_inc(pe_step, 1)

            def group(g):
                tokenizer(g)
                features_down(g, "xn1")
                reached(pe, act_step, ACT_STEPS, "x1", g)
                attention(0, g)
                features_down(g, "xn2")
                key_scores(g)

            pe.wait_ge(loaded, 16 * N_LOADS)
            for s in range(1, L + 1):
                mm(ps[:, 2, s * MID:(s + 1) * MID], w2q_s[0:C + 1, s * P:(s + 1) * P], q1_s[0:C + 1, :],
                   skip_group_check=True)
            for k, s in enumerate([0] + list(range(L + 1, 2 * L + 1))):
                ins = mm(ps[:, 2, 0:MID], w2q_s[0:C + 1, s * P:(s + 1) * P], q1_s[0:C + 1, :],
                         start=(k == 0), stop=(k == L), skip_group_check=True)
            ins.then_inc(qall_pe, 1)
            pe.wait_ge(built, 1)
            group(0)
            with pe.Fori(1, G) as g:
                group(g)
                pe.wait_ge(slots, RING + g * PIECES)
                pe.wait_ge(saved, g)
                reached(pe, act_step, ACT_STEPS, "sims1", g)
                attention(1, g - 1)
            pe.wait_ge(slots, RING + G * PIECES)
            pe.wait_ge(saved, G)
            attention(1, G - 1)

        @block.scalar
        def _(act):
            def copy(out_, in_, func=ACT.Copy, **kw):
                return nc.scalar.activation(out_, in_, func, **kw)

            def bank(b, n=BANK, rows=(0, P)):
                return ps[rows[0]:rows[1], b, 0:n]

            def layer(g, l):
                n = g * L + l
                copy(w2_now[:, :], w2_all[:, bass.ds(l * C, C)]).then_inc(staged, 1)
                copy(w1_now[:, :], w1_all[:, bass.ds(l * P, P)]).then_inc(staged, 1)
                copy(q_now[:, :], q_all[:, bass.ds(l * C, C)]).then_inc(staged, 1)
                for t in (0, 2):
                    act.wait_ge(a_full, n * 4 + t + 1)
                    copy(*ux_tile(t)).then_inc(a_act, 1)
                for c, b in ((0, 6), (2, 2)):
                    act.wait_ge(t1_full, n * 8 + c + 1)
                    copy(pix[:, c * BANK:(c + 1) * BANK], bank(b)).then_inc(t1_act, 1)
                act.wait_ge(t2_full, n * 3 + 1)
                copy(uxT[:, 0:BANK], bank(4)).then_inc(t2_act, 1)
                act.wait_ge(t2_full, n * 3 + 3)
                copy(uxT[:, 2 * BANK:3 * BANK], bank(6)).then_inc(t2_act, 1)
                act.wait_ge(t1_full, n * 8 + 6)
                copy(pix[:, 5 * BANK:6 * BANK], bank(2)).then_inc(t1_act, 1)
                act.wait_ge(v_full, n * 2 + 1)
                copy(*vk_tile(0)).then_inc(v_act, 1)
                act.wait_ge(t1_full, n * 8 + 8)
                copy(pix[:, 7 * BANK:8 * BANK], bank(4)).then_inc(t1_act, 1)
                act.wait_ge(m_full, n * 2 + 1)
                copy(*mixed_tile(0)).then_inc(m_act, 1)
                act.wait_ge(e_full, n * 3 + 2)
                copy(*mixT_tile(1)).then_inc(e_act, 1)
                for k in (0, 2):
                    act.wait_ge(f_full, n * 3 + k + 1)
                    copy(*zx_tile(k)).then_inc(f_act, 1)
                for t in (1, 3):
                    act.wait_ge(t3_full, n * 4 + t + 1)
                    copy(zxT[:, t * BANK:(t + 1) * BANK], bank(2 + t)).then_inc(t3_act, 1)
                for t in (0, 2, 4, 6):
                    act.wait_ge(r_full, n * 8 + t + 1)
                    copy(*pixT_tile(t), ACT.Relu).then_inc(r_act, 1)

            def tokenizer(g):
                with act.Fori(0, L) as l:
                    layer(g, l)
                for c in (0, 2, 4, 6):
                    act.wait_ge(l1_full, g * 8 + c + 1)
                    copy(pix[:, c * BANK:(c + 1) * BANK], bank((2, 3, 4, 5, 6, 7, 2, 3)[c])).then_inc(l1_act, 1)
                reached(act, pe_step, PE_STEPS, "mid", g)
                copy(mid[:, :], ps[:, 0:2, :].rearrange("p a b -> p (a b)"), ACT.Relu).then_inc(act_step, 1)

            def deviation(g, i):
                reached(act, dve_step, DVE_STEPS, f"var{i}", g)
                nc.scalar.activation(rs[:, 0:2], rs[:, 2:4], ACT.Sqrt).then_inc(act_step, 1)
                reached(act, pe_step, PE_STEPS, f"x{i}", g)
                copy((xT, xT2)[i - 1][0:S, :], bank(6, 256, (0, S))).then_inc(act_step, 1)

            def attention(i, turn):
                at = att[i]
                for t in range(4):
                    reached(act, at["pe"], ATT_PE[i], f"q{t}", turn)
                    copy(qT[:, t * BANK:(t + 1) * BANK], bank(2 + t, BANK, (0, S)), scale=float(S) ** -0.5).then_inc(at["act"], 1)
                if i == 0:
                    for t in range(2):
                        reached(act, at["pe"], ATT_PE[i], f"v{t}", turn)
                        copy(vv[:, t * BANK:(t + 1) * BANK], bank(2 + t)).then_inc(at["act"], 1)
                reached(act, at["dve"], ATT_DVE, "shifted", turn)
                nc.scalar.activation(sc[:, 0:1024], sc[:, 0:1024], ACT.Exp).then_inc(at["act"], 1)
                reached(act, at["pe"], ATT_PE[i], "pT0", turn)
                copy(pT[:, 0:BANK], bank(6)).then_inc(at["act"], 1)
                reached(act, at["pe"], ATT_PE[i], "o", turn)
                copy(*oT_tile(0)).then_inc(at["act"], 1)

            def group(g):
                tokenizer(g)
                deviation(g, 1)
                attention(0, g)
                deviation(g, 2)
                reached(act, pe_step, PE_STEPS, "qpk", g)
                copy(qpk[:, :], ps[:, 3:5, :].rearrange("p a b -> p (a b)")).then_inc(act_step, 1)
                for t in range(2):
                    reached(act, pe_step, PE_STEPS, f"sims{t}", g)
                    copy(sims[:, 0:BANK], bank((5, 7)[t]))
                    copy(sims[:, BANK:2 * BANK], bank((6, 0)[t])).then_inc(act_step, 1)
                    reached(act, dve_step, DVE_STEPS, f"top{t}", g)
                    nc.scalar.activation(top[:, :], top[:, :], ACT.Exp).then_inc(act_step, 1)

            def store(turn):
                act.wait_ge(out_ready, turn + 1)
                act.dma_start(out[bass.ds(turn, 1)].rearrange("a t p n -> p (a t) n"),
                              res[:, :].rearrange("p (t n) -> p t n", t=2)).then_inc(stored, 16)

            act.wait_ge(built, 1)
            group(0)
            with act.Fori(1, G) as g:
                group(g)
                attention(1, g - 1)
                store(g - 1)
            attention(1, G - 1)
            store(G - 1)
            act.wait_ge(stored, 16 * G + 16)

        @block.vector
        def _(dve):
            v = nc.vector

            def bank(b, n=BANK, rows=(0, P)):
                return ps[rows[0]:rows[1], b, 0:n]

            def relu(out_, in_):
                return v.tensor_scalar(out_, in_, 0.0, None, ALU.max)

            def piece(k, turn):
                slot = k % RING
                dve.wait_ge(gath[slot], (turn * (PIECES // RING) + k // RING + 1) * K * 16)
                rows = strided(ring, slot * K * P, [(P, K), (1, P)])
                v.tensor_tensor(rows, rows, strided(wts, k * K, [(1, K), (0, P)]), ALU.mult).then_inc(piece_seq, 1)
                dve.wait_ge(piece_seq, turn * PIECES + k + 1)
                v.tensor_reduce(kv[:, k * P:(k + 1) * P], strided(ring, slot * K * P, [(1, P), (P, K)]), AX.X,
                                ALU.add).then_inc(slots, 1)

            def layer(g, l, take):
                n = g * L + l
                for t in (1, 3):
                    dve.wait_ge(a_full, n * 4 + t + 1)
                    v.tensor_copy(*ux_tile(t)).then_inc(a_dve, 1)
                for c, b in ((1, 7), (3, 3)):
                    dve.wait_ge(t1_full, n * 8 + c + 1)
                    v.tensor_copy(pix[:, c * BANK:(c + 1) * BANK], bank(b)).then_inc(t1_dve, 1)
                dve.wait_ge(t2_full, n * 3 + 2)
                v.tensor_copy(uxT[:, BANK:2 * BANK], bank(5)).then_inc(t2_dve, 1)
                for c, b in ((4, 7), (6, 3)):
                    dve.wait_ge(t1_full, n * 8 + c + 1)
                    v.tensor_copy(pix[:, c * BANK:(c + 1) * BANK], bank(b)).then_inc(t1_dve, 1)
                dve.wait_ge(v_full, n * 2 + 2)
                v.tensor_copy(*vk_tile(1)).then_inc(v_dve, 1)
                take(0)
                dve.wait_ge(c_full, n + 1)
                for h in range(2):
                    m = strided(modes, 2 * h, [(4, GB), (1, 2), (16, J)], (64 * h, 64 * h + 64))
                    v.tensor_tensor(m, m, strided(ps, 2 * BANK, [(BANK, GB), (J, 2), (1, J)], (64 * h, 64 * h + 64)),
                                    ALU.add).then_inc(c_seq, 1)
                dve.wait_ge(c_seq, n * 2 + 2)
                v.tensor_tensor(modes[0:2 * C, 0:16], modes[0:2 * C, 0:16], b2_all[0:2 * C, l * 16:(l + 1) * 16],
                                ALU.add).then_inc(c_done, 1)
                take(1)
                dve.wait_ge(m_full, n * 2 + 2)
                v.tensor_copy(*mixed_tile(1)).then_inc(m_dve, 1)
                dve.wait_ge(e_full, n * 3 + 1)
                v.tensor_copy(*mixT_tile(0)).then_inc(e_seq, 1)
                dve.wait_ge(e_seq, n + 1)
                m = strided(mixT, 0, [(C, GB), (1, C)], (0, 1))
                v.tensor_tensor(m, m, strided(b1_all, l * C, [(0, GB), (1, C)], (0, 1)), ALU.add).then_inc(e_dve, 1)
                dve.wait_ge(e_full, n * 3 + 3)
                v.tensor_copy(*mixT_tile(2)).then_inc(e_dve, 1)
                dve.wait_ge(f_full, n * 3 + 2)
                v.tensor_copy(*zx_tile(1)).then_inc(f_dve, 1)
                for t in (0, 2):
                    dve.wait_ge(t3_full, n * 4 + t + 1)
                    v.tensor_copy(zxT[:, t * BANK:(t + 1) * BANK], bank(2 + t)).then_inc(t3_dve, 1)
                for t in (1, 3, 5, 7):
                    dve.wait_ge(r_full, n * 8 + t + 1)
                    relu(*pixT_tile(t)).then_inc(r_dve, 1)
                take(2)

            def spread_images(g, seq):
                seq.add(v.memset(pixT[:, :], 0.0))
                seq.add(v.memset(modes[:, :], 0.0))
                dve.wait_ge(img_sem, 16 * (g + 1))
                seq.so_far(dve)
                v.tensor_copy(strided(pixT, 0, [(C, XP * GB)]), img_in[:, :])
                for k in range(3):
                    ins = v.tensor_copy(strided(pixT, k + 1, [(P, XP), (C, GB)]),
                                        strided(cst, CONST_AT["grid"][0] + k, [(3, XP), (0, GB)]))
                ins.then_inc(img_done, 1)

            def normalise(h, i, g, seq):
                for t in range(2):
                    seq.add(v.bn_stats(stat[:, 6 * t:6 * t + 6], h[:, t * S:(t + 1) * S]))
                seq.so_far_apart(dve, dve_turns)
                for t in range(2):
                    seq.add(v.bn_aggr(mv[:, 2 * t:2 * t + 2], stat[:, 6 * t:6 * t + 6]))
                seq.so_far(dve)
                var, sd, r, u = rs[:, 2:4], rs[:, 0:2], rs[:, 4:6], rs[:, 6:8]
                v.tensor_scalar(var, strided(mv, 1, [(2, 2)]), EPS, None, ALU.add).then_inc(dve_step, 1)
                reached(dve, act_step, ACT_STEPS, f"sd{i}", g)
                seq.add(v.reciprocal(r, sd))
                seq.so_far(dve)
                seq.add(v.tensor_tensor(u, r, r, ALU.mult))
                seq.so_far(dve)
                seq.add(v.tensor_tensor(u, u, var, ALU.mult))
                seq.so_far(dve)
                seq.add(v.tensor_scalar(u, u, -0.5, 1.5, ALU.mult, ALU.add))
                seq.so_far(dve)
                seq.add(v.tensor_tensor(r, r, u, ALU.mult))
                seq.so_far(dve)
                for t in range(2):
                    ins = v.tensor_scalar(xn[:, t * S:(t + 1) * S], h[:, t * S:(t + 1) * S], mv[:, 2 * t:2 * t + 1],
                                          rs[:, 4 + t:5 + t], ALU.subtract, ALU.mult)
                ins.then_inc(dve_step, 1)

            def attention(i, turn):
                at, seq = att[i], Steps(att_seq[i], (5, 4)[i], turn)
                for t in range(4):
                    reached(dve, at["pe"], ATT_PE[i], f"k{t}", turn)
                    v.tensor_copy(kT[:, t * BANK:(t + 1) * BANK], bank((6, 7, 0, 1)[t], BANK, (0, S))).then_inc(at["dve"], 1)
                reached(dve, at["pe"], ATT_PE[i], "scores", turn)
                rows = strided(sc, 0, [(S, 16), (1, S)])
                o = CONST_AT[("strict", "causal")[i]][0]
                seq.add(v.tensor_tensor(rows, strided(ps, 4 * BANK, [(S, 16), (1, S)]),
                                        strided(cst, o, [(0, 16), (1, S)]), ALU.add))
                seq.so_far(dve)
                seq.add(v.tensor_reduce(red[:, 0:16], rows, AX.X, ALU.max))
                seq.so_far(dve)
                v.tensor_tensor(rows, rows, strided(red, 0, [(1, 16), (0, S)]), ALU.subtract).then_inc(at["dve"], 1)
                reached(dve, at["act"], ATT_ACT[i], "exp", turn)
                seq.add(v.tensor_reduce(red[:, 16:32], rows, AX.X, ALU.add))
                seq.so_far(dve)
                seq.add(v.reciprocal(red[:, 32:48], red[:, 16:32]))
                seq.so_far(dve)
                if i == 0:
                    seq.add(v.tensor_scalar(red[:, 32:48], red[:, 32:48], const_of("rows"), None, ALU.mult))
                    seq.so_far(dve)
                v.tensor_tensor(rows, rows, strided(red, 32, [(1, 16), (0, S)]), ALU.mult).then_inc(at["dve"], 1)
                reached(dve, at["pe"], ATT_PE[i], "pT1", turn)
                v.tensor_copy(pT[:, BANK:2 * BANK], bank(7)).then_inc(at["dve"], 1)
                reached(dve, at["pe"], ATT_PE[i], "o", turn)
                v.tensor_copy(*oT_tile(1)).then_inc(at["dve"], 1)
                reached(dve, at["pe"], ATT_PE[i], "y", turn)
                seq.close()

            def rank(t, g, seq, take):
                ranks = [strided(vi, (r // HE * 2 * HE + r % HE) * K, [(1, K)]) for r in range(2 * HE)]
                reached(dve, act_step, ACT_STEPS, f"sims{t}", g, dve_turns)
                for r in range(2 * HE):
                    ins = v.max(ranks[r][:, 0:8], sims[:, r * NK:(r + 1) * NK])
                seq.add(ins)
                seq.so_far_apart(dve, dve_turns)
                for r in range(2 * HE):
                    ins = v.match_replace(sims2[:, r * NK:(r + 1) * NK], ranks[r][:, 0:8], sims[:, r * NK:(r + 1) * NK], LOWEST)
                seq.add(ins)
                for r in range(2 * HE):
                    v.max_index(iu[:, r * K:r * K + 8], ranks[r][:, 0:8], sims[:, r * NK:(r + 1) * NK])
                seq.so_far_apart(dve, dve_turns)
                for r in range(2 * HE):
                    ins = v.max(ranks[r][:, 8:16], sims2[:, r * NK:(r + 1) * NK])
                seq.add(ins)
                seq.so_far_apart(dve, dve_turns)
                for r in range(2 * HE):
                    ins = v.max_index(iu[:, r * K + 8:r * K + 16], ranks[r][:, 8:16], sims2[:, r * NK:(r + 1) * NK])
                seq.add(ins)
                seq.so_far_apart(dve, dve_turns)
                lo, hi = HE * K, 3 * HE * K
                v.tensor_tensor(strided(vi, lo, [(K, HE), (1, K)]), strided(iu, 0, [(K, HE), (1, K)]),
                                strided(cst, CONST_AT["hoff"][0], [(1, HE), (0, K)]), ALU.add)
                seq.add(v.tensor_scalar(vi[:, hi:hi + HE * K], iu[:, HE * K:2 * HE * K], float(NK), None, ALU.mult))
                seq.so_far(dve)
                at, a = 0, 0
                while a < K:
                    n = PAIRS[a][1]
                    m = sum(1 for _, c in PAIRS if c == n)
                    ins = v.tensor_tensor(strided(cand, at, [(NC, 2 * HE), (n, m), (1, n)]),
                                          strided(vi, a, [(K, 2 * HE), (1, m), (0, n)]),
                                          strided(vi, 2 * HE * K, [(K, 2 * HE), (0, m), (1, n)]), ALU.add)
                    at, a = at + n * m, a + m
                seq.add(ins)
                seq.so_far_apart(dve, dve_turns)
                score = [cand[:, h * NC:(h + 1) * NC] for h in range(HE)]
                rest = [cand2[:, h * NC:(h + 1) * NC] for h in range(HE)]
                for h in range(HE):
                    ins = v.max(top[:, h * K:h * K + 8], score[h])
                seq.add(ins)
                seq.so_far_apart(dve, dve_turns)
                for h in range(HE):
                    ins = v.match_replace(rest[h], top[:, h * K:h * K + 8], score[h], LOWEST)
                seq.add(ins)
                for h in range(HE):
                    v.max_index(pos[:, h * K:h * K + 8], top[:, h * K:h * K + 8], score[h])
                seq.so_far_apart(dve, dve_turns)
                for h in range(HE):
                    ins = v.max(top[:, h * K + 8:h * K + 16], rest[h])
                seq.add(ins)
                seq.so_far_apart(dve, dve_turns)
                for h in range(HE):
                    ins = v.max_index(pos[:, h * K + 8:h * K + 16], top[:, h * K + 8:h * K + 16], rest[h])
                seq.add(ins)
                seq.add(v.tensor_copy(den[:, 0:HE], strided(top, 0, [(K, HE)])))
                seq.so_far(dve)
                v.tensor_tensor(strided(top, 0, [(K, HE), (1, K)]), strided(top, 0, [(K, HE), (1, K)]),
                                strided(den, 0, [(1, HE), (0, K)]), ALU.subtract).then_inc(dve_step, 1)
                seq.add(v.tensor_copy(posf[:, :], pos[:, :]))
                seq.so_far(dve)
                for hh in range(2):
                    hot = oneh[:, 0:HE // 2 * K * NC]
                    seq.add(v.tensor_tensor(hot.rearrange("p (m c) -> p m c", c=NC),
                                            strided(posf, hh * HE // 2 * K, [(1, HE // 2 * K), (0, NC)]),
                                            strided(cst, CONST_AT["iota"][0], [(0, HE // 2 * K), (1, NC)]), ALU.is_equal))
                    seq.so_far(dve)
                    hot3 = strided(oneh, 0, [(K * NC, HE // 2), (NC, K), (1, NC)])
                    seq.add(v.tensor_tensor(hot3, hot3, strided(cand, (HE + hh * HE // 2) * NC, [(NC, HE // 2), (0, K), (1, NC)]),
                                            ALU.mult))
                    seq.so_far(dve)
                    seq.add(v.tensor_reduce(found[:, hh * HE // 2 * K:(hh + 1) * HE // 2 * K],
                                            hot.rearrange("p (m c) -> p m c", c=NC), AX.X, ALU.add))
                    seq.so_far(dve)
                if t == 0:
                    v.tensor_copy(idx[:, 0:HE * K], found[:, :]).then_inc(idx_ready, 1)
                else:
                    seq.add(v.tensor_copy(idx1n[:, :], found[:, :]))
                reached(dve, act_step, ACT_STEPS, f"exp{t}", g)
                w = strided(top, 0, [(K, HE), (1, K)])
                seq.add(v.tensor_reduce(den[:, 0:HE], w, AX.X, ALU.add))
                seq.so_far(dve)
                seq.add(v.reciprocal(den[:, HE:2 * HE], den[:, 0:HE]))
                seq.so_far(dve)
                seq.add(v.tensor_tensor((wts, wts1n)[t][:, 0:HE * K].rearrange("p (h k) -> p h k", k=K), w,
                                        strided(den, HE, [(1, HE), (0, K)]), ALU.mult))
                seq.so_far(dve)

            def group(g, take):
                seq = Steps(dve_seq, DVE_SEQ, g)
                spread_images(g, seq)
                for l in range(L):
                    layer(g, l, lambda i: take(3 * l + i))
                for c in (1, 3, 5, 7):
                    dve.wait_ge(l1_full, g * 8 + c + 1)
                    v.tensor_copy(pix[:, c * BANK:(c + 1) * BANK], bank((2, 3, 4, 5, 6, 7, 2, 3)[c])).then_inc(l1_dve, 1)
                reached(dve, pe_step, PE_STEPS, "image", g)
                for x2 in range(2):
                    for ci in range(2):
                        r = (x2 * S, x2 * S + S)
                        ins = v.tensor_scalar(strided(hT, 32 * ci + x2, [(2, 4), (8, 4), (S, GB)], (0, S)),
                                              strided(ps, 4 * BANK + ci * S, [(16, 4), (4, 4), (1, GB)], r),
                                              q2b_s[r[0]:r[1], 0:1], None, ALU.add)
                ins.then_inc(dve_step, 1)
                reached(dve, pe_step, PE_STEPS, "h1", g)
                v.tensor_copy(h1[:, :], bank(5, 2 * S)).then_inc(dve_step, 1)
                reached(dve, dve_step, DVE_STEPS, "h1", g)
                normalise(h1, 1, g, seq)
                take(12)
                attention(0, g)
                seq.add(v.tensor_tensor(h2[:, :], h1[:, :], bank(2, 2 * S), ALU.add))
                seq.so_far(dve)
                h3 = h2[:, :].rearrange("p (t s) -> p t s", t=2)
                v.tensor_tensor(h3, h3, strided(bu_s, 0, [(0, 2), (1, S)]), ALU.add).then_inc(dve_step, 1)
                reached(dve, dve_step, DVE_STEPS, "h2", g)
                normalise(h2, 2, g, seq)
                take(13)
                rank(0, g, seq, take)
                take(14)
                rank(1, g, seq, take)
                take(15)
                seq.close()

            def set_aside(g, first):
                v.tensor_copy(idx[:, HE * K:2 * HE * K], idx1n[:, :]).then_inc(idx_ready, 1)
                v.tensor_copy(wts[:, HE * K:2 * HE * K], wts1n[:, :])

            def keep_tokens():
                v.tensor_copy(h2p[:, :], h2[:, :])
                v.tensor_copy(xT2p[0:S + 1, :], xT2[0:S + 1, :]).then_inc(saved, 1)

            def finish(turn):
                attention(1, turn)
                dve.wait_ge(stored, 16 * turn + 16)
                v.tensor_tensor(res[:, :], h2p[:, :], bank(2, 2 * S), ALU.add).then_inc(out_ready, 1)

            for z in (zero, modes, zx, mixT, q_all):
                v.memset(z[:, :], 0.0)
            for o in (xT, xT2):
                ins = v.memset(o[S:S + 1, :], 1.0)
            ins.then_inc(memz, 1)
            dve.wait_ge(memz, 1)
            v.memset(res[:, :], 0.0).then_inc(stored, 16)
            v.memset(ring[:, 0:1], 0.0).then_inc(slots, RING)
            dve.wait_ge(loaded, 16 * N_LOADS)
            v.tensor_scalar(b1_all[0:1, :], b1_all[0:1, :], float(S), None, ALU.mult)
            v.tensor_scalar(b2_all[0:2 * C, :], b2_all[0:2 * C, :], float(S), None, ALU.mult)
            v.tensor_scalar(q2blk[:, :], const_of("q2m"), q2_s[:, 0:1], None, ALU.mult)
            dve.wait_ge(qall_pe, 1)
            for s in range(L + 1):
                ins = v.tensor_tensor(strided(q_all, s * C, [(MID, GB), (1, MID)]), strided(ps, 2 * BANK + s * MID, [(0, GB), (1, MID)]),
                                      const_of("img").rearrange("p (b m) -> p b m", m=MID), ALU.mult)
            ins.then_inc(built, 1)

            group(0, lambda k: None)
            set_aside(0, True)
            keep_tokens()
            with dve.Fori(1, G) as g:
                group(g, lambda k: piece(k, g - 1))
                set_aside(g, False)
                finish(g - 1)
                dve.wait_ge(out_ready, g)
                keep_tokens()
            for k in range(PIECES):
                piece(k, G - 1)
            finish(G - 1)

        @block.gpsimd
        def _(pool):
            with pool.Fori(0, G) as g:
                for k in range(PIECES):
                    if k % HE == 0:
                        pool.wait_ge(idx_ready, g * 2 + k // HE + 1)
                    wait_apart(pool, slots, g * PIECES + k + 1, pool_turns)
                    for m in range(K):
                        o = (k % RING * K + m) * P
                        pool.indirect_dma_start(out=ring[:, o:o + P], out_offset=None, in_=table,
                                                in_offset=bass.IndirectOffsetOnAxis(ap=idx[:, k * K + m:k * K + m + 1], axis=0)
                                                ).then_inc(gath[k % RING], 16)


def kernel(**inputs):
    import numpy as _np
    import concourse.bacc as _bacc
    from concourse import mybir as _mybir
    from concourse.bass_utils import run_bass_kernel_spmd as _run

    a = {k.replace("L0_", ""): _np.asarray(v) for k, v in inputs.items()}
    f = _np.float32
    z = lambda *s: _np.zeros(s, f)
    laid = {}
    laid["x"] = a["x"].reshape(G, GB, XP, 2, S).transpose(0, 3, 4, 2, 1).reshape(G, P, XP * GB)
    laid["const"] = CONST
    w2s = z(C, L, C)
    w2s[0:3, 0], w2s[3, 0] = a["tok_p_w"].T, a["tok_p_b"]
    w2s[:, 1:] = a["tok_w2_w"][:L - 1].transpose(2, 0, 1)
    laid["w2s"] = _np.tile(w2s.reshape(C, L * C), (4, 1))
    w1s = z(4, C, L, 4, C)
    for q in range(4):
        w1s[q, :, :, q] = a["tok_w1_w"].transpose(2, 0, 1)
    laid["w1s"] = w1s.reshape(P, L * P)
    laid["fw"] = a["tok_fw"].transpose(0, 1, 6, 2, 4, 5, 3).reshape(L, P, J * C)
    laid["b1"] = a["tok_w1_b"].reshape(1, L * C)
    b2 = z(2, C, L, GB, 2, 2)
    b2[0, :, 1:, :, 0, 0] = a["tok_w2_b"][:L - 1].T[:, :, None]
    b2[1, :, 1:, :, 0, 1] = a["tok_w2_b"][:L - 1].T[:, :, None]
    laid["b2"] = b2.reshape(2 * C, L * 16)
    w2q = z(C + 1, 2 * L + 1, GB, C)
    w2q[:C, 0, :, 0:3] = a["tok_p_w"][:, None]
    w2q[:C, 0, :, 3] = a["tok_p_b"][:, None]
    w2q[C, 0, :, 3] = 1.0
    w2q[:C, 1:L + 1] = a["tok_w2_w"].transpose(1, 0, 2)[:, :, None]
    w2q[:C, L + 1:, :, 3] = a["tok_w2_b"].T[:, :, None]
    laid["w2q"] = w2q.reshape(C + 1, (2 * L + 1) * P)
    laid["q1t"] = _np.concatenate([a["tok_q1_w"].T, a["tok_q1_b"][None]])
    q2 = z(4, 32)
    q2[:, :GB * MID] = _np.tile(a["tok_q2_w"].reshape(1, MID), (4, GB))
    laid["q2c"] = q2.reshape(P, 1)
    laid["q2b"] = _np.tile(a["tok_q2_b"].reshape(1, 1), (P, 1))
    for n, w, b in (("wq", "attn_Wq", "attn_bq"), ("wk", "attn_Wk", "attn_bk"), ("wv", "attn_Wv", "attn_bv")):
        laid[n] = _np.concatenate([a[w], a[b][None]])
    laid["wu"] = a["attn_Wu"].reshape(4, P, S).transpose(1, 0, 2).reshape(P, 4 * S)
    laid["bu"] = _np.tile(a["attn_bu"][None], (P, 1))
    laid["wpk"] = _np.concatenate([a["ffn_Wq_pk"], z(1, HE * S)])
    pk = z(4, 32, 2, 2, 4, NK)
    keys = a["ffn_pk_keys"].reshape(2, NK, 2, 4, 32)
    for h in range(4):
        pk[h, :, :, :, h] = keys[:, :, :, h].transpose(3, 0, 2, 1)
    laid["pk"] = pk.reshape(P, 4 * 4 * NK)
    laid["wq2"] = _np.concatenate([a["ffn_Wq"], z(1, HE * S)])
    laid["wo"] = a["ffn_Wo"].reshape(4, P, S).transpose(1, 0, 2).reshape(P, 4 * S)
    laid["table"] = _np.concatenate([a["ffn_keys_table"], a["ffn_values_table"]], 1)

    nc = _bacc.Bacc("TRN2", target_bir_lowering=False, num_devices=1)
    arrays, args = {}, {}
    for name, v in laid.items():
        v = _np.ascontiguousarray(v)
        arrays[f"in_{name}"] = v
        args[name] = nc.dram_tensor(f"in_{name}", v.shape, _mybir.dt.from_np(v.dtype), kind="ExternalInput").ap()
    args["out"] = nc.dram_tensor("out_h", (G, 2, P, S), F32, kind="ExternalOutput").ap()
    build(nc, **args)
    r = _run(nc, [arrays], core_ids=[0])
    return r.results[0]["out_h"].reshape(B, S, S)
```

```python
from contextlib import ExitStack

import numpy as np

import concourse.bass as bass
from concourse import mybir

ALU = mybir.AluOpType
ACT = mybir.ActivationFunctionType
AX = mybir.AxisListType
F32 = mybir.dt.float32
U32 = mybir.dt.uint32

P = 128
B, S = 32, 64
C = 32
L = 4
M1 = 12
GB = 4
G = B // GB
HE = 8
K = 16
NK = 64
NKV = NK * NK
MID = 4
J = M1 * M1
XP = S // 2
BANK = 512
PAIRS = [(a, K // (a + 1)) for a in range(K)]
NC = sum(n for _, n in PAIRS)
RING = 4
PIECES = 2 * HE
FY, FX = 2 * 2 * M1, 3 * 2 * M1
PAD = 96
CODE = 64
CODE_AT = 7
ROUND = 2.0 ** 23
BIG = 1e30
LOWEST = -3e38
EPS = 1e-5


def shape_constants():
    one = np.zeros
    w = 2 * np.pi / S
    kx = np.concatenate([np.arange(M1), np.arange(S - M1, S)])
    y, ky = np.arange(S), np.arange(M1)
    fy = one((2, S, 2, M1, 2))
    for i in range(2):
        fy[i, :, i, :, 0] = np.cos(w * np.outer(y, ky)) / 8
        fy[i, :, i, :, 1] = -np.sin(w * np.outer(y, ky)) / 8
    fyp = one((P, PAD))
    fyp[:, :FY] = fy.reshape(P, FY)
    co, si = np.cos(w * np.outer(y, kx)) / 8, np.sin(w * np.outer(y, kx)) / 8
    fx = one((S, 2, 3, 2 * M1))
    fx[:, 0, 0], fx[:, 1, 0] = co, si
    fx[:, 0, 1], fx[:, 1, 1] = -si, co
    fx[:, 0, 2], fx[:, 1, 2] = si, -co
    fxp = one((P, PAD))
    fxp[:, :FX] = fx.reshape(P, FX)
    iv = one((M1, 2, 2, S, 2))
    for h in range(2):
        c, s = co[:, h * M1:(h + 1) * M1].T, si[:, h * M1:(h + 1) * M1].T
        iv[:, h, 0, :, 0], iv[:, h, 0, :, 1] = c, s
        iv[:, h, 1, :, 0], iv[:, h, 1, :, 1] = -s, c
    ivp = one((P, P))
    ivp[:4 * M1] = iv.reshape(4 * M1, P)
    g = one((4, 32, 2, 2, S))
    amp = np.where(ky == 0, 1.0, 2.0)[:, None] / 8
    for p in range(2):
        for i in range(2):
            g[2 * p + i, 0:2 * M1:2, p, i] = amp * np.cos(w * np.outer(ky, y))
            g[2 * p + i, 1:2 * M1:2, p, i] = -amp * np.sin(w * np.outer(ky, y))
    lin = np.linspace(0.0, 1.0, S, dtype=np.float32)
    grid = one((2, S, XP, 3))
    grid[..., 0] = lin.reshape(XP, 2).T[:, None, :]
    grid[..., 1] = lin[None, :, None]
    grid[..., 2] = 1.0
    i, j = np.arange(S)[:, None], np.arange(S)[None, :]
    strict = np.tile(np.where(j >= i, -BIG, 0.0), (2, 1))
    causal = np.tile(np.where(j > i, -BIG, 0.0), (2, 1))
    rows = np.tile((np.arange(S) > 0) * 1.0, 2)[:, None]
    img = np.kron(np.eye(GB), np.ones((C, MID)))
    q2m = np.kron(np.eye(4), np.vstack([np.kron(np.eye(GB), np.ones((MID, 1))), one((16, GB))]))
    first = np.cumsum([0] + [n for _, n in PAIRS])[:K]
    code = np.tile(((np.arange(HE)[:, None] * float(NKV) + 1) * CODE + first[None] + CODE_AT).reshape(1, HE * K), (P, 1))
    first = np.tile(first * 1.0, (P, 1))
    iota = np.tile(np.arange(K) - float(CODE_AT), (P, 1))
    parts = dict(fy=fyp, fx=fxp, iv=ivp, g=g.reshape(P, 2 * P), ident=np.eye(P), grid=grid.reshape(P, 3 * XP),
                 strict=strict, causal=causal, rows=rows, img=img, q2m=q2m, code=code, first=first, iota=iota)
    at, o = {}, 0
    for n, a in parts.items():
        at[n] = (o, a.shape[1])
        o += a.shape[1]
    return at, np.ascontiguousarray(np.concatenate(list(parts.values()), 1), dtype=np.float32)


CONST_AT, CONST = shape_constants()

PE_STEPS = ["mid", "image", "h1", "x1", "x2", "qpk", "sims0", "sims1"]
ACT_STEPS = ["mid", "sd1", "x1", "sd2", "x2", "qpk", "sims0", "sims1"]
DVE_STEPS = ["image", "h1", "var1", "xn1", "h2", "var2", "xn2"]
ATT_PE = [["q0", "q1", "q2", "q3", "k0", "k1", "k2", "k3", "v0", "v1", "scores", "pT0", "pT1", "o", "y"],
          ["q0", "q1", "q2", "q3", "k0", "k1", "k2", "k3", "scores", "pT0", "pT1", "o", "y"]]
ATT_ACT = [["q0", "q1", "q2", "q3", "v0", "v1", "exp", "pT", "oT"], ["q0", "q1", "q2", "q3", "exp", "pT", "oT"]]
ATT_DVE = [["k0", "k1", "k2", "k3", "shifted", "prob", "pT", "oT"], ["k0", "k1", "k2", "k3", "shifted", "prob"]]
BANKS = [dict(q=(2, 3, 4, 5), k=(6, 7, 2, 3), v=(4, 5), scores=6, pT=6, o=0, y=5),
         dict(q=(4, 5, 6, 7), k=(2, 3, 4, 5), scores=0, pT=0, o=2, y=4)]


def wait_apart(eng, sem, value, turns):
    eng.wait_ge(sem, value)
    if not isinstance(value, int):
        eng.sem_inc(turns, 1)


def reached(eng, sem, steps, name, turn, apart_from=None):
    value = turn * len(steps) + steps.index(name) + 1
    if apart_from is None:
        eng.wait_ge(sem, value)
    else:
        wait_apart(eng, sem, value, apart_from)


def strided(t, start, dims, rows=(0, P)):
    pitch = 1
    for n in t.shape[1:]:
        pitch *= n
    return bass.AP(tensor=t, offset=start + rows[0] * pitch,
                   ap=[[pitch, rows[1] - rows[0]]] + [[a, b] for a, b in dims])


BY_ACT = [0, 1, 3, 4, 5, 7, 11, 12, 14, 15]
DVE_SEQ = 19
RANK_SEQ = 58
LAST_SEQ = 5


class Steps:

    def __init__(self, sem, per, turn):
        self.sem, self.per, self.turn, self.n = sem, per, turn, 0

    def add(self, ins):
        ins.then_inc(self.sem, 1)
        self.n += 1

    def so_far(self, eng):
        eng.wait_ge(self.sem, self.turn * self.per + self.n)

    def so_far_apart(self, eng, turns):
        wait_apart(eng, self.sem, self.turn * self.per + self.n, turns)

    def close(self):
        assert self.n == self.per, (self.sem, self.n)


def build(nc, x, const, w2s, w1s, fw, b1, b2, w2q, q1t, q2c, q2b, wq, wk, wv, wu, bu, wpk, pk, wq2, wo, table, out):
    ctx = ExitStack()
    with ctx:
        def sb(name, n, dt=F32):
            return ctx.enter_context(nc.sbuf_tensor(name, [P, n], dt))

        def sem(name):
            return ctx.enter_context(nc.semaphore(name))

        cst = sb("cst", CONST.shape[1])

        def const_of(name, rows=(0, P)):
            o, n = CONST_AT[name]
            return cst[rows[0]:rows[1], o:o + n]

        ident = const_of("ident")
        w2_all, w1_all = sb("w2_all", L * C), sb("w1_all", L * P)
        w2_now, w1_now, q_now = sb("w2_now", C), sb("w1_now", P), sb("q_now", C)
        q_all = sb("q_all", (L + 1) * C)
        fw_now = sb("fw_now", J * C)
        b1_all, b2_all = sb("b1_all", L * C), sb("b2_all", L * 16)
        q1_s, q2_s, q2b_s, q2blk = sb("q1_s", MID), sb("q2_s", 1), sb("q2b_s", 1), sb("q2blk", 16)
        wq_s, wk_s, wv_s, wpk_s, wq2_s = (sb(n, HE * S) for n in ("wq_s", "wk_s", "wv_s", "wpk_s", "wq2_s"))
        wu_s, wo_s, bu_s = sb("wu_s", 3 * S + PAD), sb("wo_s", 3 * S + PAD), sb("bu_s", S)
        pk_s = sb("pk_s", 4 * 4 * NK)

        img_in = sb("img_in", XP * GB)
        pixT = sb("pixT", XP * P)
        pix = sb("pix", XP * P)
        ux = sb("ux", M1 * P)
        uxT = sb("uxT", M1 * P)
        vk = sb("vk", 3 * 2 * J)
        modes = sb("modes", J * 16)
        mixed = sb("mixed", 576)
        mixT = sb("mixT", M1 * P)
        zx = sb("zx", 16 * P)
        zxT = sb("zxT", 16 * P)
        mid = sb("mid", 2 * BANK)

        hT = sb("hT", GB * S)
        h1, h2, h2p = sb("h1", 2 * S), sb("h2", 2 * S), sb("h2p", 2 * S)
        zero = sb("zero", C)
        stat, mv, rs, xn = sb("stat", 12), sb("mv", 4), sb("rs", 10), sb("xn", 2 * S)
        xT, xT2, xT2p = sb("xT", GB * S), sb("xT2", GB * S), sb("xT2p", GB * S)
        NQ = HE * GB * S
        qT, kT = [pix[0:S, 0:NQ], pixT[0:S, 0:NQ]], [pix[0:S, NQ:2 * NQ], pixT[0:S, NQ:2 * NQ]]
        vv = mid
        red = sb("red", 96)
        qpk = pix
        sims, sims2, oneh = sb("sims", 4 * HE * NK), sb("sims2", 2 * HE * NK), sb("oneh", HE * K * K)
        sc_at = (0, 2 * BANK)
        pT, oT = [ux, sims2], [uxT, oneh]
        vi = sb("vi", 2 * 2 * HE * K)
        iu = sb("iu", 2 * HE * K, U32)
        cand = sb("cand", HE * NC)
        cand2 = sims2
        top, pos = sb("top", HE * K), sb("pos", HE * K, U32)
        den = sb("den", 2 * HE)
        steps, posf, code, whole, base, behind, place, found, row = [
            sims2[:, HE * NC + i * HE * K:HE * NC + (i + 1) * HE * K] for i in (0, 1, 2, 3, 0, 2, 1, 3, 2)]
        idx = sb("idx", 2 * HE * K, U32)
        wts = sb("wts", 2 * HE * K)
        ring = sb("ring", RING * K * P)
        w2q_s = ring
        kv = sb("kv", 2 * HE * P)
        kvp = sb("kvp", HE * P)
        kv_of = [kvp[:, :], kv[:, HE * P:2 * HE * P]]
        res = sb("res", 2 * S)

        ps = ctx.enter_context(nc.psum_tensor("ps", [P, 8, BANK], F32))

        cst_in, early = sem("constants_in"), sem("setup_weights_in")
        loaded, built, slots, gath = sem("loaded"), sem("built"), sem("slots_free"), [sem(f"gathered{i}") for i in range(RING)]
        memz = sem("zeroed")
        pe_turns, dve_turns, pool_turns = sem("pe_turns"), sem("dve_turns"), sem("pool_turns")
        qall_pe = sem("qall_pe")
        img_sem, img_done = sem("image_in"), sem("image_ready")
        fw_sem, staged = sem("fw_in"), sem("layer_weights")
        a_full, a_act = sem("ux_full"), sem("ux_act")
        t1_full, t1_act = sem("pix_full"), sem("pix_act")
        t2_full, t2_act = sem("uxT_full"), sem("uxT_act")
        v_full, v_act = sem("vk_full"), sem("vk_act")
        q_full = sem("mid_layer")
        c_full, c_done, c_seq = sem("modes_full"), sem("modes_done"), sem("modes_seq")
        m_full, m_act = sem("mixed_full"), sem("mixed_act")
        e_full, e_act, e_dve, e_seq = sem("mixT_full"), sem("mixT_act"), sem("mixT_dve"), sem("mixT_seq")
        f_full, f_act, f_dve = sem("zx_full"), sem("zx_act"), sem("zx_dve")
        t3_full, t3_act, t3_dve = sem("zxT_full"), sem("zxT_act"), sem("zxT_dve")
        r_full, rectified = sem("pixT_full"), sem("pixT_rectified")
        l1_full, l1_act, l1_dve = sem("last_full"), sem("last_act"), sem("last_dve")
        pe_step, act_step, dve_step = sem("pe_step"), sem("act_step"), sem("dve_step")
        att = [dict(pe=sem(f"att{i}_pe"), act=sem(f"att{i}_act"), dve=sem(f"att{i}_dve")) for i in range(2)]
        piece_seq, idx_ready = sem("piece_seq"), sem("idx_ready")
        att_seq = [sem("att0_seq"), sem("att1_seq")]
        dve_seq, rank_seq = sem("dve_seq"), sem("rank_seq")
        top_ready, exp_done, weighed, scaled = sem("top_ready"), sem("exp_done"), sem("weighed"), sem("rows_scaled")
        saved, kv_saved, out_ready, stored = sem("tokens_saved"), sem("kv_saved"), sem("out_ready"), sem("stored")
        cleared = sem("images_cleared")

        N_EARLY, N_LOADS = 6, 11

        def ux_tile(t):
            return (strided(ux, t * 32, [(2, 16), (P, M1), (1, 2)]),
                    strided(ps, (2 + t) * BANK, [(2 * M1, 16), (2, M1), (1, 2)]))

        def vk_tile(t):
            return (strided(vk, t * 6, [(1, 6), (J, 6), (M1, M1)]),
                    strided(ps, (2 + t) * BANK, [(FX, 6), (M1, 6), (1, M1)]))

        def mixed_tile(t):
            return (strided(mixed, t * 24, [(4, 6), (48, 12), (1, 4)]),
                    strided(ps, (6 + t) * BANK, [(48, 6), (4, 12), (1, 4)]))

        def mixT_tile(k):
            r = (0, 4 * M1)
            return (strided(mixT, k * BANK, [(P, 4), (C, GB), (1, C)], r),
                    strided(ps, (2 + k) * BANK, [(C, 4), (P, GB), (1, C)], r))

        def zx_tile(k):
            return (strided(zx, k * 8, [(2, 4), (32, S), (1, 2)]),
                    strided(ps, (5 + k) * BANK, [(P, 4), (2, S), (1, 2)]))

        def pixT_tile(t):
            return (strided(pixT, (t // 2 * 8 + t % 2) * P, [(2 * P, 4), (1, P)]),
                    strided(ps, (6, 7, 2, 3, 4, 5, 6, 7)[t] * BANK, [(P, 4), (1, P)]))

        def oT_tile(i, b2):
            return (strided(oT[i], b2 * S, [(P, 2), (2 * P, 4), (1, S)]),
                    strided(ps, (BANKS[i]["o"] + b2) * BANK, [(4 * S, 2), (S, 4), (1, S)]))

        block = ctx.enter_context(nc.Block())

        @block.sync
        def _(sp):
            loads = [(cst[:, :], const), (w2_all[:, :], w2s), (b2_all[0:2 * C, :], b2), (w2q_s[0:C + 1, 0:(2 * L + 1) * P], w2q),
                     (q1_s[0:C + 1, :], q1t), (q2_s[:, :], q2c), (b1_all[0:1, :], b1), (q2b_s[:, :], q2b),
                     (wq_s[0:S + 1, :], wq), (wk_s[0:S + 1, :], wk), (wv_s[0:S + 1, :], wv), (wpk_s[0:S + 1, :], wpk),
                     (wq2_s[0:S + 1, :], wq2), (wu_s[:, 0:4 * S], wu), (wo_s[:, 0:4 * S], wo), (bu_s[:, :], bu), (pk_s[:, :], pk),
                     (w1_all[:, :], w1s)]
            assert len(loads) == 1 + N_EARLY + N_LOADS
            sp.dma_start(img_in[:, :], x[0]).then_inc(img_sem, 16)
            for i, (dst, src) in enumerate(loads):
                sp.dma_start(dst, src).then_inc(cst_in if i == 0 else early if i <= N_EARLY else loaded, 16)
            def layer_weights(g):
                with sp.Fori(1, L) as l:
                    sp.wait_ge(m_full, (g * L + l) * 2)
                    sp.dma_start(fw_now[:, :], fw[bass.ds(l, 1)].rearrange("a p n -> (a p) n")).then_inc(fw_sem, 16)

            sp.dma_start(fw_now[:, :], fw[0]).then_inc(fw_sem, 16)
            with sp.Fori(1, G) as g:
                layer_weights(g - 1)
                sp.wait_ge(m_full, g * L * 2)
                sp.dma_start(fw_now[:, :], fw[0]).then_inc(fw_sem, 16)
                sp.wait_ge(img_done, g)
                sp.dma_start(img_in[:, :], x[bass.ds(g, 1)].rearrange("a p n -> (a p) n")).then_inc(img_sem, 16)
            layer_weights(G - 1)

        @block.tensor
        def _(pe):
            def mm(out_, lhsT, rhs, start=True, stop=True, **kw):
                return nc.tensor.matmul(out_, lhsT, rhs, start=start, stop=stop, **kw)

            def turned(out_, in_, rows=P):
                return nc.tensor.transpose(out_, in_, ident[0:rows, 0:rows])

            def pix_tile(c, bank, sem_):
                for i in range(4):
                    xp = 4 * c + i
                    last = turned(ps[:, bank, i * P:(i + 1) * P], pixT[:, xp * P:(xp + 1) * P])
                last.then_inc(sem_, 1)

            def mid_layer(weights, last):
                for c in range(8):
                    q = c % 4
                    ins = mm(ps[32 * q:32 * q + 32, c // 4, :], weights, pix[:, c * BANK:(c + 1) * BANK],
                             start=False, stop=last, skip_group_check=True)
                return ins

            def layer(n):
                for xp in range(XP):
                    t, i = divmod(xp, 8)
                    if i == 0:
                        pe.wait_ge(rectified, n * 8 + max(2 * t + 2, 3))
                    ins = mm(ps[:, 2 + t, i * FY:i * FY + PAD], pixT[:, xp * P:(xp + 1) * P], const_of("fy"))
                    if i == 7:
                        ins.then_inc(a_full, 1)
                pe.wait_ge(staged, n * 3 + 3)
                pix_tile(0, 6, t1_full)
                pix_tile(1, 7, t1_full)
                pe.wait_ge(a_act, n * 4 + 4)
                for ky in range(M1):
                    t, i = divmod(ky, 4)
                    ins = turned(ps[:, 2 + t, i * P:(i + 1) * P], ux[:, ky * P:(ky + 1) * P])
                    if i == 3:
                        ins.then_inc(t2_full, 1)
                pix_tile(2, 5, t1_full)
                pe.wait_ge(t1_act, n * 8 + 1)
                pix_tile(3, 6, t1_full)
                pe.wait_ge(t2_act, n * 3 + 3)
                for ky in range(M1):
                    t, i = divmod(ky, 6)
                    ins = mm(ps[:, 2 + t, i * FX:i * FX + PAD], uxT[:, ky * P:(ky + 1) * P], const_of("fx"))
                    if i == 5:
                        ins.then_inc(v_full, 1)
                pe.wait_ge(t1_act, n * 8 + 2)
                pix_tile(4, 7, t1_full)
                pix_tile(5, 4, t1_full)
                pe.wait_ge(t1_act, n * 8 + 4)
                pix_tile(6, 6, t1_full)
                pe.wait_ge(t1_act, n * 8 + 5)
                pix_tile(7, 7, t1_full)
                pe.wait_ge(v_act, n * 2 + 2)
                wait_apart(pe, t1_act, n * 8 + 6, pe_turns)
                for ro in range(2):
                    for half in range(2):
                        for ri in range(2):
                            comp = (0, 2, 1, 0)[2 * ro + ri]
                            slot = 2 * half + ri
                            for b in range(GB):
                                r = slice(32 * b, 32 * b + 32)
                                ins = mm(ps[32 * slot:32 * slot + 32, 2 + b, ro * J:(ro + 1) * J], w2_now[r, :],
                                         vk[r, (2 * comp + half) * J:(2 * comp + half + 1) * J], skip_group_check=True)
                ins.then_inc(c_full, 1)
                pe.wait_ge(t1_act, n * 8 + 8)
                mid_layer(q_now[:, :], False).then_inc(q_full, 1)
                pe.wait_ge(fw_sem, n * 16 + 16)
                for kx in range(M1):
                    if kx % 6 == 0:
                        pe.wait_ge(c_done, n * 2 + kx // 6 + 1)
                    for ky in range(M1):
                        j, q = kx * M1 + ky, ky % 4
                        at = ((kx % 6) * 3 + ky // 4) * 16
                        ins = mm(ps[32 * q:32 * q + 32, 6 + kx // 6, at:at + 16], fw_now[:, j * C:(j + 1) * C],
                                 modes[:, j * 16:(j + 1) * 16], skip_group_check=True)
                    if kx % 6 == 5:
                        ins.then_inc(m_full, 1)
                pe.wait_ge(m_act, n * 2 + 2)
                for kyi in range(3):
                    for b in range(GB):
                        ins = mm(ps[0:4 * M1, 2 + kyi, b * P:(b + 1) * P],
                                 mixed[:, (kyi * GB + b) * 48:(kyi * GB + b + 1) * 48], w1_now[:, :])
                    ins.then_inc(e_full, 1)
                pe.wait_ge(e_act, n + 1)
                pe.wait_ge(e_dve, n * 2 + 2)
                for ky in range(M1):
                    kyi, q = divmod(ky, 4)
                    ins = mm(ps[:, 5 + kyi, q * P:(q + 1) * P],
                             mixT[:, ky * P:(ky + 1) * P], const_of("iv"))
                    if q == 3:
                        ins.then_inc(f_full, 1)
                pe.wait_ge(f_act, n * 2 + 2)
                pe.wait_ge(f_dve, n + 1)
                for xq in range(16):
                    t, i = divmod(xq, 4)
                    ins = turned(ps[:, 2 + t, i * P:(i + 1) * P], zx[:, xq * P:(xq + 1) * P])
                    if i == 3:
                        ins.then_inc(t3_full, 1)
                pe.wait_ge(t3_act, n * 2 + 2)
                pe.wait_ge(t3_dve, n * 2 + 2)
                o = CONST_AT["g"][0]
                for t in range(8):
                    xqq, p = divmod(t, 2)
                    if t >= 6:
                        pe.wait_ge(rectified, n * 8 + 8 + t - 5)
                    mm(ps[:, (6, 7, 2, 3, 4, 5, 6, 7)[t], :], cst[:, o + p * P:o + (p + 1) * P],
                       zxT[:, xqq * BANK:(xqq + 1) * BANK]).then_inc(r_full, 1)

            def tokenizer(g):
                pe.wait_ge(img_done, g + 1)
                for c in range(8):
                    q = c % 4
                    mm(ps[32 * q:32 * q + 32, c // 4, 0:16], zero[:, 0:C], zero[:, 0:16], start=True, stop=False,
                       skip_group_check=True)
                with pe.Fori(0, L) as l:
                    layer(g * L + l)

            def queries(i, turn):
                X, W = ((xT, wq_s), (xT2p, wq2_s))[i]
                for t in range(4):
                    for h in (2 * t, 2 * t + 1):
                        ins = mm(ps[0:S, BANKS[i]["q"][t], (h % 2) * 256:(h % 2 + 1) * 256], W[0:S + 1, h * S:(h + 1) * S],
                                 X[0:S + 1, :])
                    ins.then_inc(att[i]["pe"], 1)

            def keys(i, turn):
                for t in range(4):
                    if t >= 2:
                        reached(pe, att[i]["act"], ATT_ACT[i], f"q{t - 2}", turn, pe_turns)
                    for h in (2 * t, 2 * t + 1):
                        bank, at = BANKS[i]["k"][t], (h % 2) * 256
                        if i == 0:
                            ins = mm(ps[0:S, bank, at:at + 256], wk_s[0:S + 1, h * S:(h + 1) * S], xT[0:S + 1, :])
                        else:
                            for tt in range(2):
                                ins = turned(ps[0:S, bank, at + tt * P:at + (tt + 1) * P],
                                             kv_of[tt][:, h * P:h * P + S])
                    ins.then_inc(att[i]["pe"], 1)

            def values(turn):
                for t in range(2):
                    reached(pe, att[0]["act"], ATT_ACT[0], f"q{2 + t}", turn)
                    mm(ps[:, BANKS[0]["v"][t], :], xT[0:S + 1, t * P:(t + 1) * P], wv_s[0:S + 1, :]).then_inc(att[0]["pe"], 1)

            def scores(i, turn):
                reached(pe, att[i]["act"], ATT_ACT[i], "q3", turn)
                reached(pe, att[i]["dve"], ATT_DVE[i], "k3", turn, pe_turns)
                for hp in range(4):
                    for b in range(GB):
                        for h2 in range(2):
                            c = (2 * hp + h2) * GB * S + b * S
                            ins = mm(ps[S * h2:S * h2 + S, BANKS[i]["scores"] + hp // 2,
                                        (hp % 2) * 256 + b * S:(hp % 2) * 256 + (b + 1) * S],
                                     qT[i][:, c:c + S], kT[i][:, c:c + S], skip_group_check=True)
                ins.then_inc(att[i]["pe"], 1)

            def turned_probs(i, turn):
                reached(pe, att[i]["dve"], ATT_DVE[i], "prob", turn)
                for k in range(8):
                    ins = turned(ps[:, BANKS[i]["pT"] + k // 4, (k % 4) * P:(k % 4 + 1) * P],
                                 zxT[:, sc_at[i] + k * P:sc_at[i] + (k + 1) * P])
                    if k % 4 == 3:
                        ins.then_inc(att[i]["pe"], 1)

            def weighted(i, turn):
                if i == 0:
                    reached(pe, att[i]["dve"], ATT_DVE[i], "pT", turn)
                reached(pe, att[i]["act"], ATT_ACT[i], "pT", turn, pe_turns)
                for hp in range(4):
                    for bp in range(2):
                        for h2 in range(2):
                            for b2 in range(2):
                                r = slice(S * b2, S * b2 + S)
                                h = 2 * hp + h2
                                v = vv[r, bp * 512 + h * S:bp * 512 + (h + 1) * S] if i == 0 else \
                                    kv_of[bp][r, h * P + S:(h + 1) * P]
                                ins = mm(ps[S * h2:S * h2 + S, BANKS[i]["o"] + b2, (bp * 4 + hp) * S:(bp * 4 + hp + 1) * S], v,
                                         pT[i][r, (hp * 2 + bp) * P + h2 * S:(hp * 2 + bp) * P + (h2 + 1) * S],
                                         skip_group_check=True)
                ins.then_inc(att[i]["pe"], 1)

            def result(i, turn):
                if i == 0:
                    reached(pe, att[i]["dve"], ATT_DVE[i], "oT", turn)
                reached(pe, att[i]["act"], ATT_ACT[i], "oT", turn)
                W = (wu_s, wo_s)[i]
                for bp in range(2):
                    for hp in range(4):
                        ins = mm(ps[:, BANKS[i]["y"], bp * P:bp * P + PAD], oT[i][:, (hp * 2 + bp) * P:(hp * 2 + bp + 1) * P],
                                 W[:, hp * S:hp * S + PAD], start=(hp == 0), stop=(hp == 3), skip_group_check=True)
                ins.then_inc(att[i]["pe"], 1)

            def stay_awake(bank, n):
                for _ in range(n):
                    mm(ps[:, bank, :], ident, cst[:, 0:BANK])

            def features_down(g, name):
                reached(pe, dve_step, DVE_STEPS, name, g, pe_turns)
                for t in range(2):
                    ins = turned(ps[0:S, 6, t * P:(t + 1) * P], xn[:, t * S:(t + 1) * S])
                ins.then_inc(pe_step, 1)

            def group(g, g_last):
                tokenizer(g)
                pe.wait_ge(rectified, g * 8 * L + 8 * L + 8)
                for c in range(8):
                    if c == 6:
                        pe.wait_ge(l1_act, g * 4 + 1)
                        pe.wait_ge(l1_dve, g * 4 + 1)
                    pix_tile(c, (2, 3, 4, 5, 6, 7, 2, 3)[c], l1_full)
                if g_last is not None:
                    pe.wait_ge(l1_act, g * 4 + 3)
                    pe.wait_ge(l1_dve, g * 4 + 3)
                    pe.wait_ge(saved, g_last + 1)
                    queries(1, g_last)
                pe.wait_ge(l1_act, g * 4 + 4)
                pe.wait_ge(l1_dve, g * 4 + 4)
                mid_layer(q_all[:, L * C:(L + 1) * C], True).then_inc(pe_step, 1)
                if g_last is not None:
                    pe.wait_ge(kv_saved, g_last + 1)
                    wait_apart(pe, slots, RING + (g_last + 1) * PIECES, pe_turns)
                    keys(1, g_last)
                if g_last is not None:
                    reached(pe, att[1]["act"], ATT_ACT[1], "q2", g_last)
                reached(pe, act_step, ACT_STEPS, "mid", g)
                for i in range(8):
                    ins = mm(ps[:, 6, i * 16:(i + 1) * 16], mid[:, i * P:(i + 1) * P], q2blk[:, :])
                ins.then_inc(pe_step, 1)
                if g_last is not None:
                    scores(1, g_last)
                reached(pe, dve_step, DVE_STEPS, "image", g, pe_turns)
                for t in range(2):
                    ins = turned(ps[:, 7, t * S:(t + 1) * S], hT[0:S, t * P:(t + 1) * P], S)
                ins.then_inc(pe_step, 1)
                stay_awake(2, 3)
                features_down(g, "xn1")
                reached(pe, act_step, ACT_STEPS, "x1", g)
                queries(0, g)
                keys(0, g)
                values(g)
                scores(0, g)
                if g_last is not None:
                    turned_probs(1, g_last)
                    weighted(1, g_last)
                else:
                    stay_awake(2, 7)
                turned_probs(0, g)
                weighted(0, g)
                result(0, g)
                if g_last is not None:
                    result(1, g_last)
                stay_awake(2, 2 if g_last is not None else 4)
                features_down(g, "xn2")
                reached(pe, act_step, ACT_STEPS, "x2", g)
                for c in range(4):
                    ins = mm(ps[:, 2 + c // 2, (c % 2) * 256:(c % 2 + 1) * 256], wpk_s[0:S + 1, c * P:(c + 1) * P], xT2[0:S + 1, :])
                ins.then_inc(pe_step, 1)
                if g_last is not None:
                    pe.wait_ge(out_ready, g_last + 1)
                reached(pe, act_step, ACT_STEPS, "qpk", g)
                for t in range(2):
                    for c in range(4):
                        ins = mm(ps[:, 4 + 2 * t + c // 2, (c % 2) * 256:(c % 2 + 1) * 256],
                                 qpk[:, c * 256 + t * P:c * 256 + (t + 1) * P], pk_s[:, c * 256:(c + 1) * 256])
                    ins.then_inc(pe_step, 1)
                reached(pe, act_step, ACT_STEPS, "sims0", g, pe_turns)

            pe.wait_ge(early, 16 * N_EARLY)
            for s in range(1, L + 1):
                mm(ps[:, 2, s * MID:(s + 1) * MID], w2q_s[0:C + 1, s * P:(s + 1) * P], q1_s[0:C + 1, :],
                   skip_group_check=True)
            for k, s in enumerate([0] + list(range(L + 1, 2 * L + 1))):
                ins = mm(ps[:, 2, 0:MID], w2q_s[0:C + 1, s * P:(s + 1) * P], q1_s[0:C + 1, :],
                         start=(k == 0), stop=(k == L), skip_group_check=True)
            ins.then_inc(qall_pe, 1)
            pe.wait_ge(built, 1)
            pe.wait_ge(loaded, 16 * N_LOADS)
            group(0, None)
            group(1, None)
            with pe.Fori(2, G) as g:
                group(g, g - 2)
            reached(pe, act_step, ACT_STEPS, "sims1", G - 1)
            for turn in (G - 2, G - 1):
                pe.wait_ge(saved, turn + 1)
                if turn == G - 1:
                    pe.wait_ge(out_ready, turn)
                queries(1, turn)
                pe.wait_ge(kv_saved, turn + 1)
                pe.wait_ge(slots, RING + (turn + 1) * PIECES)
                keys(1, turn)
                scores(1, turn)
                turned_probs(1, turn)
                weighted(1, turn)
                result(1, turn)

        @block.scalar
        def _(act):
            def copy(out_, in_, func=ACT.Copy, **kw):
                return nc.scalar.activation(out_, in_, func, **kw)

            def bank(b, n=BANK, rows=(0, P)):
                return ps[rows[0]:rows[1], b, 0:n]

            def layer(g, l, work):
                n = g * L + l
                copy(w2_now[:, :], w2_all[:, l * C:(l + 1) * C]).then_inc(staged, 1)
                copy(w1_now[:, :], w1_all[:, l * P:(l + 1) * P]).then_inc(staged, 1)
                copy(q_now[:, :], q_all[:, l * C:(l + 1) * C]).then_inc(staged, 1)

                def pix_tile(c):
                    act.wait_ge(t1_full, n * 8 + c + 1)
                    copy(pix[:, c * BANK:(c + 1) * BANK], bank((6, 7, 5, 6, 7, 4, 6, 7)[c])).then_inc(t1_act, 1)

                for t in range(4):
                    act.wait_ge(a_full, n * 4 + t + 1)
                    copy(*ux_tile(t)).then_inc(a_act, 1)
                pix_tile(0)
                for t in range(3):
                    act.wait_ge(t2_full, n * 3 + t + 1)
                    copy(uxT[:, t * BANK:(t + 1) * BANK], bank(2 + t)).then_inc(t2_act, 1)
                pix_tile(1)
                pix_tile(2)
                for t in range(2):
                    act.wait_ge(v_full, n * 2 + t + 1)
                    copy(*vk_tile(t)).then_inc(v_act, 1)
                for c in range(3, 8):
                    pix_tile(c)
                work()
                for t in range(2):
                    act.wait_ge(m_full, n * 2 + t + 1)
                    copy(*mixed_tile(t)).then_inc(m_act, 1)
                act.wait_ge(e_full, n * 3 + 2)
                copy(*mixT_tile(1)).then_inc(e_act, 1)
                for k in (0, 2):
                    act.wait_ge(f_full, n * 3 + k + 1)
                    copy(*zx_tile(k)).then_inc(f_act, 1)
                for t in (1, 3):
                    act.wait_ge(t3_full, n * 4 + t + 1)
                    copy(zxT[:, t * BANK:(t + 1) * BANK], bank(2 + t)).then_inc(t3_act, 1)
                for t in range(8):
                    act.wait_ge(r_full, n * 8 + t + 1)
                    copy(*pixT_tile(t), ACT.Relu).then_inc(rectified, 1)

            def weigh(turn, t):
                if turn is None:
                    return
                act.wait_ge(top_ready, turn * 2 + t + 1)
                nc.scalar.activation(top[:, :], top[:, :], ACT.Exp).then_inc(exp_done, 1)

            def clear_images():
                copy(pixT[:, :], strided(zero, 0, [(0, XP * P)]))
                copy(modes[:, :], strided(zero, 0, [(0, J * 16)])).then_inc(cleared, 1)

            def draw_grid(g):
                act.wait_ge(cleared, g + 1)
                for k in range(3):
                    copy(strided(pixT, k + 1, [(P, XP), (C, GB)]), strided(cst, CONST_AT["grid"][0] + k, [(3, XP), (0, GB)]))

            def tokenizer(g, g_rank, g_last):
                act.wait_ge(img_sem, 16 * g + 16)
                copy(strided(pixT, 0, [(C, XP * GB)]), img_in[:, :]).then_inc(img_done, 1)
                if g_last is None:
                    work = [lambda: weigh(g_rank, 0), lambda: weigh_rows(g_rank, [0, 1]),
                            lambda: (weigh(g_rank, 1), weigh_rows(g_rank, [3, 4])), lambda: weigh_rows(g_rank, [5])]
                else:
                    save_keys(g_last)
                    work = [lambda: weigh_rows(g_last, [11, 12]),
                            lambda: (weigh(g_rank, 0), weigh_rows(g_last, [14, 15])),
                            lambda: weigh_rows(g_rank, [0, 1]),
                            lambda: (weigh(g_rank, 1), weigh_rows(g_rank, [3, 4]))]
                for l in range(L):
                    layer(g, l, work[l])

            def weigh_rows(turn, ks):
                if turn is None:
                    return
                for k in ks:
                    slot = k % RING
                    act.wait_ge(weighed, turn * 2 + k // HE + 1)
                    act.wait_ge(gath[slot], (turn * (PIECES // RING) + k // RING + 1) * K * 16)
                    for m in range(K):
                        rows = ring[:, (slot * K + m) * P:(slot * K + m + 1) * P]
                        ins = nc.scalar.activation(rows, rows, ACT.Copy, scale=wts[:, k * K + m:k * K + m + 1])
                    ins.then_inc(scaled, 1)

            def deviation(g, i):
                reached(act, dve_step, DVE_STEPS, f"var{i}", g)
                nc.scalar.activation(rs[:, 0:2], rs[:, 2:4], ACT.Sqrt).then_inc(act_step, 1)
                reached(act, pe_step, PE_STEPS, f"x{i}", g)
                copy((xT, xT2)[i - 1][0:S, :], bank(6, 256, (0, S))).then_inc(act_step, 1)

            def save_keys(turn):
                act.wait_ge(slots, RING + turn * PIECES + HE)
                copy(kvp[:, :], kv[:, 0:HE * P]).then_inc(kv_saved, 1)

            def queries(i, turn, ts=range(4)):
                for t in ts:
                    reached(act, att[i]["pe"], ATT_PE[i], f"q{t}", turn)
                    copy(qT[i][:, t * BANK:(t + 1) * BANK], bank(BANKS[i]["q"][t], BANK, (0, S)),
                         scale=float(S) ** -0.5).then_inc(att[i]["act"], 1)

            def values(turn):
                for t in range(2):
                    reached(act, att[0]["pe"], ATT_PE[0], f"v{t}", turn)
                    copy(vv[:, t * BANK:(t + 1) * BANK], bank(BANKS[0]["v"][t])).then_inc(att[0]["act"], 1)

            def exp(i, turn):
                reached(act, att[i]["dve"], ATT_DVE[i], "shifted", turn)
                s = zxT[:, sc_at[i]:sc_at[i] + 2 * BANK]
                nc.scalar.activation(s, s, ACT.Exp).then_inc(att[i]["act"], 1)

            def turned_probs(i, turn):
                if i == 0:
                    reached(act, att[i]["pe"], ATT_PE[i], "pT0", turn)
                    copy(pT[i][:, 0:BANK], bank(BANKS[i]["pT"])).then_inc(att[i]["act"], 1)
                else:
                    reached(act, att[i]["pe"], ATT_PE[i], "pT1", turn)
                    copy(pT[i][:, 0:2 * BANK], ps[:, BANKS[i]["pT"]:BANKS[i]["pT"] + 2, :].rearrange("p a b -> p (a b)")
                         ).then_inc(att[i]["act"], 1)

            def weighted(i, turn):
                reached(act, att[i]["pe"], ATT_PE[i], "o", turn)
                if i == 1:
                    copy(*oT_tile(i, 1))
                copy(*oT_tile(i, 0)).then_inc(att[i]["act"], 1)

            def group(g, g_rank, g_last):
                tokenizer(g, g_rank, g_last)
                for c in (0, 2, 4, 6):
                    act.wait_ge(l1_full, g * 8 + c + 1)
                    copy(pix[:, c * BANK:(c + 1) * BANK], bank((2, 3, 4, 5, 6, 7, 2, 3)[c])).then_inc(l1_act, 1)
                if g_last is not None:
                    queries(1, g_last, range(3))
                reached(act, pe_step, PE_STEPS, "mid", g)
                copy(mid[:, :], ps[:, 0:2, :].rearrange("p a b -> p (a b)"), ACT.Relu).then_inc(act_step, 1)
                if g_last is not None:
                    queries(1, g_last, [3])
                weigh_rows(g_rank, [5] if g_last is not None else [7])
                deviation(g, 1)
                if g_last is not None:
                    exp(1, g_last)
                queries(0, g)
                values(g)
                if g_last is not None:
                    weigh_rows(g_rank, [7])
                    turned_probs(1, g_last)
                exp(0, g)
                if g_last is not None:
                    weighted(1, g_last)
                turned_probs(0, g)
                clear_images()
                weighted(0, g)
                draw_grid(g + 1)
                deviation(g, 2)
                reached(act, pe_step, PE_STEPS, "qpk", g)
                copy(qpk[:, 0:2 * BANK], ps[:, 2:4, :].rearrange("p a b -> p (a b)")).then_inc(act_step, 1)
                for t in range(2):
                    reached(act, pe_step, PE_STEPS, f"sims{t}", g)
                    copy(sims[:, t * 2 * BANK:(t + 1) * 2 * BANK],
                         ps[:, 4 + 2 * t:6 + 2 * t, :].rearrange("p a b -> p (a b)")).then_inc(act_step, 1)
                if g_last is not None:
                    store(g_last)

            def store(turn):
                act.wait_ge(out_ready, turn + 1)
                act.dma_start(out[bass.ds(turn, 1)].rearrange("a t p n -> p (a t) n"),
                              res[:, :].rearrange("p (t n) -> p t n", t=2)).then_inc(stored, 16)

            act.wait_ge(memz, 1)
            clear_images()
            act.wait_ge(cst_in, 16)
            draw_grid(0)
            act.wait_ge(built, 1)
            act.wait_ge(loaded, 16 * N_LOADS)
            group(0, None, None)
            group(1, 0, None)
            with act.Fori(2, G) as g:
                group(g, g - 1, g - 2)
            weigh(G - 1, 0)
            save_keys(G - 2)
            weigh_rows(G - 2, [11, 12, 14, 15])
            weigh(G - 1, 1)
            weigh_rows(G - 1, [0, 1, 3])
            for turn in (G - 2, G - 1):
                queries(1, turn)
                exp(1, turn)
                turned_probs(1, turn)
                weighted(1, turn)
                store(turn)
                if turn == G - 2:
                    weigh_rows(G - 1, [4, 5, 7])
                    save_keys(G - 1)
                    weigh_rows(G - 1, [11, 12, 14, 15])
            act.wait_ge(stored, 16 * G + 16)

        @block.vector
        def _(dve):
            v = nc.vector

            def bank(b, n=BANK, rows=(0, P)):
                return ps[rows[0]:rows[1], b, 0:n]

            def piece(k, turn):
                slot = k % RING
                if k in BY_ACT:
                    dve.wait_ge(scaled, turn * len(BY_ACT) + BY_ACT.index(k) + 1)
                else:
                    mine = [i for i in range(PIECES) if i not in BY_ACT]
                    dve.wait_ge(gath[slot], (turn * (PIECES // RING) + k // RING + 1) * K * 16)
                    rows = strided(ring, slot * K * P, [(P, K), (1, P)])
                    v.tensor_tensor(rows, rows, strided(wts, k * K, [(1, K), (0, P)]), ALU.mult).then_inc(piece_seq, 1)
                    dve.wait_ge(piece_seq, turn * len(mine) + mine.index(k) + 1)
                v.tensor_reduce(kv[:, k * P:(k + 1) * P], strided(ring, slot * K * P, [(1, P), (P, K)]), AX.X,
                                ALU.add).then_inc(slots, 1)

            def layer(g, l, work):
                n = g * L + l
                v.tensor_tensor(modes[0:2 * C, 0:16], modes[0:2 * C, 0:16], b2_all[0:2 * C, l * 16:(l + 1) * 16],
                                ALU.add).then_inc(c_seq, 1)
                work(0)
                dve.wait_ge(c_seq, n + 1)
                dve.wait_ge(c_full, n + 1)
                for part in range(2):
                    for h in range(2):
                        r = (64 * h, 64 * h + 64)
                        m = strided(modes, part * J // 2 * 16 + 2 * h, [(4, GB), (1, 2), (16, J // 2)], r)
                        ins = v.tensor_tensor(m, m, strided(ps, 2 * BANK + part * J // 2, [(BANK, GB), (J, 2), (1, J // 2)], r),
                                              ALU.add)
                    ins.then_inc(c_done, 1)
                work(1)
                dve.wait_ge(e_full, n * 3 + 1)
                v.tensor_copy(*mixT_tile(0)).then_inc(e_seq, 1)
                dve.wait_ge(e_seq, n + 1)
                m = strided(mixT, 0, [(C, GB), (1, C)], (0, 1))
                v.tensor_tensor(m, m, strided(b1_all, l * C, [(0, GB), (1, C)], (0, 1)), ALU.add).then_inc(e_dve, 1)
                dve.wait_ge(e_full, n * 3 + 3)
                v.tensor_copy(*mixT_tile(2)).then_inc(e_dve, 1)
                dve.wait_ge(f_full, n * 3 + 2)
                v.tensor_copy(*zx_tile(1)).then_inc(f_dve, 1)
                for t in (0, 2):
                    dve.wait_ge(t3_full, n * 4 + t + 1)
                    v.tensor_copy(zxT[:, t * BANK:(t + 1) * BANK], bank(2 + t)).then_inc(t3_dve, 1)

            def normalise(h, i, g, seq):
                for t in range(2):
                    seq.add(v.bn_stats(stat[:, 6 * t:6 * t + 6], h[:, t * S:(t + 1) * S]))
                seq.so_far_apart(dve, dve_turns)
                for t in range(2):
                    seq.add(v.bn_aggr(mv[:, 2 * t:2 * t + 2], stat[:, 6 * t:6 * t + 6]))
                seq.so_far(dve)
                var, sd, r, u = rs[:, 2:4], rs[:, 0:2], rs[:, 4:6], rs[:, 6:8]
                v.tensor_scalar(var, strided(mv, 1, [(2, 2)]), EPS, None, ALU.add).then_inc(dve_step, 1)
                reached(dve, act_step, ACT_STEPS, f"sd{i}", g)
                seq.add(v.reciprocal(r, sd))
                seq.so_far(dve)
                seq.add(v.tensor_tensor(u, r, r, ALU.mult))
                seq.so_far(dve)
                seq.add(v.tensor_tensor(u, u, var, ALU.mult))
                seq.so_far(dve)
                seq.add(v.tensor_scalar(u, u, -0.5, 1.5, ALU.mult, ALU.add))
                seq.so_far(dve)
                seq.add(v.tensor_tensor(r, r, u, ALU.mult))
                seq.so_far(dve)
                for t in range(2):
                    ins = v.tensor_scalar(xn[:, t * S:(t + 1) * S], h[:, t * S:(t + 1) * S], mv[:, 2 * t:2 * t + 1],
                                          rs[:, 4 + t:5 + t], ALU.subtract, ALU.mult)
                ins.then_inc(dve_step, 1)

            def keys(i, turn, ts=range(4)):
                for t in ts:
                    reached(dve, att[i]["pe"], ATT_PE[i], f"k{t}", turn)
                    v.tensor_copy(kT[i][:, t * BANK:(t + 1) * BANK], bank(BANKS[i]["k"][t], BANK, (0, S))
                                  ).then_inc(att[i]["dve"], 1)

            def masked(i, turn, seq):
                reached(dve, att[i]["pe"], ATT_PE[i], "scores", turn)
                rows = strided(zxT, sc_at[i], [(S, 16), (1, S)])
                o = CONST_AT[("strict", "causal")[i]][0]
                seq.add(v.tensor_tensor(rows, strided(ps, BANKS[i]["scores"] * BANK, [(S, 16), (1, S)]),
                                        strided(cst, o, [(0, 16), (1, S)]), ALU.add))
                seq.so_far(dve)
                seq.add(v.tensor_reduce(red[:, 48 * i:48 * i + 16], rows, AX.X, ALU.max))
                seq.so_far(dve)
                v.tensor_tensor(rows, rows, strided(red, 48 * i, [(1, 16), (0, S)]), ALU.subtract).then_inc(att[i]["dve"], 1)

            def result(i):
                return strided(ps, BANKS[i]["y"] * BANK, [(P, 2), (1, S)])

            def probabilities(i, turn, seq):
                rows = strided(zxT, sc_at[i], [(S, 16), (1, S)])
                total, inverse = red[:, 48 * i + 16:48 * i + 32], red[:, 48 * i + 32:48 * i + 48]
                reached(dve, att[i]["act"], ATT_ACT[i], "exp", turn)
                seq.add(v.tensor_reduce(total, rows, AX.X, ALU.add))
                seq.so_far(dve)
                seq.add(v.reciprocal(inverse, total))
                seq.so_far(dve)
                if i == 0:
                    seq.add(v.tensor_scalar(inverse, inverse, const_of("rows")[:, 0:1], None, ALU.mult))
                    seq.so_far(dve)
                v.tensor_tensor(rows, rows, strided(red, 48 * i + 32, [(1, 16), (0, S)]), ALU.mult).then_inc(att[i]["dve"], 1)

            def rank(t, g, seq):
                ranks = [strided(vi, (r // HE * 2 * HE + r % HE) * K, [(1, K)]) for r in range(2 * HE)]
                sim = [sims[:, (t * 2 * HE + r) * NK:(t * 2 * HE + r + 1) * NK] for r in range(2 * HE)]
                reached(dve, act_step, ACT_STEPS, f"sims{t}", g, dve_turns)
                for r in range(2 * HE):
                    ins = v.max(ranks[r][:, 0:8], sim[r])
                seq.add(ins)
                seq.so_far_apart(dve, dve_turns)
                for r in range(2 * HE):
                    ins = v.match_replace(sims2[:, r * NK:(r + 1) * NK], ranks[r][:, 0:8], sim[r], LOWEST)
                seq.add(ins)
                yield
                for r in range(2 * HE):
                    v.max_index(iu[:, r * K:r * K + 8], ranks[r][:, 0:8], sim[r])
                yield
                seq.so_far_apart(dve, dve_turns)
                for r in range(2 * HE):
                    ins = v.max(ranks[r][:, 8:16], sims2[:, r * NK:(r + 1) * NK])
                seq.add(ins)
                seq.so_far_apart(dve, dve_turns)
                for r in range(2 * HE):
                    ins = v.max_index(iu[:, r * K + 8:r * K + 16], ranks[r][:, 8:16], sims2[:, r * NK:(r + 1) * NK])
                seq.add(ins)
                seq.so_far_apart(dve, dve_turns)
                lo, hi = HE * K, 3 * HE * K
                seq.add(v.tensor_scalar(vi[:, lo:lo + HE * K], iu[:, 0:HE * K], float(CODE), None, ALU.mult))
                seq.add(v.tensor_scalar(vi[:, hi:hi + HE * K], iu[:, HE * K:2 * HE * K], float(NK), None, ALU.mult))
                yield
                at, a = 0, 0
                while a < K:
                    n = PAIRS[a][1]
                    m = sum(1 for _, c in PAIRS if c == n)
                    ins = v.tensor_tensor(strided(cand, at, [(NC, HE), (n, m), (1, n)]),
                                          strided(vi, a, [(K, HE), (1, m), (0, n)]),
                                          strided(vi, 2 * HE * K, [(K, HE), (0, m), (1, n)]), ALU.add)
                    at, a = at + n * m, a + m
                seq.add(ins)
                seq.so_far(dve)
                codes = vi[:, lo:lo + HE * K]
                seq.add(v.tensor_tensor(codes, codes, const_of("code"), ALU.add))
                seq.so_far(dve)
                by_head = [(K, HE), (1, K - 1)]
                v.tensor_tensor(strided(sims2, HE * NC + 1, by_head), strided(vi, lo + 1, by_head),
                                strided(vi, lo, by_head), ALU.subtract)
                seq.add(v.tensor_copy(strided(sims2, HE * NC, [(K, HE)]), strided(vi, lo, [(K, HE)])))
                seq.so_far_apart(dve, dve_turns)
                score = [cand[:, h * NC:(h + 1) * NC] for h in range(HE)]
                rest = [cand2[:, h * NC:(h + 1) * NC] for h in range(HE)]
                for h in range(HE):
                    ins = v.max(top[:, h * K:h * K + 8], score[h])
                seq.add(ins)
                yield
                seq.so_far_apart(dve, dve_turns)
                for h in range(HE):
                    ins = v.match_replace(rest[h], top[:, h * K:h * K + 8], score[h], LOWEST)
                seq.add(ins)
                for h in range(HE):
                    v.max_index(pos[:, h * K:h * K + 8], top[:, h * K:h * K + 8], score[h])
                yield
                seq.so_far_apart(dve, dve_turns)
                for h in range(HE):
                    ins = v.max(top[:, h * K + 8:h * K + 16], rest[h])
                seq.add(ins)
                seq.so_far_apart(dve, dve_turns)
                for h in range(HE):
                    ins = v.max_index(pos[:, h * K + 8:h * K + 16], top[:, h * K + 8:h * K + 16], rest[h])
                seq.add(ins)
                seq.add(v.tensor_copy(den[:, 0:HE], strided(top, 0, [(K, HE)])))
                seq.so_far(dve)
                v.tensor_tensor(strided(top, 0, [(K, HE), (1, K)]), strided(top, 0, [(K, HE), (1, K)]),
                                strided(den, 0, [(1, HE), (0, K)]), ALU.subtract).then_inc(top_ready, 1)
                seq.add(v.tensor_copy(posf, pos[:, :]))
                yield
                hot = oneh[:, :].rearrange("p (m c) -> p m c", c=K)
                hot3 = strided(oneh, 0, [(K * K, HE), (K, K), (1, K)])
                per_pair = lambda i: strided(sims2, HE * NC + i * HE * K, [(1, HE * K), (0, K)])
                seq.so_far(dve)
                seq.add(v.tensor_tensor(hot, per_pair(1), strided(cst, CONST_AT["first"][0], [(0, HE * K), (1, K)]), ALU.is_ge))
                seq.so_far(dve)
                seq.add(v.tensor_tensor(hot3, hot3, strided(sims2, HE * NC, [(K, HE), (0, K), (1, K)]), ALU.mult))
                seq.so_far(dve)
                yield
                seq.add(v.tensor_reduce(code, hot, AX.X, ALU.add))
                seq.so_far(dve)
                seq.add(v.tensor_scalar(whole, code, 1.0 / CODE, ROUND - 0.5, ALU.mult, ALU.add))
                seq.add(v.tensor_tensor(posf, posf, code, ALU.subtract))
                seq.so_far(dve)
                seq.add(v.tensor_scalar(base, whole, -ROUND - 1.0, None, ALU.add))
                seq.add(v.tensor_scalar(behind, whole, -ROUND, float(CODE), ALU.add, ALU.mult))
                seq.so_far(dve)
                seq.add(v.tensor_tensor(place, posf, behind, ALU.add))
                seq.so_far(dve)
                yield
                seq.add(v.tensor_tensor(hot, per_pair(1), strided(cst, CONST_AT["iota"][0], [(0, HE * K), (1, K)]), ALU.is_equal))
                seq.so_far(dve)
                seq.add(v.tensor_tensor(hot3, hot3, strided(vi, hi, [(K, HE), (0, K), (1, K)]), ALU.mult))
                seq.so_far(dve)
                yield
                seq.add(v.tensor_reduce(found, hot, AX.X, ALU.add))
                seq.so_far(dve)
                seq.add(v.tensor_tensor(row, found, base, ALU.add))
                seq.so_far(dve)
                v.tensor_copy(idx[:, t * HE * K:(t + 1) * HE * K], row).then_inc(idx_ready, 1)
                yield
                dve.wait_ge(exp_done, g * 2 + t + 1)
                w = strided(top, 0, [(K, HE), (1, K)])
                seq.add(v.tensor_reduce(den[:, 0:HE], w, AX.X, ALU.add))
                seq.so_far(dve)
                seq.add(v.reciprocal(den[:, HE:2 * HE], den[:, 0:HE]))
                seq.so_far(dve)
                v.tensor_tensor(wts[:, t * HE * K:(t + 1) * HE * K].rearrange("p (h k) -> p h k", k=K), w,
                                strided(den, HE, [(1, HE), (0, K)]), ALU.mult).then_inc(weighed, 1)
                dve.wait_ge(weighed, g * 2 + t + 1)

            def group(g, g_rank, g_last):
                seq = Steps(dve_seq, DVE_SEQ, g)
                rseq = Steps(rank_seq, RANK_SEQ, g_rank)
                seq0, seq1 = Steps(att_seq[0], 5, g), Steps(att_seq[1], LAST_SEQ, g_last)
                ranking = [rank(t, g_rank, rseq) if g_rank is not None else None for t in range(2)]

                def ranks(t, count):
                    for _ in range(count):
                        if ranking[t]:
                            next(ranking[t], None)

                def pieces(turn, ks):
                    if turn is not None:
                        for k in ks:
                            if k == 0 and g_last is not None:
                                dve.wait_ge(kv_saved, g_last + 1)
                            piece(k, turn)

                if g_last is None:
                    plan = [(lambda: ranks(0, 12), lambda: ranks(1, 2)),
                            (lambda: ranks(1, 4), lambda: pieces(g_rank, [0, 1])),
                            (lambda: ranks(1, 4), lambda: (ranks(1, 4), pieces(g_rank, [2, 3, 4]))),
                            (lambda: None, lambda: pieces(g_rank, [5, 6]))]
                    later = [[7], [8], [9], [10]]
                else:
                    plan = [(lambda: ranks(0, 5), lambda: (ranks(0, 1), pieces(g_last, [11, 12]))),
                            (lambda: (ranks(0, 4), pieces(g_last, [13])), lambda: (ranks(0, 1), pieces(g_last, [14, 15]))),
                            (lambda: ranks(1, 5), lambda: (ranks(1, 1), pieces(g_rank, [0, 1]))),
                            (lambda: (ranks(1, 4), pieces(g_rank, [2])), lambda: (ranks(1, 1), pieces(g_rank, [3, 4])))]
                    later = [[5], [6], [7], [8, 9, 10]]
                dve.wait_ge(img_done, g + 1)
                for l in range(L):
                    layer(g, l, lambda i: plan[l][i]())
                if g_rank is not None:
                    rseq.close()
                for c in (1, 3, 5, 7):
                    dve.wait_ge(l1_full, g * 8 + c + 1)
                    v.tensor_copy(pix[:, c * BANK:(c + 1) * BANK], bank((2, 3, 4, 5, 6, 7, 2, 3)[c])).then_inc(l1_dve, 1)
                if g_last is not None:
                    keys(1, g_last)
                reached(dve, pe_step, PE_STEPS, "image", g)
                for x2 in range(2):
                    for ci in range(2):
                        r = (x2 * S, x2 * S + S)
                        ins = v.tensor_scalar(strided(hT, 32 * ci + x2, [(2, 4), (8, 4), (S, GB)], (0, S)),
                                              strided(ps, 6 * BANK + ci * S, [(16, 4), (4, 4), (1, GB)], r),
                                              q2b_s[r[0]:r[1], 0:1], None, ALU.add)
                ins.then_inc(dve_step, 1)
                turn_over(g_rank, g_last, seq1)
                reached(dve, pe_step, PE_STEPS, "h1", g)
                v.tensor_copy(h1[:, :], bank(7, 2 * S)).then_inc(dve_step, 1)
                reached(dve, dve_step, DVE_STEPS, "h1", g)
                normalise(h1, 1, g, seq)
                pieces(g_rank, later[0])
                if g_last is not None:
                    masked(1, g_last, seq1)
                keys(0, g, range(2))
                if g_last is not None:
                    probabilities(1, g_last, seq1)
                keys(0, g, range(2, 4))
                pieces(g_rank, later[1])
                masked(0, g, seq0)
                probabilities(0, g, seq0)
                reached(dve, att[0]["pe"], ATT_PE[0], "pT1", g)
                v.tensor_copy(pT[0][:, BANK:2 * BANK], bank(BANKS[0]["pT"] + 1)).then_inc(att[0]["dve"], 1)
                pieces(g_rank, later[2])
                reached(dve, att[0]["pe"], ATT_PE[0], "o", g)
                v.tensor_copy(*oT_tile(0, 1)).then_inc(att[0]["dve"], 1)
                reached(dve, att[0]["pe"], ATT_PE[0], "y", g)
                h3 = h2[:, :].rearrange("p (t s) -> p t s", t=2)
                seq.add(v.tensor_tensor(h3, h1[:, :].rearrange("p (t s) -> p t s", t=2), result(0), ALU.add))
                seq.so_far(dve)
                v.tensor_tensor(h3, h3, strided(bu_s, 0, [(0, 2), (1, S)]), ALU.add).then_inc(dve_step, 1)
                reached(dve, dve_step, DVE_STEPS, "h2", g)
                normalise(h2, 2, g, seq)
                if g_last is not None:
                    finish(g_last, seq1)
                pieces(g_rank, later[3])
                seq.close()

            def turn_over(g_rank, g_last, seq):
                if g_last is not None:
                    dve.wait_ge(stored, 16 * g_last + 16)
                    seq.add(v.tensor_copy(res[:, :], h2p[:, :]))
                    seq.so_far(dve)
                if g_rank is not None:
                    reached(dve, dve_step, DVE_STEPS, "h2", g_rank)
                    v.tensor_copy(h2p[:, :], h2[:, :])
                    if g_last is not None:
                        reached(dve, att[1]["pe"], ATT_PE[1], "q3", g_last)
                    v.tensor_copy(xT2p[0:S + 1, :], xT2[0:S + 1, :]).then_inc(saved, 1)

            def finish(turn, seq):
                reached(dve, att[1]["pe"], ATT_PE[1], "y", turn)
                r = res[:, :].rearrange("p (t s) -> p t s", t=2)
                v.tensor_tensor(r, r, result(1), ALU.add).then_inc(out_ready, 1)
                seq.close()

            v.memset(zero[:, :], 0.0).then_inc(memz, 1)
            for z in (q_all, zx, mixT):
                v.memset(z[:, :], 0.0)
            for z in (wu_s, wo_s):
                v.memset(z[:, 4 * S:3 * S + PAD], 0.0)
            for o in (xT, xT2):
                ins = v.memset(o[S:S + 1, :], 1.0)
            ins.then_inc(memz, 1)
            dve.wait_ge(memz, 2)
            v.memset(res[:, :], 0.0).then_inc(stored, 16)
            v.memset(red[:, :], 0.0).then_inc(slots, RING)
            v.memset(top[:, :], 0.0).then_inc(rectified, 8)
            dve.wait_ge(cst_in, 16)
            dve.wait_ge(early, 16 * N_EARLY)
            v.tensor_scalar(b1_all[0:1, :], b1_all[0:1, :], float(S), None, ALU.mult)
            v.tensor_scalar(b2_all[0:2 * C, :], b2_all[0:2 * C, :], float(S), None, ALU.mult)
            v.tensor_scalar(q2blk[:, :], const_of("q2m"), q2_s[:, 0:1], None, ALU.mult)
            dve.wait_ge(qall_pe, 1)
            for s in range(L + 1):
                ins = v.tensor_tensor(strided(q_all, s * C, [(MID, GB), (1, MID)]), strided(ps, 2 * BANK + s * MID, [(0, GB), (1, MID)]),
                                      const_of("img").rearrange("p (b m) -> p b m", m=MID), ALU.mult)
            ins.then_inc(built, 1)
            dve.wait_ge(loaded, 16 * N_LOADS)

            group(0, None, None)
            group(1, 0, None)
            with dve.Fori(2, G) as g:
                group(g, g - 1, g - 2)
            rseq = Steps(rank_seq, RANK_SEQ, G - 1)
            for _ in rank(0, G - 1, rseq):
                pass
            for k in range(11, PIECES):
                piece(k, G - 2)
            for _ in rank(1, G - 1, rseq):
                pass
            rseq.close()
            dve.wait_ge(kv_saved, G - 1)
            for k in range(4):
                piece(k, G - 1)
            for turn in (G - 2, G - 1):
                seq1 = Steps(att_seq[1], LAST_SEQ, turn)
                if turn == G - 1:
                    for k in range(4, PIECES):
                        piece(k, turn)
                keys(1, turn)
                turn_over(turn + 1 if turn < G - 1 else None, turn, seq1)
                masked(1, turn, seq1)
                probabilities(1, turn, seq1)
                finish(turn, seq1)

        @block.gpsimd
        def _(pool):
            with pool.Fori(0, G) as g:
                for k in range(PIECES):
                    if k % HE == 0:
                        pool.wait_ge(idx_ready, g * 2 + k // HE + 1)
                    wait_apart(pool, slots, g * PIECES + k + 1, pool_turns)
                    for m in range(K):
                        o = (k % RING * K + m) * P
                        pool.indirect_dma_start(out=ring[:, o:o + P], out_offset=None, in_=table,
                                                in_offset=bass.IndirectOffsetOnAxis(ap=idx[:, k * K + m:k * K + m + 1], axis=0)
                                                ).then_inc(gath[k % RING], 16)


def kernel(**inputs):
    import numpy as _np
    import concourse.bacc as _bacc
    from concourse import mybir as _mybir
    from concourse.bass_utils import run_bass_kernel_spmd as _run

    a = {k.replace("L0_", ""): _np.asarray(v) for k, v in inputs.items()}
    f = _np.float32
    z = lambda *s: _np.zeros(s, f)
    laid = {}
    laid["x"] = a["x"].reshape(G, GB, XP, 2, S).transpose(0, 3, 4, 2, 1).reshape(G, P, XP * GB)
    laid["const"] = CONST
    w2s = z(C, L, C)
    w2s[0:3, 0], w2s[3, 0] = a["tok_p_w"].T, a["tok_p_b"]
    w2s[:, 1:] = a["tok_w2_w"][:L - 1].transpose(2, 0, 1)
    laid["w2s"] = _np.tile(w2s.reshape(C, L * C), (4, 1))
    w1s = z(4, C, L, 4, C)
    for q in range(4):
        w1s[q, :, :, q] = a["tok_w1_w"].transpose(2, 0, 1)
    laid["w1s"] = w1s.reshape(P, L * P)
    laid["fw"] = a["tok_fw"].transpose(0, 1, 6, 2, 4, 5, 3).reshape(L, P, J * C)
    laid["b1"] = a["tok_w1_b"].reshape(1, L * C)
    b2 = z(2, C, L, GB, 2, 2)
    b2[0, :, 1:, :, 0, 0] = a["tok_w2_b"][:L - 1].T[:, :, None]
    b2[1, :, 1:, :, 0, 1] = a["tok_w2_b"][:L - 1].T[:, :, None]
    laid["b2"] = b2.reshape(2 * C, L * 16)
    w2q = z(C + 1, 2 * L + 1, GB, C)
    w2q[:C, 0, :, 0:3] = a["tok_p_w"][:, None]
    w2q[:C, 0, :, 3] = a["tok_p_b"][:, None]
    w2q[C, 0, :, 3] = 1.0
    w2q[:C, 1:L + 1] = a["tok_w2_w"].transpose(1, 0, 2)[:, :, None]
    w2q[:C, L + 1:, :, 3] = a["tok_w2_b"].T[:, :, None]
    laid["w2q"] = w2q.reshape(C + 1, (2 * L + 1) * P)
    laid["q1t"] = _np.concatenate([a["tok_q1_w"].T, a["tok_q1_b"][None]])
    q2 = z(4, 32)
    q2[:, :GB * MID] = _np.tile(a["tok_q2_w"].reshape(1, MID), (4, GB))
    laid["q2c"] = q2.reshape(P, 1)
    laid["q2b"] = _np.tile(a["tok_q2_b"].reshape(1, 1), (P, 1))
    for n, w, b in (("wq", "attn_Wq", "attn_bq"), ("wk", "attn_Wk", "attn_bk"), ("wv", "attn_Wv", "attn_bv")):
        laid[n] = _np.concatenate([a[w], a[b][None]])
    laid["wu"] = a["attn_Wu"].reshape(4, P, S).transpose(1, 0, 2).reshape(P, 4 * S)
    laid["bu"] = _np.tile(a["attn_bu"][None], (P, 1))
    laid["wpk"] = _np.concatenate([a["ffn_Wq_pk"], z(1, HE * S)])
    pk = z(4, 32, 2, 2, 4, NK)
    keys = a["ffn_pk_keys"].reshape(2, NK, 2, 4, 32)
    for h in range(4):
        pk[h, :, :, :, h] = keys[:, :, :, h].transpose(3, 0, 2, 1)
    laid["pk"] = pk.reshape(P, 4 * 4 * NK)
    laid["wq2"] = _np.concatenate([a["ffn_Wq"], z(1, HE * S)])
    laid["wo"] = a["ffn_Wo"].reshape(4, P, S).transpose(1, 0, 2).reshape(P, 4 * S)
    laid["table"] = _np.concatenate([a["ffn_keys_table"], a["ffn_values_table"]], 1)

    nc = _bacc.Bacc("TRN2", target_bir_lowering=False, num_devices=1)
    arrays, args = {}, {}
    for name, v in laid.items():
        v = _np.ascontiguousarray(v)
        arrays[f"in_{name}"] = v
        args[name] = nc.dram_tensor(f"in_{name}", v.shape, _mybir.dt.from_np(v.dtype), kind="ExternalInput").ap()
    args["out"] = nc.dram_tensor("out_h", (G, 2, P, S), F32, kind="ExternalOutput").ap()
    build(nc, **args)
    r = _run(nc, [arrays], core_ids=[0])
    return r.results[0]["out_h"].reshape(B, S, S)
```

```python
from contextlib import ExitStack

import numpy as np

import concourse.bass as bass
from concourse import mybir

ALU = mybir.AluOpType
ACT = mybir.ActivationFunctionType
AX = mybir.AxisListType
F32 = mybir.dt.float32
U32 = mybir.dt.uint32

P = 128
B, S = 32, 64
C = 32
L = 4
M1 = 12
GB = 4
G = B // GB
HE = 8
K = 16
NK = 64
NKV = NK * NK
MID = 4
J = M1 * M1
XP = S // 2
BANK = 512
PAIRS = [(a, K // (a + 1)) for a in range(K)]
NC = sum(n for _, n in PAIRS)
RING = 4
PIECES = 2 * HE
FY, FX = 2 * 2 * M1, 3 * 2 * M1
PAD = 96
CODE = 64
CODE_AT = 7
ROUND = 2.0 ** 23
BIG = 1e30
LOWEST = -3e38
EPS = 1e-5


def shape_constants():
    one = np.zeros
    w = 2 * np.pi / S
    kx = np.concatenate([np.arange(M1), np.arange(S - M1, S)])
    y, ky = np.arange(S), np.arange(M1)
    fy = one((2, S, 2, M1, 2))
    for i in range(2):
        fy[i, :, i, :, 0] = np.cos(w * np.outer(y, ky)) / 8
        fy[i, :, i, :, 1] = -np.sin(w * np.outer(y, ky)) / 8
    fyp = one((P, PAD))
    fyp[:, :FY] = fy.reshape(P, FY)
    co, si = np.cos(w * np.outer(y, kx)) / 8, np.sin(w * np.outer(y, kx)) / 8
    fx = one((S, 2, 3, 2 * M1))
    fx[:, 0, 0], fx[:, 1, 0] = co, si
    fx[:, 0, 1], fx[:, 1, 1] = -si, co
    fx[:, 0, 2], fx[:, 1, 2] = si, -co
    fxp = one((P, PAD))
    fxp[:, :FX] = fx.reshape(P, FX)
    iv = one((M1, 2, 2, S, 2))
    for h in range(2):
        c, s = co[:, h * M1:(h + 1) * M1].T, si[:, h * M1:(h + 1) * M1].T
        iv[:, h, 0, :, 0], iv[:, h, 0, :, 1] = c, s
        iv[:, h, 1, :, 0], iv[:, h, 1, :, 1] = -s, c
    ivp = one((P, P))
    ivp[:4 * M1] = iv.reshape(4 * M1, P)
    g = one((4, 32, 2, 2, S))
    amp = np.where(ky == 0, 1.0, 2.0)[:, None] / 8
    for p in range(2):
        for i in range(2):
            g[2 * p + i, 0:2 * M1:2, p, i] = amp * np.cos(w * np.outer(ky, y))
            g[2 * p + i, 1:2 * M1:2, p, i] = -amp * np.sin(w * np.outer(ky, y))
    lin = np.linspace(0.0, 1.0, S, dtype=np.float32)
    grid = one((2, S, XP, 3))
    grid[..., 0] = lin.reshape(XP, 2).T[:, None, :]
    grid[..., 1] = lin[None, :, None]
    grid[..., 2] = 1.0
    i, j = np.arange(S)[:, None], np.arange(S)[None, :]
    strict = np.tile(np.where(j >= i, -BIG, 0.0), (2, 1))
    causal = np.tile(np.where(j > i, -BIG, 0.0), (2, 1))
    rows = np.tile((np.arange(S) > 0) * 1.0, 2)[:, None]
    img = np.kron(np.eye(GB), np.ones((C, MID)))
    q2m = np.kron(np.eye(4), np.vstack([np.kron(np.eye(GB), np.ones((MID, 1))), one((16, GB))]))
    first = np.cumsum([0] + [n for _, n in PAIRS])[:K]
    code = np.tile(((np.arange(HE)[:, None] * float(NKV) + 1) * CODE + first[None] + CODE_AT).reshape(1, HE * K), (P, 1))
    first = np.tile(first * 1.0, (P, 1))
    iota = np.tile(np.arange(K) - float(CODE_AT), (P, 1))
    parts = dict(fy=fyp, fx=fxp, iv=ivp, g=g.reshape(P, 2 * P), ident=np.eye(P), grid=grid.reshape(P, 3 * XP),
                 strict=strict, causal=causal, rows=rows, img=img, q2m=q2m, code=code, first=first, iota=iota)
    at, o = {}, 0
    for n, a in parts.items():
        at[n] = (o, a.shape[1])
        o += a.shape[1]
    return at, np.ascontiguousarray(np.concatenate(list(parts.values()), 1), dtype=np.float32)


CONST_AT, CONST = shape_constants()

PE_STEPS = ["mid", "image", "h1", "x1", "x2", "qpk", "sims0", "sims1"]
ACT_STEPS = ["mid", "sd1", "x1", "sd2", "x2", "qpk", "sims0", "sims1"]
DVE_STEPS = ["image", "h1", "var1", "xn1", "h2", "var2", "xn2"]
ATT_PE = [["q0", "q1", "q2", "q3", "k0", "k1", "k2", "k3", "v0", "v1", "scores", "pT0", "pT1", "o", "y"],
          ["q0", "q1", "q2", "q3", "k0", "k1", "k2", "k3", "scores", "pT0", "pT1", "o", "y"]]
ATT_ACT = [["q0", "q1", "q2", "q3", "v0", "v1", "exp", "pT", "oT"], ["q0", "q1", "q2", "q3", "exp", "pT", "oT"]]
ATT_DVE = [["k0", "k1", "k2", "k3", "shifted", "prob", "pT", "oT"], ["k0", "k1", "k2", "k3", "shifted", "prob"]]
TAIL_PE = ["k0", "k1", "k2", "k3", "scores", "pT", "o", "y"]
TAIL_ACT = ["exp", "pT", "oT"]
TAIL_DVE = ["k0", "k1", "k2", "k3", "shifted", "prob"]
BANKS = [dict(q=(2, 3, 4, 5), k=(6, 7, 2, 3), v=(4, 5), scores=6, pT=6, o=0, y=5),
         dict(q=(4, 5, 6, 7), k=(2, 3, 4, 5), scores=0, pT=0, o=2, y=4)]


def wait_apart(eng, sem, value, turns):
    eng.wait_ge(sem, value)
    if not isinstance(value, int):
        eng.sem_inc(turns, 1)


def reached(eng, sem, steps, name, turn, apart_from=None):
    value = turn * len(steps) + steps.index(name) + 1
    if apart_from is None:
        eng.wait_ge(sem, value)
    else:
        wait_apart(eng, sem, value, apart_from)


def strided(t, start, dims, rows=(0, P)):
    pitch = 1
    for n in t.shape[1:]:
        pitch *= n
    return bass.AP(tensor=t, offset=start + rows[0] * pitch,
                   ap=[[pitch, rows[1] - rows[0]]] + [[a, b] for a, b in dims])


BY_ACT = [0, 1, 3, 4, 5, 7, 11, 12, 14, 15]
DVE_SEQ = 19
RANK_SEQ = 58
LAST_SEQ = 5
TAIL_SEQ = 9


class Steps:

    def __init__(self, sem, per, turn):
        self.sem, self.per, self.turn, self.n = sem, per, turn, 0

    def add(self, ins):
        ins.then_inc(self.sem, 1)
        self.n += 1

    def so_far(self, eng):
        eng.wait_ge(self.sem, self.turn * self.per + self.n)

    def so_far_apart(self, eng, turns):
        wait_apart(eng, self.sem, self.turn * self.per + self.n, turns)

    def close(self):
        assert self.n == self.per, (self.sem, self.n)


def build(nc, x, const, w2s, w1s, fw, b1, b2, w2q, q1t, q2c, q2b, wq, wk, wv, wu, bu, wpk, pk, wq2, wo, table, out):
    ctx = ExitStack()
    with ctx:
        def sb(name, n, dt=F32):
            return ctx.enter_context(nc.sbuf_tensor(name, [P, n], dt))

        def sem(name):
            return ctx.enter_context(nc.semaphore(name))

        cst = sb("cst", CONST.shape[1])

        def const_of(name, rows=(0, P)):
            o, n = CONST_AT[name]
            return cst[rows[0]:rows[1], o:o + n]

        ident = const_of("ident")
        w2_all, w1_all = sb("w2_all", L * C), sb("w1_all", L * P)
        w2_now, w1_now, q_now = sb("w2_now", C), sb("w1_now", P), sb("q_now", C)
        q_all = sb("q_all", (L + 1) * C)
        fw_now = sb("fw_now", J * C)
        b1_all, b2_all = sb("b1_all", L * C), sb("b2_all", L * 16)
        q1_s, q2_s, q2b_s, q2blk = sb("q1_s", MID), sb("q2_s", 1), sb("q2b_s", 1), sb("q2blk", 16)
        wq_s, wk_s, wv_s, wpk_s, wq2_s = (sb(n, HE * S) for n in ("wq_s", "wk_s", "wv_s", "wpk_s", "wq2_s"))
        wu_s, wo_s, bu_s = sb("wu_s", 3 * S + PAD), sb("wo_s", 3 * S + PAD), sb("bu_s", S)
        pk_s = sb("pk_s", 4 * 4 * NK)

        img_in = sb("img_in", XP * GB)
        pixT = sb("pixT", XP * P)
        pix = sb("pix", XP * P)
        ux = sb("ux", M1 * P)
        uxT = sb("uxT", M1 * P)
        vk = sb("vk", 3 * 2 * J)
        modes = sb("modes", J * 16)
        mixed = sb("mixed", 576)
        mixT = sb("mixT", M1 * P)
        zx = sb("zx", 16 * P)
        zxT = sb("zxT", 16 * P)
        mid = sb("mid", 2 * BANK)

        hT = sb("hT", GB * S)
        h1, h2, h2p = sb("h1", 2 * S), sb("h2", 2 * S), sb("h2p", 2 * S)
        zero = sb("zero", C)
        stat, mv, rs, xn = sb("stat", 12), sb("mv", 4), sb("rs", 10), sb("xn", 2 * S)
        xT, xT2, xT2p = sb("xT", GB * S), sb("xT2", GB * S), sb("xT2p", GB * S)
        NQ = HE * GB * S
        qT, kT = [pix[0:S, 0:NQ], pixT[0:S, 0:NQ]], [pix[0:S, NQ:2 * NQ], pixT[0:S, NQ:2 * NQ]]
        kT1 = pixT
        vv = mid
        red = sb("red", 96)
        qpk = pix
        sims, sims2, oneh = sb("sims", 4 * HE * NK), sb("sims2", 2 * HE * NK), sb("oneh", HE * K * K)
        sc_at = (0, 2 * BANK)
        pT, oT = [ux, sims2], [uxT, oneh]
        vi = sb("vi", 2 * 2 * HE * K)
        iu = sb("iu", 2 * HE * K, U32)
        cand = sb("cand", HE * NC)
        cand2 = sims2
        top, pos = sb("top", HE * K), sb("pos", HE * K, U32)
        den = sb("den", 2 * HE)
        idx = sb("idx", 2 * HE * K, U32)
        wts = sb("wts", 2 * HE * K)
        ring = sb("ring", RING * K * P)
        w2q_s = ring
        kv = sb("kv", 2 * HE * P)
        kvp = sb("kvp", HE * P)
        kv_of = [kvp[:, :], kv[:, HE * P:2 * HE * P]]
        res = sb("res", 2 * S)

        ps = ctx.enter_context(nc.psum_tensor("ps", [P, 8, BANK], F32))

        cst_in, early = sem("constants_in"), sem("setup_weights_in")
        loaded, built, slots, gath = sem("loaded"), sem("built"), sem("slots_free"), [sem(f"gathered{i}") for i in range(RING)]
        memz = sem("zeroed")
        pe_turns, dve_turns, pool_turns = sem("pe_turns"), sem("dve_turns"), sem("pool_turns")
        qall_pe = sem("qall_pe")
        img_sem, img_done = sem("image_in"), sem("image_ready")
        fw_sem, staged = sem("fw_in"), sem("layer_weights")
        a_full, a_act = sem("ux_full"), sem("ux_act")
        t1_full, t1_act = sem("pix_full"), sem("pix_act")
        t2_full, t2_act = sem("uxT_full"), sem("uxT_act")
        v_full, v_act = sem("vk_full"), sem("vk_act")
        q_full = sem("mid_layer")
        c_full, c_done, c_seq = sem("modes_full"), sem("modes_done"), sem("modes_seq")
        m_full, m_act = sem("mixed_full"), sem("mixed_act")
        e_full, e_act, e_dve, e_seq = sem("mixT_full"), sem("mixT_act"), sem("mixT_dve"), sem("mixT_seq")
        f_full, f_act, f_dve = sem("zx_full"), sem("zx_act"), sem("zx_dve")
        t3_full, t3_act, t3_dve = sem("zxT_full"), sem("zxT_act"), sem("zxT_dve")
        r_full, rectified = sem("pixT_full"), sem("pixT_rectified")
        l1_full, l1_act, l1_dve = sem("last_full"), sem("last_act"), sem("last_dve")
        pe_step, act_step, dve_step = sem("pe_step"), sem("act_step"), sem("dve_step")
        att = [dict(pe=sem(f"att{i}_pe"), act=sem(f"att{i}_act"), dve=sem(f"att{i}_dve")) for i in range(2)]
        piece_seq, idx_ready = sem("piece_seq"), sem("idx_ready")
        att_seq = [sem("att0_seq"), sem("att1_seq")]
        dve_seq, rank_seq, first_seq, idx_first = sem("dve_seq"), sem("rank_seq"), sem("first_seq"), sem("idx_first")
        tail_pe, tail_act, tail_dve, tail_seq = sem("tail_pe"), sem("tail_act"), sem("tail_dve"), sem("tail_seq")
        top_ready, exp_done, weighed, scaled = sem("top_ready"), sem("exp_done"), sem("weighed"), sem("rows_scaled")
        saved, kv_saved, out_ready, stored = sem("tokens_saved"), sem("kv_saved"), sem("out_ready"), sem("stored")
        cleared = sem("images_cleared")

        N_EARLY, N_LOADS = 6, 11

        def ux_tile(t):
            return (strided(ux, t * 32, [(2, 16), (P, M1), (1, 2)]),
                    strided(ps, (2 + t) * BANK, [(2 * M1, 16), (2, M1), (1, 2)]))

        def vk_tile(t):
            return (strided(vk, t * 6, [(1, 6), (J, 6), (M1, M1)]),
                    strided(ps, (2 + t) * BANK, [(FX, 6), (M1, 6), (1, M1)]))

        def mixed_tile(t):
            return (strided(mixed, t * 24, [(4, 6), (48, 12), (1, 4)]),
                    strided(ps, (6 + t) * BANK, [(48, 6), (4, 12), (1, 4)]))

        def mixT_tile(k):
            r = (0, 4 * M1)
            return (strided(mixT, k * BANK, [(P, 4), (C, GB), (1, C)], r),
                    strided(ps, (2 + k) * BANK, [(C, 4), (P, GB), (1, C)], r))

        def zx_tile(k):
            return (strided(zx, k * 8, [(2, 4), (32, S), (1, 2)]),
                    strided(ps, (5 + k) * BANK, [(P, 4), (2, S), (1, 2)]))

        def pixT_tile(t):
            return (strided(pixT, (t // 2 * 8 + t % 2) * P, [(2 * P, 4), (1, P)]),
                    strided(ps, (6, 7, 2, 3, 4, 5, 6, 7)[t] * BANK, [(P, 4), (1, P)]))

        def oT_tile(i, b2):
            return (strided(oT[i], b2 * S, [(P, 2), (2 * P, 4), (1, S)]),
                    strided(ps, (BANKS[i]["o"] + b2) * BANK, [(4 * S, 2), (S, 4), (1, S)]))

        block = ctx.enter_context(nc.Block())

        @block.sync
        def _(sp):
            loads = [(cst[:, :], const), (w2_all[:, :], w2s), (b2_all[0:2 * C, :], b2), (w2q_s[0:C + 1, 0:(2 * L + 1) * P], w2q),
                     (q1_s[0:C + 1, :], q1t), (q2_s[:, :], q2c), (b1_all[0:1, :], b1), (q2b_s[:, :], q2b),
                     (wq_s[0:S + 1, :], wq), (wk_s[0:S + 1, :], wk), (wv_s[0:S + 1, :], wv), (wpk_s[0:S + 1, :], wpk),
                     (wq2_s[0:S + 1, :], wq2), (wu_s[:, 0:4 * S], wu), (wo_s[:, 0:4 * S], wo), (bu_s[:, :], bu), (pk_s[:, :], pk),
                     (w1_all[:, :], w1s)]
            assert len(loads) == 1 + N_EARLY + N_LOADS
            sp.dma_start(img_in[:, :], x[0]).then_inc(img_sem, 16)
            for i, (dst, src) in enumerate(loads):
                sp.dma_start(dst, src).then_inc(cst_in if i == 0 else early if i <= N_EARLY else loaded, 16)
            def layer_weights(g):
                with sp.Fori(1, L) as l:
                    sp.wait_ge(m_full, (g * L + l) * 2)
                    sp.dma_start(fw_now[:, :], fw[bass.ds(l, 1)].rearrange("a p n -> (a p) n")).then_inc(fw_sem, 16)

            sp.dma_start(fw_now[:, :], fw[0]).then_inc(fw_sem, 16)
            with sp.Fori(1, G) as g:
                layer_weights(g - 1)
                sp.wait_ge(m_full, g * L * 2)
                sp.dma_start(fw_now[:, :], fw[0]).then_inc(fw_sem, 16)
                sp.wait_ge(img_done, g)
                sp.dma_start(img_in[:, :], x[bass.ds(g, 1)].rearrange("a p n -> (a p) n")).then_inc(img_sem, 16)
            layer_weights(G - 1)

        @block.tensor
        def _(pe):
            def mm(out_, lhsT, rhs, start=True, stop=True, **kw):
                return nc.tensor.matmul(out_, lhsT, rhs, start=start, stop=stop, **kw)

            def turned(out_, in_, rows=P):
                return nc.tensor.transpose(out_, in_, ident[0:rows, 0:rows])

            def pix_tile(c, bank, sem_):
                for i in range(4):
                    xp = 4 * c + i
                    last = turned(ps[:, bank, i * P:(i + 1) * P], pixT[:, xp * P:(xp + 1) * P])
                last.then_inc(sem_, 1)

            def mid_layer(weights, last):
                for c in range(8):
                    q = c % 4
                    ins = mm(ps[32 * q:32 * q + 32, c // 4, :], weights, pix[:, c * BANK:(c + 1) * BANK],
                             start=False, stop=last, skip_group_check=True)
                return ins

            def layer(n):
                for xp in range(XP):
                    t, i = divmod(xp, 8)
                    if i == 0:
                        pe.wait_ge(rectified, n * 8 + max(2 * t + 2, 3))
                    ins = mm(ps[:, 2 + t, i * FY:i * FY + PAD], pixT[:, xp * P:(xp + 1) * P], const_of("fy"))
                    if i == 7:
                        ins.then_inc(a_full, 1)
                pe.wait_ge(staged, n * 3 + 3)
                pix_tile(0, 6, t1_full)
                pix_tile(1, 7, t1_full)
                pe.wait_ge(a_act, n * 4 + 4)
                for ky in range(M1):
                    t, i = divmod(ky, 4)
                    ins = turned(ps[:, 2 + t, i * P:(i + 1) * P], ux[:, ky * P:(ky + 1) * P])
                    if i == 3:
                        ins.then_inc(t2_full, 1)
                pix_tile(2, 5, t1_full)
                pe.wait_ge(t1_act, n * 8 + 1)
                pix_tile(3, 6, t1_full)
                pe.wait_ge(t2_act, n * 3 + 3)
                for ky in range(M1):
                    t, i = divmod(ky, 6)
                    ins = mm(ps[:, 2 + t, i * FX:i * FX + PAD], uxT[:, ky * P:(ky + 1) * P], const_of("fx"))
                    if i == 5:
                        ins.then_inc(v_full, 1)
                pe.wait_ge(t1_act, n * 8 + 2)
                pix_tile(4, 7, t1_full)
                pix_tile(5, 4, t1_full)
                pe.wait_ge(t1_act, n * 8 + 4)
                pix_tile(6, 6, t1_full)
                pe.wait_ge(t1_act, n * 8 + 5)
                pix_tile(7, 7, t1_full)
                pe.wait_ge(v_act, n * 2 + 2)
                wait_apart(pe, t1_act, n * 8 + 6, pe_turns)
                for ro in range(2):
                    for half in range(2):
                        for ri in range(2):
                            comp = (0, 2, 1, 0)[2 * ro + ri]
                            slot = 2 * half + ri
                            for b in range(GB):
                                r = slice(32 * b, 32 * b + 32)
                                ins = mm(ps[32 * slot:32 * slot + 32, 2 + b, ro * J:(ro + 1) * J], w2_now[r, :],
                                         vk[r, (2 * comp + half) * J:(2 * comp + half + 1) * J], skip_group_check=True)
                ins.then_inc(c_full, 1)
                pe.wait_ge(t1_act, n * 8 + 8)
                mid_layer(q_now[:, :], False).then_inc(q_full, 1)
                pe.wait_ge(fw_sem, n * 16 + 16)
                for kx in range(M1):
                    if kx % 6 == 0:
                        pe.wait_ge(c_done, n * 2 + kx // 6 + 1)
                    for ky in range(M1):
                        j, q = kx * M1 + ky, ky % 4
                        at = ((kx % 6) * 3 + ky // 4) * 16
                        ins = mm(ps[32 * q:32 * q + 32, 6 + kx // 6, at:at + 16], fw_now[:, j * C:(j + 1) * C],
                                 modes[:, j * 16:(j + 1) * 16], skip_group_check=True)
                    if kx % 6 == 5:
                        ins.then_inc(m_full, 1)
                pe.wait_ge(m_act, n * 2 + 2)
                for kyi in range(3):
                    for b in range(GB):
                        ins = mm(ps[0:4 * M1, 2 + kyi, b * P:(b + 1) * P],
                                 mixed[:, (kyi * GB + b) * 48:(kyi * GB + b + 1) * 48], w1_now[:, :])
                    ins.then_inc(e_full, 1)
                pe.wait_ge(e_act, n + 1)
                pe.wait_ge(e_dve, n * 2 + 2)
                for ky in range(M1):
                    kyi, q = divmod(ky, 4)
                    ins = mm(ps[:, 5 + kyi, q * P:(q + 1) * P],
                             mixT[:, ky * P:(ky + 1) * P], const_of("iv"))
                    if q == 3:
                        ins.then_inc(f_full, 1)
                pe.wait_ge(f_act, n * 2 + 2)
                pe.wait_ge(f_dve, n + 1)
                for xq in range(16):
                    t, i = divmod(xq, 4)
                    ins = turned(ps[:, 2 + t, i * P:(i + 1) * P], zx[:, xq * P:(xq + 1) * P])
                    if i == 3:
                        ins.then_inc(t3_full, 1)
                pe.wait_ge(t3_act, n * 2 + 2)
                pe.wait_ge(t3_dve, n * 2 + 2)
                o = CONST_AT["g"][0]
                for t in range(8):
                    xqq, p = divmod(t, 2)
                    if t >= 6:
                        pe.wait_ge(rectified, n * 8 + 8 + t - 5)
                    mm(ps[:, (6, 7, 2, 3, 4, 5, 6, 7)[t], :], cst[:, o + p * P:o + (p + 1) * P],
                       zxT[:, xqq * BANK:(xqq + 1) * BANK]).then_inc(r_full, 1)

            def tokenizer(g):
                pe.wait_ge(img_done, g + 1)
                for c in range(8):
                    q = c % 4
                    mm(ps[32 * q:32 * q + 32, c // 4, 0:16], zero[:, 0:C], zero[:, 0:16], start=True, stop=False,
                       skip_group_check=True)
                with pe.Fori(0, L) as l:
                    layer(g * L + l)

            def queries(i, turn):
                X, W = ((xT, wq_s), (xT2p, wq2_s))[i]
                for t in range(4):
                    for h in (2 * t, 2 * t + 1):
                        ins = mm(ps[0:S, BANKS[i]["q"][t], (h % 2) * 256:(h % 2 + 1) * 256], W[0:S + 1, h * S:(h + 1) * S],
                                 X[0:S + 1, :])
                    ins.then_inc(att[i]["pe"], 1)

            def keys(i, turn):
                for t in range(4):
                    if t >= 2:
                        reached(pe, att[i]["act"], ATT_ACT[i], f"q{t - 2}", turn, pe_turns)
                    for h in (2 * t, 2 * t + 1):
                        bank, at = BANKS[i]["k"][t], (h % 2) * 256
                        if i == 0:
                            ins = mm(ps[0:S, bank, at:at + 256], wk_s[0:S + 1, h * S:(h + 1) * S], xT[0:S + 1, :])
                        else:
                            for tt in range(2):
                                ins = turned(ps[0:S, bank, at + tt * P:at + (tt + 1) * P],
                                             kv_of[tt][:, h * P:h * P + S])
                    ins.then_inc(att[i]["pe"], 1)

            def values(turn):
                for t in range(2):
                    reached(pe, att[0]["act"], ATT_ACT[0], f"q{2 + t}", turn)
                    mm(ps[:, BANKS[0]["v"][t], :], xT[0:S + 1, t * P:(t + 1) * P], wv_s[0:S + 1, :]).then_inc(att[0]["pe"], 1)

            def scores(i, turn):
                reached(pe, att[i]["act"], ATT_ACT[i], "q3", turn)
                reached(pe, att[i]["dve"], ATT_DVE[i], "k3", turn, pe_turns)
                for hp in range(4):
                    for b in range(GB):
                        for h2 in range(2):
                            c = (2 * hp + h2) * GB * S + b * S
                            ins = mm(ps[S * h2:S * h2 + S, BANKS[i]["scores"] + hp // 2,
                                        (hp % 2) * 256 + b * S:(hp % 2) * 256 + (b + 1) * S],
                                     qT[i][:, c:c + S], kT[i][:, c:c + S], skip_group_check=True)
                ins.then_inc(att[i]["pe"], 1)

            def turned_probs(i, turn):
                reached(pe, att[i]["dve"], ATT_DVE[i], "prob", turn)
                for k in range(8):
                    ins = turned(ps[:, BANKS[i]["pT"] + k // 4, (k % 4) * P:(k % 4 + 1) * P],
                                 zxT[:, sc_at[i] + k * P:sc_at[i] + (k + 1) * P])
                    if k % 4 == 3:
                        ins.then_inc(att[i]["pe"], 1)

            def weighted(i, turn):
                if i == 0:
                    reached(pe, att[i]["dve"], ATT_DVE[i], "pT", turn)
                reached(pe, att[i]["act"], ATT_ACT[i], "pT", turn, pe_turns)
                for hp in range(4):
                    for bp in range(2):
                        for h2 in range(2):
                            for b2 in range(2):
                                r = slice(S * b2, S * b2 + S)
                                h = 2 * hp + h2
                                v = vv[r, bp * 512 + h * S:bp * 512 + (h + 1) * S] if i == 0 else \
                                    kv_of[bp][r, h * P + S:(h + 1) * P]
                                ins = mm(ps[S * h2:S * h2 + S, BANKS[i]["o"] + b2, (bp * 4 + hp) * S:(bp * 4 + hp + 1) * S], v,
                                         pT[i][r, (hp * 2 + bp) * P + h2 * S:(hp * 2 + bp) * P + (h2 + 1) * S],
                                         skip_group_check=True)
                ins.then_inc(att[i]["pe"], 1)

            def result(i, turn):
                if i == 0:
                    reached(pe, att[i]["dve"], ATT_DVE[i], "oT", turn)
                reached(pe, att[i]["act"], ATT_ACT[i], "oT", turn)
                W = (wu_s, wo_s)[i]
                for bp in range(2):
                    for hp in range(4):
                        ins = mm(ps[:, BANKS[i]["y"], bp * P:bp * P + PAD], oT[i][:, (hp * 2 + bp) * P:(hp * 2 + bp + 1) * P],
                                 W[:, hp * S:hp * S + PAD], start=(hp == 0), stop=(hp == 3), skip_group_check=True)
                ins.then_inc(att[i]["pe"], 1)

            def stay_awake(bank, n):
                for _ in range(n):
                    mm(ps[:, bank, :], ident, cst[:, 0:BANK])

            def features_down(g, name):
                reached(pe, dve_step, DVE_STEPS, name, g, pe_turns)
                for t in range(2):
                    ins = turned(ps[0:S, 6, t * P:(t + 1) * P], xn[:, t * S:(t + 1) * S])
                ins.then_inc(pe_step, 1)

            def group(g, g_last):
                tokenizer(g)
                pe.wait_ge(rectified, g * 8 * L + 8 * L + 8)
                for c in range(8):
                    if c == 6:
                        pe.wait_ge(l1_act, g * 4 + 1)
                        pe.wait_ge(l1_dve, g * 4 + 1)
                    pix_tile(c, (2, 3, 4, 5, 6, 7, 2, 3)[c], l1_full)
                if g_last is not None:
                    pe.wait_ge(l1_act, g * 4 + 3)
                    pe.wait_ge(l1_dve, g * 4 + 3)
                    pe.wait_ge(saved, g_last + 1)
                    queries(1, g_last)
                pe.wait_ge(l1_act, g * 4 + 4)
                pe.wait_ge(l1_dve, g * 4 + 4)
                mid_layer(q_all[:, L * C:(L + 1) * C], True).then_inc(pe_step, 1)
                if g_last is not None:
                    pe.wait_ge(kv_saved, g_last + 1)
                    wait_apart(pe, slots, RING + (g_last + 1) * PIECES, pe_turns)
                    keys(1, g_last)
                if g_last is not None:
                    reached(pe, att[1]["act"], ATT_ACT[1], "q2", g_last)
                reached(pe, act_step, ACT_STEPS, "mid", g)
                for i in range(8):
                    ins = mm(ps[:, 6, i * 16:(i + 1) * 16], mid[:, i * P:(i + 1) * P], q2blk[:, :])
                ins.then_inc(pe_step, 1)
                if g_last is not None:
                    scores(1, g_last)
                reached(pe, dve_step, DVE_STEPS, "image", g, pe_turns)
                for t in range(2):
                    ins = turned(ps[:, 7, t * S:(t + 1) * S], hT[0:S, t * P:(t + 1) * P], S)
                ins.then_inc(pe_step, 1)
                stay_awake(2, 3)
                features_down(g, "xn1")
                reached(pe, act_step, ACT_STEPS, "x1", g)
                queries(0, g)
                keys(0, g)
                values(g)
                scores(0, g)
                if g_last is not None:
                    turned_probs(1, g_last)
                    weighted(1, g_last)
                else:
                    stay_awake(2, 7)
                turned_probs(0, g)
                weighted(0, g)
                result(0, g)
                if g_last is not None:
                    result(1, g_last)
                stay_awake(2, 2 if g_last is not None else 4)
                features_down(g, "xn2")
                reached(pe, act_step, ACT_STEPS, "x2", g)
                for c in range(4):
                    ins = mm(ps[:, 2 + c // 2, (c % 2) * 256:(c % 2 + 1) * 256], wpk_s[0:S + 1, c * P:(c + 1) * P], xT2[0:S + 1, :])
                ins.then_inc(pe_step, 1)
                if g_last is not None:
                    pe.wait_ge(out_ready, g_last + 1)
                reached(pe, act_step, ACT_STEPS, "qpk", g)
                for t in range(2):
                    for c in range(4):
                        ins = mm(ps[:, 4 + 2 * t + c // 2, (c % 2) * 256:(c % 2 + 1) * 256],
                                 qpk[:, c * 256 + t * P:c * 256 + (t + 1) * P], pk_s[:, c * 256:(c + 1) * 256])
                    ins.then_inc(pe_step, 1)
                reached(pe, act_step, ACT_STEPS, "sims0", g, pe_turns)

            pe.wait_ge(early, 16 * N_EARLY)
            for s in range(1, L + 1):
                mm(ps[:, 2, s * MID:(s + 1) * MID], w2q_s[0:C + 1, s * P:(s + 1) * P], q1_s[0:C + 1, :],
                   skip_group_check=True)
            for k, s in enumerate([0] + list(range(L + 1, 2 * L + 1))):
                ins = mm(ps[:, 2, 0:MID], w2q_s[0:C + 1, s * P:(s + 1) * P], q1_s[0:C + 1, :],
                         start=(k == 0), stop=(k == L), skip_group_check=True)
            ins.then_inc(qall_pe, 1)
            pe.wait_ge(built, 1)
            pe.wait_ge(loaded, 16 * N_LOADS)
            group(0, None)
            group(1, None)
            with pe.Fori(2, G) as g:
                group(g, g - 2)
            reached(pe, act_step, ACT_STEPS, "sims1", G - 1)
            pe.wait_ge(saved, G - 1)
            queries(1, G - 2)
            pe.wait_ge(kv_saved, G - 1)
            pe.wait_ge(slots, RING + (G - 1) * PIECES)
            keys(1, G - 2)
            scores(1, G - 2)
            turned_probs(1, G - 2)
            weighted(1, G - 2)
            result(1, G - 2)
            pe.wait_ge(saved, G)
            pe.wait_ge(out_ready, G - 1)
            queries(1, G - 1)
            reached(pe, att[1]["act"], ATT_ACT[1], "q3", G - 1)
            for bp in range(2):
                if bp:
                    pe.wait_ge(slots, RING + G * PIECES - 1)
                    stay_awake(7, 8)
                pe.wait_ge(slots, RING + (G - 1) * PIECES + HE * (bp + 1))
                for h in range(HE):
                    ins = turned(ps[0:S, BANKS[1]["k"][h // 2], (h % 2) * P:(h % 2 + 1) * P],
                                 kv[:, (bp * HE + h) * P:(bp * HE + h) * P + S])
                    if h % 2:
                        ins.then_inc(tail_pe, 1)
                reached(pe, tail_dve, TAIL_DVE, "k3", bp)
                for hp in range(4):
                    for b in (2 * bp, 2 * bp + 1):
                        for h2 in range(2):
                            c = (2 * hp + h2) * GB * S + b * S
                            ins = mm(ps[S * h2:S * h2 + S, BANKS[1]["scores"] + hp // 2,
                                        (hp % 2) * 256 + b * S:(hp % 2) * 256 + (b + 1) * S],
                                     qT[1][:, c:c + S], kT[1][:, c:c + S], skip_group_check=True)
                ins.then_inc(tail_pe, 1)
                stay_awake(2, 4)
                reached(pe, tail_dve, TAIL_DVE, "prob", bp)
                for hp in range(4):
                    k = 2 * hp + bp
                    ins = turned(ps[:, BANKS[1]["pT"] + k // 4, (k % 4) * P:(k % 4 + 1) * P],
                                 zxT[:, sc_at[1] + k * P:sc_at[1] + (k + 1) * P])
                ins.then_inc(tail_pe, 1)
                reached(pe, tail_act, TAIL_ACT, "pT", bp)
                for hp in range(4):
                    for h2 in range(2):
                        for b2 in range(2):
                            r = slice(S * b2, S * b2 + S)
                            h = 2 * hp + h2
                            ins = mm(ps[S * h2:S * h2 + S, BANKS[1]["o"] + b2, (bp * 4 + hp) * S:(bp * 4 + hp + 1) * S],
                                     kv[r, (bp * HE + h) * P + S:(bp * HE + h + 1) * P],
                                     pT[1][r, (hp * 2 + bp) * P + h2 * S:(hp * 2 + bp) * P + (h2 + 1) * S],
                                     skip_group_check=True)
                ins.then_inc(tail_pe, 1)
                reached(pe, tail_act, TAIL_ACT, "oT", bp)
                for hp in range(4):
                    ins = mm(ps[:, 6 + bp, 0:PAD], oT[1][:, (hp * 2 + bp) * P:(hp * 2 + bp + 1) * P],
                             wo_s[:, hp * S:hp * S + PAD], start=(hp == 0), stop=(hp == 3), skip_group_check=True)
                ins.then_inc(tail_pe, 1)

        @block.scalar
        def _(act):
            def copy(out_, in_, func=ACT.Copy, **kw):
                return nc.scalar.activation(out_, in_, func, **kw)

            def bank(b, n=BANK, rows=(0, P)):
                return ps[rows[0]:rows[1], b, 0:n]

            def layer(g, l, work):
                n = g * L + l
                copy(w2_now[:, :], w2_all[:, l * C:(l + 1) * C]).then_inc(staged, 1)
                copy(w1_now[:, :], w1_all[:, l * P:(l + 1) * P]).then_inc(staged, 1)
                copy(q_now[:, :], q_all[:, l * C:(l + 1) * C]).then_inc(staged, 1)

                def pix_tile(c):
                    act.wait_ge(t1_full, n * 8 + c + 1)
                    copy(pix[:, c * BANK:(c + 1) * BANK], bank((6, 7, 5, 6, 7, 4, 6, 7)[c])).then_inc(t1_act, 1)

                for t in range(4):
                    act.wait_ge(a_full, n * 4 + t + 1)
                    copy(*ux_tile(t)).then_inc(a_act, 1)
                pix_tile(0)
                for t in range(3):
                    act.wait_ge(t2_full, n * 3 + t + 1)
                    copy(uxT[:, t * BANK:(t + 1) * BANK], bank(2 + t)).then_inc(t2_act, 1)
                pix_tile(1)
                pix_tile(2)
                for t in range(2):
                    act.wait_ge(v_full, n * 2 + t + 1)
                    copy(*vk_tile(t)).then_inc(v_act, 1)
                for c in range(3, 8):
                    pix_tile(c)
                work()
                for t in range(2):
                    act.wait_ge(m_full, n * 2 + t + 1)
                    copy(*mixed_tile(t)).then_inc(m_act, 1)
                act.wait_ge(e_full, n * 3 + 2)
                copy(*mixT_tile(1)).then_inc(e_act, 1)
                for k in (0, 2):
                    act.wait_ge(f_full, n * 3 + k + 1)
                    copy(*zx_tile(k)).then_inc(f_act, 1)
                for t in (1, 3):
                    act.wait_ge(t3_full, n * 4 + t + 1)
                    copy(zxT[:, t * BANK:(t + 1) * BANK], bank(2 + t)).then_inc(t3_act, 1)
                for t in range(8):
                    act.wait_ge(r_full, n * 8 + t + 1)
                    copy(*pixT_tile(t), ACT.Relu).then_inc(rectified, 1)

            def weigh(turn, t):
                if turn is None:
                    return
                act.wait_ge(top_ready, turn * 2 + t + 1)
                nc.scalar.activation(top[:, :], top[:, :], ACT.Exp).then_inc(exp_done, 1)

            def clear_images():
                copy(pixT[:, :], strided(zero, 0, [(0, XP * P)]))

            def clear_modes():
                copy(modes[:, :], strided(zero, 0, [(0, J * 16)])).then_inc(cleared, 1)

            def draw_grid(g):
                act.wait_ge(cleared, g + 1)
                for k in range(3):
                    copy(strided(pixT, k + 1, [(P, XP), (C, GB)]), strided(cst, CONST_AT["grid"][0] + k, [(3, XP), (0, GB)]))

            def tokenizer(g, g_rank, g_last):
                act.wait_ge(img_sem, 16 * g + 16)
                copy(strided(pixT, 0, [(C, XP * GB)]), img_in[:, :]).then_inc(img_done, 1)
                if g_last is None:
                    work = [lambda: None, lambda: weigh_rows(g_rank, [0, 1]),
                            lambda: weigh_rows(g_rank, [3, 4]), lambda: (weigh(g_rank, 1), weigh_rows(g_rank, [5]))]
                else:
                    save_keys(g_last)
                    work = [lambda: weigh_rows(g_last, [11, 12]),
                            lambda: (weigh(g_rank, 0), weigh_rows(g_last, [14, 15])),
                            lambda: weigh_rows(g_rank, [0, 1]),
                            lambda: (weigh(g_rank, 1), weigh_rows(g_rank, [3, 4]))]
                for l in range(L):
                    if l == 1 and g_last is None:
                        weigh(g_rank, 0)
                    layer(g, l, work[l])

            def weigh_rows(turn, ks):
                if turn is None:
                    return
                for k in ks:
                    slot = k % RING
                    act.wait_ge(weighed, turn * 2 + k // HE + 1)
                    act.wait_ge(gath[slot], (turn * (PIECES // RING) + k // RING + 1) * K * 16)
                    for m in range(K):
                        rows = ring[:, (slot * K + m) * P:(slot * K + m + 1) * P]
                        ins = nc.scalar.activation(rows, rows, ACT.Copy, scale=wts[:, k * K + m:k * K + m + 1])
                    ins.then_inc(scaled, 1)

            def deviation(g, i):
                reached(act, dve_step, DVE_STEPS, f"var{i}", g)
                nc.scalar.activation(rs[:, 0:2], rs[:, 2:4], ACT.Sqrt).then_inc(act_step, 1)
                reached(act, pe_step, PE_STEPS, f"x{i}", g)
                copy((xT, xT2)[i - 1][0:S, :], bank(6, 256, (0, S))).then_inc(act_step, 1)

            def save_keys(turn):
                act.wait_ge(slots, RING + turn * PIECES + HE)
                copy(kvp[:, :], kv[:, 0:HE * P]).then_inc(kv_saved, 1)

            def queries(i, turn, ts=range(4)):
                for t in ts:
                    reached(act, att[i]["pe"], ATT_PE[i], f"q{t}", turn)
                    copy(qT[i][:, t * BANK:(t + 1) * BANK], bank(BANKS[i]["q"][t], BANK, (0, S)),
                         scale=float(S) ** -0.5).then_inc(att[i]["act"], 1)

            def values(turn):
                for t in range(2):
                    reached(act, att[0]["pe"], ATT_PE[0], f"v{t}", turn)
                    copy(vv[:, t * BANK:(t + 1) * BANK], bank(BANKS[0]["v"][t])).then_inc(att[0]["act"], 1)

            def exp(i, turn):
                reached(act, att[i]["dve"], ATT_DVE[i], "shifted", turn)
                s = zxT[:, sc_at[i]:sc_at[i] + 2 * BANK]
                nc.scalar.activation(s, s, ACT.Exp).then_inc(att[i]["act"], 1)

            def turned_probs(i, turn):
                if i == 0:
                    reached(act, att[i]["pe"], ATT_PE[i], "pT0", turn)
                    copy(pT[i][:, 0:BANK], bank(BANKS[i]["pT"])).then_inc(att[i]["act"], 1)
                else:
                    reached(act, att[i]["pe"], ATT_PE[i], "pT1", turn)
                    copy(pT[i][:, 0:2 * BANK], ps[:, BANKS[i]["pT"]:BANKS[i]["pT"] + 2, :].rearrange("p a b -> p (a b)")
                         ).then_inc(att[i]["act"], 1)

            def weighted(i, turn):
                reached(act, att[i]["pe"], ATT_PE[i], "o", turn)
                if i == 1:
                    copy(*oT_tile(i, 1))
                copy(*oT_tile(i, 0)).then_inc(att[i]["act"], 1)

            def group(g, g_rank, g_last):
                tokenizer(g, g_rank, g_last)
                for c in (0, 2, 4, 6):
                    act.wait_ge(l1_full, g * 8 + c + 1)
                    copy(pix[:, c * BANK:(c + 1) * BANK], bank((2, 3, 4, 5, 6, 7, 2, 3)[c])).then_inc(l1_act, 1)
                if g_last is not None:
                    queries(1, g_last, range(3))
                reached(act, pe_step, PE_STEPS, "mid", g)
                copy(mid[:, :], ps[:, 0:2, :].rearrange("p a b -> p (a b)"), ACT.Relu).then_inc(act_step, 1)
                if g_last is not None:
                    queries(1, g_last, [3])
                weigh_rows(g_rank, [5] if g_last is not None else [7])
                deviation(g, 1)
                if g_last is not None:
                    exp(1, g_last)
                queries(0, g)
                values(g)
                if g_last is not None:
                    weigh_rows(g_rank, [7])
                    turned_probs(1, g_last)
                exp(0, g)
                if g_last is not None:
                    weighted(1, g_last)
                turned_probs(0, g)
                clear_images()
                weighted(0, g)
                clear_modes()
                draw_grid(g + 1)
                deviation(g, 2)
                reached(act, pe_step, PE_STEPS, "qpk", g)
                copy(qpk[:, 0:2 * BANK], ps[:, 2:4, :].rearrange("p a b -> p (a b)")).then_inc(act_step, 1)
                for t in range(2):
                    reached(act, pe_step, PE_STEPS, f"sims{t}", g)
                    copy(sims[:, t * 2 * BANK:(t + 1) * 2 * BANK],
                         ps[:, 4 + 2 * t:6 + 2 * t, :].rearrange("p a b -> p (a b)")).then_inc(act_step, 1)
                if g_last is not None:
                    store(g_last)

            def store(turn):
                act.wait_ge(out_ready, turn + 1)
                act.dma_start(out[bass.ds(turn, 1)].rearrange("a t p n -> p (a t) n"),
                              res[:, :].rearrange("p (t n) -> p t n", t=2)).then_inc(stored, 16)

            act.wait_ge(memz, 1)
            clear_images()
            clear_modes()
            act.wait_ge(cst_in, 16)
            draw_grid(0)
            act.wait_ge(built, 1)
            act.wait_ge(loaded, 16 * N_LOADS)
            group(0, None, None)
            group(1, 0, None)
            with act.Fori(2, G) as g:
                group(g, g - 1, g - 2)
            weigh(G - 1, 0)
            save_keys(G - 2)
            weigh_rows(G - 2, [11, 12, 14, 15])
            weigh(G - 1, 1)
            weigh_rows(G - 1, [0, 1, 3])
            queries(1, G - 2)
            exp(1, G - 2)
            turned_probs(1, G - 2)
            weighted(1, G - 2)
            store(G - 2)
            weigh_rows(G - 1, [4, 5, 7])
            queries(1, G - 1)
            for bp in range(2):
                reached(act, tail_dve, TAIL_DVE, "shifted", bp)
                half = [(2 * P, 4), (1, P)]
                probs = strided(zxT, sc_at[1] + bp * P, half)
                nc.scalar.activation(probs, probs, ACT.Exp).then_inc(tail_act, 1)
                reached(act, tail_pe, TAIL_PE, "pT", bp)
                copy(strided(pT[1], bp * P, half), strided(ps, BANKS[1]["pT"] * BANK + bp * P, half)).then_inc(tail_act, 1)
                reached(act, tail_pe, TAIL_PE, "o", bp)
                for b2 in range(2):
                    ins = copy(strided(oT[1], bp * P + b2 * S, [(2 * P, 4), (1, S)]),
                               strided(ps, (BANKS[1]["o"] + b2) * BANK + bp * 4 * S, [(S, 4), (1, S)]))
                ins.then_inc(tail_act, 1)
                if bp == 0:
                    weigh_rows(G - 1, [11, 12, 14])
            store(G - 1)
            act.wait_ge(stored, 16 * G + 16)

        @block.vector
        def _(dve):
            v = nc.vector

            def bank(b, n=BANK, rows=(0, P)):
                return ps[rows[0]:rows[1], b, 0:n]

            def piece(k, turn, last=False):
                slot = k % RING
                if k in BY_ACT and not last:
                    dve.wait_ge(scaled, turn * len(BY_ACT) + BY_ACT.index(k) + 1)
                else:
                    mine = [i for i in range(PIECES) if i not in BY_ACT]
                    dve.wait_ge(gath[slot], (turn * (PIECES // RING) + k // RING + 1) * K * 16)
                    rows = strided(ring, slot * K * P, [(P, K), (1, P)])
                    v.tensor_tensor(rows, rows, strided(wts, k * K, [(1, K), (0, P)]), ALU.mult).then_inc(piece_seq, 1)
                    dve.wait_ge(piece_seq, turn * len(mine) + (len(mine) if last else mine.index(k)) + 1)
                v.tensor_reduce(kv[:, k * P:(k + 1) * P], strided(ring, slot * K * P, [(1, P), (P, K)]), AX.X,
                                ALU.add).then_inc(slots, 1)

            def layer(g, l, work):
                n = g * L + l
                work(0)
                if l == 0:
                    dve.wait_ge(img_done, g + 1)
                v.tensor_tensor(modes[0:2 * C, 0:16], modes[0:2 * C, 0:16], b2_all[0:2 * C, l * 16:(l + 1) * 16],
                                ALU.add).then_inc(c_seq, 1)
                dve.wait_ge(c_seq, n + 1)
                dve.wait_ge(c_full, n + 1)
                for part in range(2):
                    for h in range(2):
                        r = (64 * h, 64 * h + 64)
                        m = strided(modes, part * J // 2 * 16 + 2 * h, [(4, GB), (1, 2), (16, J // 2)], r)
                        ins = v.tensor_tensor(m, m, strided(ps, 2 * BANK + part * J // 2, [(BANK, GB), (J, 2), (1, J // 2)], r),
                                              ALU.add)
                    ins.then_inc(c_done, 1)
                work(1)
                dve.wait_ge(e_full, n * 3 + 1)
                v.tensor_copy(*mixT_tile(0)).then_inc(e_seq, 1)
                dve.wait_ge(e_seq, n + 1)
                m = strided(mixT, 0, [(C, GB), (1, C)], (0, 1))
                v.tensor_tensor(m, m, strided(b1_all, l * C, [(0, GB), (1, C)], (0, 1)), ALU.add).then_inc(e_dve, 1)
                dve.wait_ge(e_full, n * 3 + 3)
                v.tensor_copy(*mixT_tile(2)).then_inc(e_dve, 1)
                dve.wait_ge(f_full, n * 3 + 2)
                v.tensor_copy(*zx_tile(1)).then_inc(f_dve, 1)
                for t in (0, 2):
                    dve.wait_ge(t3_full, n * 4 + t + 1)
                    v.tensor_copy(zxT[:, t * BANK:(t + 1) * BANK], bank(2 + t)).then_inc(t3_dve, 1)

            def normalise(h, i, g, seq):
                for t in range(2):
                    seq.add(v.bn_stats(stat[:, 6 * t:6 * t + 6], h[:, t * S:(t + 1) * S]))
                seq.so_far_apart(dve, dve_turns)
                for t in range(2):
                    seq.add(v.bn_aggr(mv[:, 2 * t:2 * t + 2], stat[:, 6 * t:6 * t + 6]))
                seq.so_far(dve)
                var, sd, r, u = rs[:, 2:4], rs[:, 0:2], rs[:, 4:6], rs[:, 6:8]
                v.tensor_scalar(var, strided(mv, 1, [(2, 2)]), EPS, None, ALU.add).then_inc(dve_step, 1)
                reached(dve, act_step, ACT_STEPS, f"sd{i}", g)
                seq.add(v.reciprocal(r, sd))
                seq.so_far(dve)
                seq.add(v.tensor_tensor(u, r, r, ALU.mult))
                seq.so_far(dve)
                seq.add(v.tensor_tensor(u, u, var, ALU.mult))
                seq.so_far(dve)
                seq.add(v.tensor_scalar(u, u, -0.5, 1.5, ALU.mult, ALU.add))
                seq.so_far(dve)
                seq.add(v.tensor_tensor(r, r, u, ALU.mult))
                seq.so_far(dve)
                for t in range(2):
                    ins = v.tensor_scalar(xn[:, t * S:(t + 1) * S], h[:, t * S:(t + 1) * S], mv[:, 2 * t:2 * t + 1],
                                          rs[:, 4 + t:5 + t], ALU.subtract, ALU.mult)
                ins.then_inc(dve_step, 1)

            def keys(i, turn, ts=range(4)):
                for t in ts:
                    reached(dve, att[i]["pe"], ATT_PE[i], f"k{t}", turn)
                    v.tensor_copy(kT[i][:, t * BANK:(t + 1) * BANK], bank(BANKS[i]["k"][t], BANK, (0, S))
                                  ).then_inc(att[i]["dve"], 1)

            def masked(i, turn, seq):
                reached(dve, att[i]["pe"], ATT_PE[i], "scores", turn)
                rows = strided(zxT, sc_at[i], [(S, 16), (1, S)])
                o = CONST_AT[("strict", "causal")[i]][0]
                seq.add(v.tensor_tensor(rows, strided(ps, BANKS[i]["scores"] * BANK, [(S, 16), (1, S)]),
                                        strided(cst, o, [(0, 16), (1, S)]), ALU.add))
                seq.so_far(dve)
                seq.add(v.tensor_reduce(red[:, 48 * i:48 * i + 16], rows, AX.X, ALU.max))
                seq.so_far(dve)
                v.tensor_tensor(rows, rows, strided(red, 48 * i, [(1, 16), (0, S)]), ALU.subtract).then_inc(att[i]["dve"], 1)

            def result(i):
                return strided(ps, BANKS[i]["y"] * BANK, [(P, 2), (1, S)])

            def probabilities(i, turn, seq):
                rows = strided(zxT, sc_at[i], [(S, 16), (1, S)])
                total, inverse = red[:, 48 * i + 16:48 * i + 32], red[:, 48 * i + 32:48 * i + 48]
                reached(dve, att[i]["act"], ATT_ACT[i], "exp", turn)
                seq.add(v.tensor_reduce(total, rows, AX.X, ALU.add))
                seq.so_far(dve)
                seq.add(v.reciprocal(inverse, total))
                seq.so_far(dve)
                if i == 0:
                    seq.add(v.tensor_scalar(inverse, inverse, const_of("rows")[:, 0:1], None, ALU.mult))
                    seq.so_far(dve)
                v.tensor_tensor(rows, rows, strided(red, 48 * i + 32, [(1, 16), (0, S)]), ALU.mult).then_inc(att[i]["dve"], 1)

            def rank(t, g, seq):
                reached(dve, act_step, ACT_STEPS, f"sims{t}", g, dve_turns)
                if isinstance(g, int) and g == t == 0:
                    first = Steps(first_seq, RANK_SEQ // 2 - 2, 0)
                    yield from rank_heads(t, 0, HE // 2, first, idx_first)
                    first.so_far(dve)
                    first.close()
                    yield
                    yield from rank_heads(t, HE // 2, HE // 2, seq, idx_ready)
                else:
                    yield from rank_heads(t, 0, HE, seq, idx_ready)
                yield
                dve.wait_ge(exp_done, g * 2 + t + 1)
                w = strided(top, 0, [(K, HE), (1, K)])
                seq.add(v.tensor_reduce(den[:, 0:HE], w, AX.X, ALU.add))
                seq.so_far(dve)
                seq.add(v.reciprocal(den[:, HE:2 * HE], den[:, 0:HE]))
                seq.so_far(dve)
                v.tensor_tensor(wts[:, t * HE * K:(t + 1) * HE * K].rearrange("p (h k) -> p h k", k=K), w,
                                strided(den, HE, [(1, HE), (0, K)]), ALU.mult).then_inc(weighed, 1)
                dve.wait_ge(weighed, g * 2 + t + 1)

            def rank_heads(t, h0, n, seq, done):
                heads = range(h0, h0 + n)
                halves = [half * HE + h for half in range(2) for h in heads]
                ranks = {r: strided(vi, (r // HE * 2 * HE + r % HE) * K, [(1, K)]) for r in halves}
                sim = {r: sims[:, (t * 2 * HE + r) * NK:(t * 2 * HE + r + 1) * NK] for r in halves}
                mine = slice(h0 * K, (h0 + n) * K)
                steps, posf, code, whole, base, behind, place, found, row = [
                    sims2[:, HE * NC + i * HE * K + mine.start:HE * NC + i * HE * K + mine.stop]
                    for i in (0, 1, 2, 3, 0, 2, 1, 3, 2)]
                for r in halves:
                    ins = v.max(ranks[r][:, 0:8], sim[r])
                seq.add(ins)
                seq.so_far_apart(dve, dve_turns)
                for r in halves:
                    ins = v.match_replace(sims2[:, r * NK:(r + 1) * NK], ranks[r][:, 0:8], sim[r], LOWEST)
                seq.add(ins)
                yield
                for r in halves:
                    v.max_index(iu[:, r * K:r * K + 8], ranks[r][:, 0:8], sim[r])
                yield
                seq.so_far_apart(dve, dve_turns)
                for r in halves:
                    ins = v.max(ranks[r][:, 8:16], sims2[:, r * NK:(r + 1) * NK])
                seq.add(ins)
                seq.so_far_apart(dve, dve_turns)
                for r in halves:
                    ins = v.max_index(iu[:, r * K + 8:r * K + 16], ranks[r][:, 8:16], sims2[:, r * NK:(r + 1) * NK])
                seq.add(ins)
                seq.so_far_apart(dve, dve_turns)
                lo, hi = HE * K + mine.start, 3 * HE * K + mine.start
                seq.add(v.tensor_scalar(vi[:, lo:lo + n * K], iu[:, mine], float(CODE), None, ALU.mult))
                seq.add(v.tensor_scalar(vi[:, hi:hi + n * K], iu[:, HE * K + mine.start:HE * K + mine.stop], float(NK), None, ALU.mult))
                yield
                at, a = 0, 0
                while a < K:
                    wide = PAIRS[a][1]
                    m = sum(1 for _, c in PAIRS if c == wide)
                    ins = v.tensor_tensor(strided(cand, h0 * NC + at, [(NC, n), (wide, m), (1, wide)]),
                                          strided(vi, mine.start + a, [(K, n), (1, m), (0, wide)]),
                                          strided(vi, 2 * HE * K + mine.start, [(K, n), (0, m), (1, wide)]), ALU.add)
                    at, a = at + wide * m, a + m
                seq.add(ins)
                seq.so_far(dve)
                codes = vi[:, lo:lo + n * K]
                seq.add(v.tensor_tensor(codes, codes, const_of("code")[:, mine], ALU.add))
                seq.so_far(dve)
                by_head = [(K, n), (1, K - 1)]
                at = HE * NC + mine.start
                v.tensor_tensor(strided(sims2, at + 1, by_head), strided(vi, lo + 1, by_head), strided(vi, lo, by_head), ALU.subtract)
                seq.add(v.tensor_copy(strided(sims2, at, [(K, n)]), strided(vi, lo, [(K, n)])))
                seq.so_far_apart(dve, dve_turns)
                score = {h: cand[:, h * NC:(h + 1) * NC] for h in heads}
                rest = {h: cand2[:, h * NC:(h + 1) * NC] for h in heads}
                for h in heads:
                    ins = v.max(top[:, h * K:h * K + 8], score[h])
                seq.add(ins)
                yield
                seq.so_far_apart(dve, dve_turns)
                for h in heads:
                    ins = v.match_replace(rest[h], top[:, h * K:h * K + 8], score[h], LOWEST)
                seq.add(ins)
                for h in heads:
                    v.max_index(pos[:, h * K:h * K + 8], top[:, h * K:h * K + 8], score[h])
                yield
                seq.so_far_apart(dve, dve_turns)
                for h in heads:
                    ins = v.max(top[:, h * K + 8:h * K + 16], rest[h])
                seq.add(ins)
                seq.so_far_apart(dve, dve_turns)
                for h in heads:
                    ins = v.max_index(pos[:, h * K + 8:h * K + 16], top[:, h * K + 8:h * K + 16], rest[h])
                seq.add(ins)
                seq.add(v.tensor_copy(den[:, h0:h0 + n], strided(top, mine.start, [(K, n)])))
                seq.so_far(dve)
                chosen = strided(top, mine.start, [(K, n), (1, K)])
                ins = v.tensor_tensor(chosen, chosen, strided(den, h0, [(1, n), (0, K)]), ALU.subtract)
                if h0 + n == HE:
                    ins.then_inc(top_ready, 1)
                seq.add(v.tensor_copy(posf, pos[:, mine]))
                yield
                hot = oneh[:, 0:n * K * K].rearrange("p (m c) -> p m c", c=K)
                hot3 = strided(oneh, 0, [(K * K, n), (K, K), (1, K)])
                place_of = strided(sims2, HE * NC + HE * K + mine.start, [(1, n * K), (0, K)])
                seq.so_far(dve)
                seq.add(v.tensor_tensor(hot, place_of, strided(cst, CONST_AT["first"][0], [(0, n * K), (1, K)]), ALU.is_ge))
                seq.so_far(dve)
                seq.add(v.tensor_tensor(hot3, hot3, strided(sims2, at, [(K, n), (0, K), (1, K)]), ALU.mult))
                seq.so_far(dve)
                yield
                seq.add(v.tensor_reduce(code, hot, AX.X, ALU.add))
                seq.so_far(dve)
                seq.add(v.tensor_scalar(whole, code, 1.0 / CODE, ROUND - 0.5, ALU.mult, ALU.add))
                seq.add(v.tensor_tensor(posf, posf, code, ALU.subtract))
                seq.so_far(dve)
                seq.add(v.tensor_scalar(base, whole, -ROUND - 1.0, None, ALU.add))
                seq.add(v.tensor_scalar(behind, whole, -ROUND, float(CODE), ALU.add, ALU.mult))
                seq.so_far(dve)
                seq.add(v.tensor_tensor(place, posf, behind, ALU.add))
                seq.so_far(dve)
                yield
                seq.add(v.tensor_tensor(hot, place_of, strided(cst, CONST_AT["iota"][0], [(0, n * K), (1, K)]), ALU.is_equal))
                seq.so_far(dve)
                seq.add(v.tensor_tensor(hot3, hot3, strided(vi, hi, [(K, n), (0, K), (1, K)]), ALU.mult))
                seq.so_far(dve)
                yield
                seq.add(v.tensor_reduce(found, hot, AX.X, ALU.add))
                seq.so_far(dve)
                seq.add(v.tensor_tensor(row, found, base, ALU.add))
                seq.so_far(dve)
                v.tensor_copy(idx[:, t * HE * K + mine.start:t * HE * K + mine.stop], row).then_inc(done, 1)

            def group(g, g_rank, g_last):
                seq = Steps(dve_seq, DVE_SEQ, g)
                rseq = Steps(rank_seq, RANK_SEQ, g_rank)
                seq0, seq1 = Steps(att_seq[0], 5, g), Steps(att_seq[1], LAST_SEQ, g_last)
                ranking = [rank(t, g_rank, rseq) if g_rank is not None else None for t in range(2)]

                def ranks(t, count):
                    for _ in range(count):
                        if ranking[t]:
                            next(ranking[t], None)

                def pieces(turn, ks):
                    if turn is not None:
                        for k in ks:
                            if k == 0 and g_last is not None:
                                dve.wait_ge(kv_saved, g_last + 1)
                            piece(k, turn)

                if g_last is None:
                    plan = [(lambda: ranks(0, 10), lambda: ranks(0, 5)),
                            (lambda: (ranks(0, 7), ranks(1, 2)), lambda: pieces(g_rank, [0, 1])),
                            (lambda: (pieces(g_rank, [2]), ranks(1, 4)), lambda: (pieces(g_rank, [3, 4]), ranks(1, 1))),
                            (lambda: ranks(1, 3), lambda: (ranks(1, 2), pieces(g_rank, [5, 6])))]
                    later = [[7], [8], [9], [10]]
                else:
                    plan = [(lambda: ranks(0, 5), lambda: (ranks(0, 1), pieces(g_last, [11, 12]))),
                            (lambda: (ranks(0, 4), pieces(g_last, [13])), lambda: (ranks(0, 1), pieces(g_last, [14, 15]))),
                            (lambda: ranks(1, 5), lambda: (ranks(1, 1), pieces(g_rank, [0, 1]))),
                            (lambda: (ranks(1, 4), pieces(g_rank, [2])), lambda: (ranks(1, 1), pieces(g_rank, [3, 4])))]
                    later = [[5], [6], [7], [8, 9, 10]]
                for l in range(L):
                    layer(g, l, lambda i: plan[l][i]())
                if g_rank is not None:
                    rseq.close()
                for c in (1, 3, 5, 7):
                    dve.wait_ge(l1_full, g * 8 + c + 1)
                    v.tensor_copy(pix[:, c * BANK:(c + 1) * BANK], bank((2, 3, 4, 5, 6, 7, 2, 3)[c])).then_inc(l1_dve, 1)
                if g_last is not None:
                    keys(1, g_last)
                reached(dve, pe_step, PE_STEPS, "image", g)
                for x2 in range(2):
                    for ci in range(2):
                        r = (x2 * S, x2 * S + S)
                        ins = v.tensor_scalar(strided(hT, 32 * ci + x2, [(2, 4), (8, 4), (S, GB)], (0, S)),
                                              strided(ps, 6 * BANK + ci * S, [(16, 4), (4, 4), (1, GB)], r),
                                              q2b_s[r[0]:r[1], 0:1], None, ALU.add)
                ins.then_inc(dve_step, 1)
                turn_over(g_rank, g_last, seq1)
                reached(dve, pe_step, PE_STEPS, "h1", g)
                v.tensor_copy(h1[:, :], bank(7, 2 * S)).then_inc(dve_step, 1)
                reached(dve, dve_step, DVE_STEPS, "h1", g)
                normalise(h1, 1, g, seq)
                pieces(g_rank, later[0])
                if g_last is not None:
                    masked(1, g_last, seq1)
                keys(0, g, range(2))
                if g_last is not None:
                    probabilities(1, g_last, seq1)
                keys(0, g, range(2, 4))
                pieces(g_rank, later[1])
                masked(0, g, seq0)
                probabilities(0, g, seq0)
                reached(dve, att[0]["pe"], ATT_PE[0], "pT1", g)
                v.tensor_copy(pT[0][:, BANK:2 * BANK], bank(BANKS[0]["pT"] + 1)).then_inc(att[0]["dve"], 1)
                pieces(g_rank, later[2])
                reached(dve, att[0]["pe"], ATT_PE[0], "o", g)
                v.tensor_copy(*oT_tile(0, 1)).then_inc(att[0]["dve"], 1)
                reached(dve, att[0]["pe"], ATT_PE[0], "y", g)
                h3 = h2[:, :].rearrange("p (t s) -> p t s", t=2)
                seq.add(v.tensor_tensor(h3, h1[:, :].rearrange("p (t s) -> p t s", t=2), result(0), ALU.add))
                seq.so_far(dve)
                v.tensor_tensor(h3, h3, strided(bu_s, 0, [(0, 2), (1, S)]), ALU.add).then_inc(dve_step, 1)
                reached(dve, dve_step, DVE_STEPS, "h2", g)
                normalise(h2, 2, g, seq)
                if g_last is not None:
                    finish(g_last, seq1)
                pieces(g_rank, later[3])
                seq.close()

            def turn_over(g_rank, g_last, seq):
                if g_last is not None:
                    dve.wait_ge(stored, 16 * g_last + 16)
                    seq.add(v.tensor_copy(res[:, :], h2p[:, :]))
                    seq.so_far(dve)
                if g_rank is not None:
                    reached(dve, dve_step, DVE_STEPS, "h2", g_rank)
                    v.tensor_copy(h2p[:, :], h2[:, :])
                    if g_last is not None:
                        reached(dve, att[1]["pe"], ATT_PE[1], "q3", g_last)
                    v.tensor_copy(xT2p[0:S + 1, :], xT2[0:S + 1, :]).then_inc(saved, 1)

            def finish(turn, seq):
                reached(dve, att[1]["pe"], ATT_PE[1], "y", turn)
                r = res[:, :].rearrange("p (t s) -> p t s", t=2)
                v.tensor_tensor(r, r, result(1), ALU.add).then_inc(out_ready, 1)
                seq.close()

            v.memset(zero[:, :], 0.0).then_inc(memz, 1)
            for z in (q_all, zx, mixT):
                v.memset(z[:, :], 0.0)
            for z in (wu_s, wo_s):
                v.memset(z[:, 4 * S:3 * S + PAD], 0.0)
            for o in (xT, xT2):
                ins = v.memset(o[S:S + 1, :], 1.0)
            ins.then_inc(memz, 1)
            dve.wait_ge(memz, 2)
            v.memset(res[:, :], 0.0).then_inc(stored, 16)
            v.memset(red[:, :], 0.0).then_inc(slots, RING)
            v.memset(top[:, :], 0.0).then_inc(rectified, 8)
            dve.wait_ge(cst_in, 16)
            dve.wait_ge(early, 16 * N_EARLY)
            v.tensor_scalar(b1_all[0:1, :], b1_all[0:1, :], float(S), None, ALU.mult)
            v.tensor_scalar(b2_all[0:2 * C, :], b2_all[0:2 * C, :], float(S), None, ALU.mult)
            v.tensor_scalar(q2blk[:, :], const_of("q2m"), q2_s[:, 0:1], None, ALU.mult)
            dve.wait_ge(qall_pe, 1)
            for s in range(L + 1):
                ins = v.tensor_tensor(strided(q_all, s * C, [(MID, GB), (1, MID)]), strided(ps, 2 * BANK + s * MID, [(0, GB), (1, MID)]),
                                      const_of("img").rearrange("p (b m) -> p b m", m=MID), ALU.mult)
            ins.then_inc(built, 1)
            dve.wait_ge(loaded, 16 * N_LOADS)

            group(0, None, None)
            group(1, 0, None)
            with dve.Fori(2, G) as g:
                group(g, g - 1, g - 2)
            rseq = Steps(rank_seq, RANK_SEQ, G - 1)
            for _ in rank(0, G - 1, rseq):
                pass
            for k in range(11, PIECES):
                piece(k, G - 2)
            for _ in rank(1, G - 1, rseq):
                pass
            rseq.close()
            dve.wait_ge(kv_saved, G - 1)
            for k in range(4):
                piece(k, G - 1)
            seq1 = Steps(att_seq[1], LAST_SEQ, G - 2)
            keys(1, G - 2)
            turn_over(G - 1, G - 2, seq1)
            masked(1, G - 2, seq1)
            probabilities(1, G - 2, seq1)
            finish(G - 2, seq1)
            seq = Steps(tail_seq, TAIL_SEQ, 0)
            for bp in range(2):
                for k in range(4 if bp == 0 else HE, HE * (bp + 1)):
                    piece(k, G - 1, last=k == PIECES - 1)
                if bp == 0:
                    dve.wait_ge(stored, 16 * (G - 1) + 16)
                    seq.add(v.tensor_copy(res[:, :], h2p[:, :]))
                for t in range(4):
                    reached(dve, tail_pe, TAIL_PE, f"k{t}", bp)
                    v.tensor_copy(strided(kT1, NQ + t * BANK + bp * P, [(2 * P, 2), (1, P)], (0, S)),
                                  strided(ps, BANKS[1]["k"][t] * BANK, [(P, 2), (1, P)], (0, S))).then_inc(tail_dve, 1)
                reached(dve, tail_pe, TAIL_PE, "scores", bp)
                rows = strided(zxT, sc_at[1] + bp * P, [(2 * P, 4), (S, 2), (1, S)])
                of_rows = lambda at: strided(red, at, [(2, 4), (1, 2), (0, S)])
                seq.add(v.tensor_tensor(rows, strided(ps, BANKS[1]["scores"] * BANK + bp * P, [(2 * P, 4), (S, 2), (1, S)]),
                                        strided(cst, CONST_AT["causal"][0], [(0, 4), (0, 2), (1, S)]), ALU.add))
                seq.so_far(dve)
                seq.add(v.tensor_reduce(red[:, 0:8], rows, AX.X, ALU.max))
                seq.so_far(dve)
                v.tensor_tensor(rows, rows, of_rows(0), ALU.subtract).then_inc(tail_dve, 1)
                reached(dve, tail_act, TAIL_ACT, "exp", bp)
                seq.add(v.tensor_reduce(red[:, 8:16], rows, AX.X, ALU.add))
                seq.so_far(dve)
                seq.add(v.reciprocal(red[:, 16:24], red[:, 8:16]))
                seq.so_far(dve)
                v.tensor_tensor(rows, rows, of_rows(16), ALU.mult).then_inc(tail_dve, 1)
                reached(dve, tail_pe, TAIL_PE, "y", bp)
                r = res[:, bp * S:(bp + 1) * S]
                ins = v.tensor_tensor(r, r, bank(6 + bp, S), ALU.add)
            ins.then_inc(out_ready, 1)
            seq.close()

        @block.gpsimd
        def _(pool):
            def gathers(g, first):
                for k in range(PIECES):
                    if first and k == 0:
                        pool.wait_ge(idx_first, 1)
                    elif k % HE == 0 or first and k == HE // 2:
                        pool.wait_ge(idx_ready, g * 2 + k // HE + 1)
                    wait_apart(pool, slots, g * PIECES + k + 1, pool_turns)
                    for m in range(K):
                        o = (k % RING * K + m) * P
                        pool.indirect_dma_start(out=ring[:, o:o + P], out_offset=None, in_=table,
                                                in_offset=bass.IndirectOffsetOnAxis(ap=idx[:, k * K + m:k * K + m + 1], axis=0)
                                                ).then_inc(gath[k % RING], 16)

            gathers(0, True)
            with pool.Fori(1, G) as g:
                gathers(g, False)


def kernel(**inputs):
    import numpy as _np
    import concourse.bacc as _bacc
    from concourse import mybir as _mybir
    from concourse.bass_utils import run_bass_kernel_spmd as _run

    a = {k.replace("L0_", ""): _np.asarray(v) for k, v in inputs.items()}
    f = _np.float32
    z = lambda *s: _np.zeros(s, f)
    laid = {}
    laid["x"] = a["x"].reshape(G, GB, XP, 2, S).transpose(0, 3, 4, 2, 1).reshape(G, P, XP * GB)
    laid["const"] = CONST
    w2s = z(C, L, C)
    w2s[0:3, 0], w2s[3, 0] = a["tok_p_w"].T, a["tok_p_b"]
    w2s[:, 1:] = a["tok_w2_w"][:L - 1].transpose(2, 0, 1)
    laid["w2s"] = _np.tile(w2s.reshape(C, L * C), (4, 1))
    w1s = z(4, C, L, 4, C)
    for q in range(4):
        w1s[q, :, :, q] = a["tok_w1_w"].transpose(2, 0, 1)
    laid["w1s"] = w1s.reshape(P, L * P)
    laid["fw"] = a["tok_fw"].transpose(0, 1, 6, 2, 4, 5, 3).reshape(L, P, J * C)
    laid["b1"] = a["tok_w1_b"].reshape(1, L * C)
    b2 = z(2, C, L, GB, 2, 2)
    b2[0, :, 1:, :, 0, 0] = a["tok_w2_b"][:L - 1].T[:, :, None]
    b2[1, :, 1:, :, 0, 1] = a["tok_w2_b"][:L - 1].T[:, :, None]
    laid["b2"] = b2.reshape(2 * C, L * 16)
    w2q = z(C + 1, 2 * L + 1, GB, C)
    w2q[:C, 0, :, 0:3] = a["tok_p_w"][:, None]
    w2q[:C, 0, :, 3] = a["tok_p_b"][:, None]
    w2q[C, 0, :, 3] = 1.0
    w2q[:C, 1:L + 1] = a["tok_w2_w"].transpose(1, 0, 2)[:, :, None]
    w2q[:C, L + 1:, :, 3] = a["tok_w2_b"].T[:, :, None]
    laid["w2q"] = w2q.reshape(C + 1, (2 * L + 1) * P)
    laid["q1t"] = _np.concatenate([a["tok_q1_w"].T, a["tok_q1_b"][None]])
    q2 = z(4, 32)
    q2[:, :GB * MID] = _np.tile(a["tok_q2_w"].reshape(1, MID), (4, GB))
    laid["q2c"] = q2.reshape(P, 1)
    laid["q2b"] = _np.tile(a["tok_q2_b"].reshape(1, 1), (P, 1))
    for n, w, b in (("wq", "attn_Wq", "attn_bq"), ("wk", "attn_Wk", "attn_bk"), ("wv", "attn_Wv", "attn_bv")):
        laid[n] = _np.concatenate([a[w], a[b][None]])
    laid["wu"] = a["attn_Wu"].reshape(4, P, S).transpose(1, 0, 2).reshape(P, 4 * S)
    laid["bu"] = _np.tile(a["attn_bu"][None], (P, 1))
    laid["wpk"] = _np.concatenate([a["ffn_Wq_pk"], z(1, HE * S)])
    pk = z(4, 32, 2, 2, 4, NK)
    keys = a["ffn_pk_keys"].reshape(2, NK, 2, 4, 32)
    for h in range(4):
        pk[h, :, :, :, h] = keys[:, :, :, h].transpose(3, 0, 2, 1)
    laid["pk"] = pk.reshape(P, 4 * 4 * NK)
    laid["wq2"] = _np.concatenate([a["ffn_Wq"], z(1, HE * S)])
    laid["wo"] = a["ffn_Wo"].reshape(4, P, S).transpose(1, 0, 2).reshape(P, 4 * S)
    laid["table"] = _np.concatenate([a["ffn_keys_table"], a["ffn_values_table"]], 1)

    nc = _bacc.Bacc("TRN2", target_bir_lowering=False, num_devices=1)
    arrays, args = {}, {}
    for name, v in laid.items():
        v = _np.ascontiguousarray(v)
        arrays[f"in_{name}"] = v
        args[name] = nc.dram_tensor(f"in_{name}", v.shape, _mybir.dt.from_np(v.dtype), kind="ExternalInput").ap()
    args["out"] = nc.dram_tensor("out_h", (G, 2, P, S), F32, kind="ExternalOutput").ap()
    build(nc, **args)
    r = _run(nc, [arrays], core_ids=[0])
    return r.results[0]["out_h"].reshape(B, S, S)
```
